# Optimizing a Trainium2 kernel written in Bass

```python
import numpy as np
import jax
import jax.numpy as jnp

def _softmax(x, axis=-1):
    return jax.nn.softmax(x, axis=axis)

def _gelu(x):
    return jax.nn.gelu(x, approximate=True)

def _silu(x):
    return jax.nn.silu(x)

def _sigmoid(x):
    return jax.nn.sigmoid(x)

def _layernorm(x, axis=-1, eps=1e-05):
    m = jnp.mean(x, axis=axis, keepdims=True)
    v = jnp.var(x, axis=axis, keepdims=True)
    return (x - m) / jnp.sqrt(v + eps)

def _scatter_add(tgt, idx, src, axis=0):
    return tgt.at[idx].add(src)

def _segment_sum(src, seg, n):
    return jax.ops.segment_sum(src, seg, n)
kernel_name = 'mk_perceiver_d2_seqx_r4_ac04f2'

def setup_inputs(seed: int=0):
    np.random.seed(seed)
    _w = jnp.asarray

    def _rec_inputs():
        import jax
        import jax.numpy as jnp
        _rk = jax.random.key(seed)
        x = 7.22e-05 + 1 * jax.random.normal(jax.random.fold_in(_rk, 1), (128, 32, 256), jnp.float32)
        _lenS = 32 - jax.random.randint(jax.random.fold_in(_rk, 7), (128,), 0, max(1, 32 // 4) + 1, jnp.int32)
        _lenS2 = 257 - jax.random.randint(jax.random.fold_in(_rk, 8), (128,), 0, max(1, 257 // 4) + 1, jnp.int32)
        _ctx_1024P = jax.random.normal(jax.random.fold_in(_rk, 11), (128, 16, 256), jnp.float32)
        _ctx_1024c = jax.random.dirichlet(jax.random.fold_in(_rk, 511), 0.3 * jnp.ones((16,), jnp.float32), (128, 257))
        _ctx_1024t = jnp.einsum('bsk,bkd->bsd', _ctx_1024c, _ctx_1024P)
        _ctx_1024t = _ctx_1024t * jax.lax.rsqrt(jnp.mean(jnp.square(_ctx_1024t)) + 1e-12) * 0.953939
        ctx_1024 = 4.13588e-05 + 0.999923 * (_ctx_1024t + 0.3 * jax.random.normal(jax.random.fold_in(_rk, 611), (128, 257, 256), jnp.float32))
        return (x, ctx_1024)
    x, ctx_1024 = _rec_inputs()

    def _L0_xattn_setup():
        import jax, jax.numpy as jnp
        import numpy as np
        D_MODEL = 256
        D_KQ = 256
        D_V = 256
        key = jax.random.key(seed)
        ks = jax.random.split(key, 8)
        B, N, M = (4, 512, 512)
        x_1 = jax.random.normal(ks[0], (B, N, D_MODEL), dtype=jnp.float32)
        x_2 = jax.random.normal(ks[1], (B, M, D_MODEL), dtype=jnp.float32)
        s = 1.0 / np.sqrt(D_MODEL)
        Wq = jax.random.normal(ks[2], (D_MODEL, D_KQ), dtype=jnp.float32) * s
        bq = jnp.zeros((D_KQ,), dtype=jnp.float32)
        Wk = jax.random.normal(ks[3], (D_MODEL, D_KQ), dtype=jnp.float32) * s
        bk = jnp.zeros((D_KQ,), dtype=jnp.float32)
        Wv = jax.random.normal(ks[4], (D_MODEL, D_V), dtype=jnp.float32) * s
        bv = jnp.zeros((D_V,), dtype=jnp.float32)
        return {'x_1': x_1, 'x_2': x_2, 'Wq': Wq, 'bq': bq, 'Wk': Wk, 'bk': bk, 'Wv': Wv, 'bv': bv}
    _L0_xattn_all = _L0_xattn_setup()
    _L0_xattn_in = {k: v for k, v in _L0_xattn_all.items() if k in ('Wq', 'bq', 'Wk', 'bk', 'Wv', 'bv')}
    del _L0_xattn_all

    def _L0_attn_setup():
        import jax, jax.numpy as jnp
        import numpy as np
        E = 256
        H = 16
        HD = E // H
        key = jax.random.key(seed)
        k1, k2, k3, k4, k5 = jax.random.split(key, 5)
        x = jax.random.normal(k1, (2, 512, E), dtype=jnp.float32)
        s = 1.0 / np.sqrt(E)
        qkv_w = jax.random.uniform(k2, (3 * E, E), jnp.float32, -s, s)
        qkv_b = jax.random.uniform(k3, (3 * E,), jnp.float32, -s, s)
        o_w = jax.random.uniform(k4, (E, E), jnp.float32, -s, s)
        o_b = jax.random.uniform(k5, (E,), jnp.float32, -s, s)
        return {'x': x, 'qkv_w': qkv_w, 'qkv_b': qkv_b, 'o_w': o_w, 'o_b': o_b}
    _L0_attn_all = _L0_attn_setup()
    _L0_attn_in = {k: v for k, v in _L0_attn_all.items() if k in ('qkv_w', 'qkv_b', 'o_w', 'o_b')}
    del _L0_attn_all

    def _L0_ffn_setup():
        import jax, jax.numpy as jnp
        import numpy as np
        HIDDEN = 256
        INNER = 1024

        def _weight_quant(w):
            scale = 1.0 / jnp.clip(jnp.mean(jnp.abs(w)), 1e-05)
            wq = jnp.clip(jnp.round(w * scale), -1.0, 1.0) / scale
            return w + jax.lax.stop_gradient(wq - w)

        def _act_quant(x):
            scale = 127.0 / jnp.clip(jnp.max(jnp.abs(x), axis=-1, keepdims=True), 1e-05)
            xq = jnp.clip(jnp.round(x * scale), -128.0, 127.0) / scale
            return x + jax.lax.stop_gradient(xq - x)

        def _bitlinear(x, w):
            return jnp.einsum('bsi,oi->bso', _act_quant(x), _weight_quant(w))
        key = jax.random.key(seed)
        k0, k1, k2, k3 = jax.random.split(key, 4)
        x = jax.random.normal(k0, (4, 512, HIDDEN), dtype=jnp.float32)
        w_gate = jax.random.normal(k1, (INNER, HIDDEN), dtype=jnp.float32) / np.sqrt(HIDDEN)
        w_up = jax.random.normal(k2, (INNER, HIDDEN), dtype=jnp.float32) / np.sqrt(HIDDEN)
        w_down = jax.random.normal(k3, (HIDDEN, INNER), dtype=jnp.float32) / np.sqrt(INNER)
        return {'x': x, 'w_gate': w_gate, 'w_up': w_up, 'w_down': w_down}
    _L0_ffn_all = _L0_ffn_setup()
    _L0_ffn_in = {k: v for k, v in _L0_ffn_all.items() if k in ('w_gate', 'w_up', 'w_down')}
    del _L0_ffn_all

    def _L1_xattn_setup():
        import jax, jax.numpy as jnp
        import numpy as np
        DIM = 256
        NUM_HEADS = 16
        HEAD_DIM = DIM // NUM_HEADS
        SCALE = HEAD_DIM ** (-0.5)
        key = jax.random.key(seed)
        k1, k2, k3, k4, k5, k6 = jax.random.split(key, 6)
        B, S, L = (4, 2048, 128)
        x = jax.random.normal(k1, (B, S, DIM), dtype=jnp.float32)
        latents = jax.random.normal(k2, (B, L, DIM), dtype=jnp.float32)
        w_q = jax.random.normal(k3, (DIM, DIM), dtype=jnp.float32) * DIM ** (-0.5)
        w_kv = jax.random.normal(k4, (2 * DIM, DIM), dtype=jnp.float32) * DIM ** (-0.5)
        w_out = jax.random.normal(k5, (DIM, DIM), dtype=jnp.float32) * DIM ** (-0.5)
        b_out = jax.random.normal(k6, (DIM,), dtype=jnp.float32) * 0.01
        return {'x': x, 'latents': latents, 'w_q': w_q, 'w_kv': w_kv, 'w_out': w_out, 'b_out': b_out}
    _L1_xattn_all = _L1_xattn_setup()
    _L1_xattn_in = {k: v for k, v in _L1_xattn_all.items() if k in ('w_q', 'w_kv', 'w_out', 'b_out')}
    del _L1_xattn_all

    def _L1_attn_setup():
        import jax, jax.numpy as jnp
        import numpy as np
        B, T, D = (4, 512, 256)
        H, Dh = (16, 64)
        key = jax.random.key(seed)
        ks = jax.random.split(key, 5)
        std_qkv = float(np.sqrt(2.0 / (Dh * D)))
        std_o = float(np.sqrt(2.0 / (D * Dh)))
        return {'x': jax.random.normal(ks[0], (B, T, D), dtype=jnp.float32), 'W_Q': jax.random.normal(ks[1], (H, Dh, D), dtype=jnp.float32) * std_qkv, 'b_Q': jnp.zeros((H, Dh), dtype=jnp.float32), 'W_K': jax.random.normal(ks[2], (H, Dh, D), dtype=jnp.float32) * std_qkv, 'b_K': jnp.zeros((H, Dh), dtype=jnp.float32), 'W_V': jax.random.normal(ks[3], (H, Dh, D), dtype=jnp.float32) * std_qkv, 'b_V': jnp.zeros((H, Dh), dtype=jnp.float32), 'W_O': jax.random.normal(ks[4], (H, D, Dh), dtype=jnp.float32) * std_o, 'b_O': jnp.zeros((D,), dtype=jnp.float32)}
    _L1_attn_all = _L1_attn_setup()
    _L1_attn_in = {k: v for k, v in _L1_attn_all.items() if k in ('W_Q', 'b_Q', 'W_K', 'b_K', 'W_V', 'b_V', 'W_O', 'b_O')}
    del _L1_attn_all

    def _L1_ffn_setup():
        import jax, jax.numpy as jnp
        import numpy as np
        D = 256
        H = 256
        E = 8
        K = 2
        I = 2 * 256
        ROUTE_SCALE = 1.0
        key = jax.random.key(seed)
        ks = jax.random.split(key, 12)
        s = lambda *sh: 1.0 / np.sqrt(sh[-1])
        return {'x': jax.random.normal(ks[0], (1, 512, D), jnp.float32), 'gate_w': jax.random.normal(ks[1], (E, D), jnp.float32) * s(E, D), 'w1': jax.random.normal(ks[2], (E, H, D), jnp.float32) * s(H, D), 'b1': jax.random.normal(ks[3], (E, H), jnp.float32) * 0.01, 'w2': jax.random.normal(ks[4], (E, D, H), jnp.float32) * s(D, H), 'b2': jax.random.normal(ks[5], (E, D), jnp.float32) * 0.01, 'w3': jax.random.normal(ks[6], (E, H, D), jnp.float32) * s(H, D), 'b3': jax.random.normal(ks[7], (E, H), jnp.float32) * 0.01, 'sw1': jax.random.normal(ks[8], (I, D), jnp.float32) * s(I, D), 'sw2': jax.random.normal(ks[9], (I, D), jnp.float32) * s(I, D), 'sw3': jax.random.normal(ks[10], (D, I), jnp.float32) * s(D, I)}
    _L1_ffn_all = _L1_ffn_setup()
    _L1_ffn_in = {k: v for k, v in _L1_ffn_all.items() if k in ('gate_w', 'w1', 'b1', 'w2', 'b2', 'w3', 'b3', 'sw1', 'sw2', 'sw3')}
    del _L1_ffn_all
    return {'x': x, 'ctx_1024': ctx_1024, 'L0_xattn_Wq': _L0_xattn_in['Wq'], 'L0_xattn_bq': _L0_xattn_in['bq'], 'L0_xattn_Wk': _L0_xattn_in['Wk'], 'L0_xattn_bk': _L0_xattn_in['bk'], 'L0_xattn_Wv': _L0_xattn_in['Wv'], 'L0_xattn_bv': _L0_xattn_in['bv'], 'L0_attn_qkv_w': _L0_attn_in['qkv_w'], 'L0_attn_qkv_b': _L0_attn_in['qkv_b'], 'L0_attn_o_w': _L0_attn_in['o_w'], 'L0_attn_o_b': _L0_attn_in['o_b'], 'L0_ffn_w_gate': _L0_ffn_in['w_gate'], 'L0_ffn_w_up': _L0_ffn_in['w_up'], 'L0_ffn_w_down': _L0_ffn_in['w_down'], 'L1_xattn_w_q': _L1_xattn_in['w_q'], 'L1_xattn_w_kv': _L1_xattn_in['w_kv'], 'L1_xattn_w_out': _L1_xattn_in['w_out'], 'L1_xattn_b_out': _L1_xattn_in['b_out'], 'L1_attn_W_Q': _L1_attn_in['W_Q'], 'L1_attn_b_Q': _L1_attn_in['b_Q'], 'L1_attn_W_K': _L1_attn_in['W_K'], 'L1_attn_b_K': _L1_attn_in['b_K'], 'L1_attn_W_V': _L1_attn_in['W_V'], 'L1_attn_b_V': _L1_attn_in['b_V'], 'L1_attn_W_O': _L1_attn_in['W_O'], 'L1_attn_b_O': _L1_attn_in['b_O'], 'L1_ffn_gate_w': _L1_ffn_in['gate_w'], 'L1_ffn_w1': _L1_ffn_in['w1'], 'L1_ffn_b1': _L1_ffn_in['b1'], 'L1_ffn_w2': _L1_ffn_in['w2'], 'L1_ffn_b2': _L1_ffn_in['b2'], 'L1_ffn_w3': _L1_ffn_in['w3'], 'L1_ffn_b3': _L1_ffn_in['b3'], 'L1_ffn_sw1': _L1_ffn_in['sw1'], 'L1_ffn_sw2': _L1_ffn_in['sw2'], 'L1_ffn_sw3': _L1_ffn_in['sw3']}

def reference(x, ctx_1024, L0_xattn_Wq, L0_xattn_bq, L0_xattn_Wk, L0_xattn_bk, L0_xattn_Wv, L0_xattn_bv, L0_attn_qkv_w, L0_attn_qkv_b, L0_attn_o_w, L0_attn_o_b, L0_ffn_w_gate, L0_ffn_w_up, L0_ffn_w_down, L1_xattn_w_q, L1_xattn_w_kv, L1_xattn_w_out, L1_xattn_b_out, L1_attn_W_Q, L1_attn_b_Q, L1_attn_W_K, L1_attn_b_K, L1_attn_W_V, L1_attn_b_V, L1_attn_W_O, L1_attn_b_O, L1_ffn_gate_w, L1_ffn_w1, L1_ffn_b1, L1_ffn_w2, L1_ffn_b2, L1_ffn_w3, L1_ffn_b3, L1_ffn_sw1, L1_ffn_sw2, L1_ffn_sw3):
    import jax
    import jax.numpy as jnp

    def _L0_xattn_ref(x_1, x_2, Wq, bq, Wk, bk, Wv, bv):
        import jax, jax.numpy as jnp
        import numpy as np
        D_MODEL = 256
        D_KQ = 256
        D_V = 256
        q = jnp.einsum('bnd,de->bne', x_1, Wq) + bq
        k = jnp.einsum('bmd,de->bme', x_2, Wk) + bk
        v = jnp.einsum('bmd,de->bme', x_2, Wv) + bv
        scores = jnp.einsum('bne,bme->bnm', q, k) / jnp.sqrt(jnp.float32(D_KQ)).astype(q.dtype)
        attn = jax.nn.softmax(scores, axis=-1)
        return jnp.einsum('bnm,bme->bne', attn, v)

    def _L0_attn_ref(x, qkv_w, qkv_b, o_w, o_b):
        import jax, jax.numpy as jnp
        import numpy as np
        E = 256
        H = 16
        HD = E // H
        B, T, _ = x.shape
        qkv = x @ qkv_w.T + qkv_b
        q, k, v = jnp.split(qkv, 3, axis=-1)
        q = q.reshape(B, T, H, HD).transpose(0, 2, 1, 3)
        k = k.reshape(B, T, H, HD).transpose(0, 2, 1, 3)
        v = v.reshape(B, T, H, HD).transpose(0, 2, 1, 3)
        scores = jnp.einsum('bhqd,bhkd->bhqk', q, k) / np.sqrt(HD)
        causal = jnp.tril(jnp.ones((T, T), dtype=bool))
        scores = jnp.where(causal, scores, -jnp.inf)
        attn = jax.nn.softmax(scores, axis=-1)
        y = jnp.einsum('bhqk,bhkd->bhqd', attn, v)
        y = y.transpose(0, 2, 1, 3).reshape(B, T, E)
        return y @ o_w.T + o_b

    def _L0_ffn_ref(x, w_gate, w_up, w_down):
        import jax, jax.numpy as jnp
        import numpy as np
        HIDDEN = 256
        INNER = 1024

        def _weight_quant(w):
            scale = 1.0 / jnp.clip(jnp.mean(jnp.abs(w)), 1e-05)
            wq = jnp.clip(jnp.round(w * scale), -1.0, 1.0) / scale
            return w + jax.lax.stop_gradient(wq - w)

        def _act_quant(x):
            scale = 127.0 / jnp.clip(jnp.max(jnp.abs(x), axis=-1, keepdims=True), 1e-05)
            xq = jnp.clip(jnp.round(x * scale), -128.0, 127.0) / scale
            return x + jax.lax.stop_gradient(xq - x)

        def _bitlinear(x, w):
            return jnp.einsum('bsi,oi->bso', _act_quant(x), _weight_quant(w))
        gate = jax.nn.silu(_bitlinear(x, w_gate))
        up = _bitlinear(x, w_up)
        return _bitlinear(gate * up, w_down)

    def _L1_xattn_ref(x, latents, w_q, w_kv, w_out, b_out):
        import jax, jax.numpy as jnp
        import numpy as np
        DIM = 256
        NUM_HEADS = 16
        HEAD_DIM = DIM // NUM_HEADS
        SCALE = HEAD_DIM ** (-0.5)
        B, L, _ = latents.shape
        S = x.shape[1]
        q = latents @ w_q.T
        kv = x @ w_kv.T
        k, v = jnp.split(kv, 2, axis=-1)
        q = q.reshape(B, L, NUM_HEADS, HEAD_DIM)
        k = k.reshape(B, S, NUM_HEADS, HEAD_DIM)
        v = v.reshape(B, S, NUM_HEADS, HEAD_DIM)
        attn = jnp.einsum('blhd,bshd->bhls', q, k) * SCALE
        attn = jax.nn.softmax(attn, axis=-1)
        out = jnp.einsum('bhls,bshd->blhd', attn, v)
        out = out.reshape(B, L, DIM)
        return out @ w_out.T + b_out

    def _L1_attn_ref(x, W_Q, b_Q, W_K, b_K, W_V, b_V, W_O, b_O):
        import jax, jax.numpy as jnp
        import numpy as np
        B, T, D = (4, 512, 256)
        H, Dh = (16, 64)
        Q = jnp.einsum('btd,hkd->bthk', x, W_Q) + b_Q
        K = jnp.einsum('btd,hkd->bthk', x, W_K) + b_K
        V = jnp.einsum('btd,hkd->bthk', x, W_V) + b_V
        d_head = W_Q.shape[1]
        scores = jnp.einsum('bqhk,bshk->bhqs', Q, K) / jnp.sqrt(jnp.asarray(d_head, x.dtype))
        attn = jax.nn.softmax(scores, axis=-1)
        out_h = jnp.einsum('bhqs,bshk->bqhk', attn, V)
        return jnp.einsum('bqhk,hdk->bqd', out_h, W_O) + b_O

    def _L1_ffn_ref(x, gate_w, w1, b1, w2, b2, w3, b3, sw1, sw2, sw3):
        import jax, jax.numpy as jnp
        import numpy as np
        D = 256
        H = 256
        E = 8
        K = 2
        I = 2 * 256
        ROUTE_SCALE = 1.0
        B, S, _ = x.shape
        xt = x.reshape(-1, D)
        logits = xt @ gate_w.T
        scores = jax.nn.softmax(logits.astype(jnp.float32), axis=-1)
        top_vals, idx = jax.lax.top_k(scores, K)
        weights = jnp.take_along_axis(scores, idx, axis=1).astype(x.dtype) * ROUTE_SCALE
        xs = xt[:, None, :] * weights[:, :, None]
        y = jnp.zeros_like(xt)
        for e in range(E):
            mask = (idx == e).astype(x.dtype)
            h = jax.nn.silu(jnp.einsum('tkd,hd->tkh', xs, w1[e]) + b1[e])
            x2 = jnp.einsum('tkh,dh->tkd', h, w2[e]) + b2[e]
            x3 = jnp.einsum('tkd,hd->tkh', xs, w3[e]) + b3[e]
            y = y + jnp.sum(x2 * x3 * mask[:, :, None], axis=1)
        z = jax.nn.silu(xt @ sw1.T) * (xt @ sw2.T) @ sw3.T
        return (y + z).reshape(B, S, D)
    x = x + _L0_xattn_ref(_layernorm(x, axis=-1), ctx_1024, L0_xattn_Wq, L0_xattn_bq, L0_xattn_Wk, L0_xattn_bk, L0_xattn_Wv, L0_xattn_bv)
    x = x + _L0_attn_ref(_layernorm(x, axis=-1), L0_attn_qkv_w, L0_attn_qkv_b, L0_attn_o_w, L0_attn_o_b)
    x = x + _L0_ffn_ref(_layernorm(x, axis=-1), L0_ffn_w_gate, L0_ffn_w_up, L0_ffn_w_down)
    x = x + _L1_xattn_ref(ctx_1024, _layernorm(x, axis=-1), L1_xattn_w_q, L1_xattn_w_kv, L1_xattn_w_out, L1_xattn_b_out)
    x = x + _L1_attn_ref(_layernorm(x, axis=-1), L1_attn_W_Q, L1_attn_b_Q, L1_attn_W_K, L1_attn_b_K, L1_attn_W_V, L1_attn_b_V, L1_attn_W_O, L1_attn_b_O)
    x = x + _L1_ffn_ref(_layernorm(x, axis=-1), L1_ffn_gate_w, L1_ffn_w1, L1_ffn_b1, L1_ffn_w2, L1_ffn_b2, L1_ffn_w3, L1_ffn_b3, L1_ffn_sw1, L1_ffn_sw2, L1_ffn_sw3)
    return x

_drawn_inputs = setup_inputs


def setup_inputs(seed=0):
    import zlib

    import numpy as np

    out = dict(_drawn_inputs(seed))
    spreads = {'L0_xattn_bq': (0.0, 0.387),
     'L0_xattn_bk': (0.0, 2.0),
     'L0_xattn_bv': (0.0, 0.1),
     'L1_attn_b_Q': (0.0, 2.0),
     'L1_attn_b_K': (0.0, 2.0),
     'L1_attn_b_V': (0.0, 0.1),
     'L1_attn_b_O': (0.0, 0.1)}
    factors = {'L1_xattn_b_out': 6.259,
     'L1_attn_W_Q': 26.254,
     'L1_attn_W_K': 24.173,
     'L1_ffn_b1': 33.78,
     'L1_ffn_b2': 8.0,
     'L1_ffn_b3': 30.274}
    for name, (base, spread) in spreads.items():
        noise = np.random.default_rng([zlib.crc32(name.encode()), seed]).standard_normal(out[name].shape)
        drawn = base * np.exp(spread * noise) if base else spread * noise
        out[name] = jnp.asarray(drawn.astype(out[name].dtype))
    for name, factor in factors.items():
        out[name] = (out[name] * factor).astype(out[name].dtype)
    return out
```

```python
from contextlib import ExitStack

import concourse.bass as bass
from concourse import mybir

F32 = mybir.dt.float32
F16 = mybir.dt.float16
BF16 = mybir.dt.bfloat16
U32 = mybir.dt.uint32
ALU = mybir.AluOpType
ACT = mybir.ActivationFunctionType
X = mybir.AxisListType.X

P = 128
D = 256
C = D // P
SEQ = 32
SEQS = 128
KEYS = 257
NB = P // SEQ
TILES = SEQS // NB
HEADS = 16
GROUPS = HEADS // 4
WIDE = 1024
EXPERTS = 8
SHARED = 512
EPS = 1e-5
ROUND = 1.5 * 2.0**23
FAR = -1.0e30

_SIZES = [
    ("q0", C * D), ("k0t", C * D), ("v0", C * D), ("qkv0", C * 3 * D), ("o0", C * D),
    ("xq", C * D), ("xkv", C * 2 * D), ("xo", C * D),
    ("aq", C * WIDE), ("ak", C * WIDE), ("av", C * WIDE), ("ao", WIDE // P * D),
    ("gate", C * EXPERTS), ("w1", EXPERTS * C * D), ("w2", EXPERTS * C * D), ("w3", EXPERTS * C * D),
    ("sw1", C * SHARED), ("sw2", C * SHARED), ("sw3", SHARED // P * D),
]
W_AT, W_COLS = {}, 0
for _name, _n in _SIZES:
    W_AT[_name] = (W_COLS, _n)
    W_COLS += _n
W_CHUNK = 730
W_SLOTS = 5
ARENA = 8198 + 2 * C * KEYS + 4 * D + D
assert W_COLS % (W_CHUNK * W_SLOTS) == 0

_CONSTS = [("ident", P), ("sel", SEQ), ("causal", SEQ), ("mask8", 8), ("quad", 4), ("half", 2), ("eye4", 16), ("iota8", 8)]
C_AT, C_COLS = {}, 0
for _name, _n in _CONSTS:
    C_AT[_name] = (C_COLS, C_COLS + _n)
    C_COLS += _n
_BIASES = [("bq0", 2), ("bk0", 2), ("bqk0", 4), ("bv0", 2), ("bqk1", 16), ("bv1", 8), ("b1", 16), ("b2", 16), ("b3", 16)]
B_AT, B_COLS = {}, 0
for _name, _n in _BIASES:
    B_AT[_name] = (B_COLS, B_COLS + _n)
    B_COLS += _n

SETUP_STEPS = 17

PER_TRIP = {
    "ln_var": 6, "ln_rstd": 6, "xn": 5, "xt_ps": 5, "xt_hi": 5, "xt_lo": 5, "ctx_hi": 8, "ctx_done": 9, "last_hi": 1,
    "q0_ps": 1, "q0_f": 1, "q0_hi": 1, "q0_lo": 1, "qp_ps": 1, "qp_hi": 1, "qp_lo": 1, "qbk_ps": 1, "s1_ps": 1,
    "s1_bias": 1, "p1": 1, "p1_last": 1, "pt1_ps": 1, "pt1_hi": 1, "pt1_lo": 1, "a1_ps": 1, "a1_hi": 1, "a1_lo": 1,
    "y1_ps": 1, "x_1": 1, "qk2_ps": 1, "qk2_f": 1, "qk2_hi": 1, "v2_ps": 1, "v2_hi": 1, "qbd2": 1, "vblk": 1,
    "s2_ps": 1, "s2_shift": 1, "p2": 1, "pt2_ps": 1, "pt2_hi": 1, "pt2_lo": 1, "o2g_ps": 1, "om_f": 4, "om_hi": 1,
    "om_lo": 1, "o2_ps": 1, "o2_hi": 2, "o2_lo": 2, "y2_ps": 1, "xq": 1, "xq_ps": 1, "xqt": 1, "gate_ps": 1,
    "up_ps": 1, "th3": 1, "hq": 1, "hq_ps": 1, "hqt": 1, "y3_ps": 1, "q4_ps": 1, "q4_hi": 1, "q4_lo": 1, "qbd4": 1,
    "vl_ps": 1, "vl_hi": 1, "vl_lo": 1, "k4_ps": 4, "k4_hi": 4, "k4_lo": 4, "v4_ps": 4, "v4_hi": 4, "v4_lo": 4,
    "s4_ps": 4, "s4_bias": 4, "p4": 16, "p4_last": 4, "pt4_ps": 4, "pt4_hi": 4, "pt4_lo": 4, "o4_ps": 4, "om4_f": 4,
    "om4_hi": 4, "om4_lo": 4, "sel_ps": 4, "sel_hi": 4, "sel_lo": 4, "y4_ps": 1, "v5_ps": 1, "v5_hi": 1, "v5_lo": 1,
    "qk5_ps": 4, "qk5_f": 4, "qk5_hi": 4, "qk5_lo": 4, "qb5": 4, "s5_ps": 4, "s5_shift": 1, "p5": 1, "p5_norm": 1,
    "pt5_ps": 1, "pt5_hi": 1, "ptb": 1, "o5_ps": 4, "o5_f": 8, "o5_hi": 1, "o5_lo": 1, "y5_ps": 1, "logit_ps": 1,
    "gate_max": 1, "gate_exp": 1, "gate_p": 1, "sh_ps": 1, "th_sh": 1, "sh_f": 1, "sh_hi": 1, "sh_lo": 1, "wb_ps": 1,
    "wb": 2, "z_ps": 1, "y_0": 1, "e13_ps": 8, "u4": 8, "th_e": 32, "he_f": 8, "he_hi": 8, "he_lo": 8, "e2_ps": 8,
    "x2": 16, "a3": 8, "prod": 8, "y_add": 8, "y6_ps": 1, "x_final": 1, "dve_order": 125,
}
AHEAD = ("x_1", "ctx_done", "y4_ps", "stored", "w_split")
SETUP_SIGNALS = ["const_in", "ffn_in", "pool_set", "ffn_abs", "ffn_sum", "dve_setup", "w_hi", "w_split",
                 "x_in", "last_in", "ctx_in0", "ctx_in1", "stored"] + [f"w_in{j}" for j in range(W_SLOTS)]


def build(nc, x_in, ctx_t, ctx_n, ctx_l, weights, ffn, consts, biases, rows, out):
    ctx = ExitStack()
    with ctx:
        def sb(name, shape, dt):
            return ctx.enter_context(nc.sbuf_tensor(name, shape, dt))

        def sem(name):
            return ctx.enter_context(nc.semaphore(name))

        wp = sb("wp", [P, 2, W_COLS], F16)
        ffn_w = sb("ffn_w", [P, 3, 2048], BF16)
        cst = sb("cst", [P, C_COLS], F32)
        bias = sb("bias", [P, B_COLS], F32)
        row_bias = sb("row_bias", [P, 4, D], F32)
        ident16 = sb("ident16", [P, P], F16)
        identb = sb("identb", [P, P], BF16)
        sel16 = sb("sel16", [P, SEQ], F16)
        ones = sb("ones", [P, P], F32)
        bk_pair = sb("bk_pair", [P, 2, C], F16)
        half_b1 = sb("half_b1", [P, EXPERTS * C], F32)
        ffn_inv = sb("ffn_inv", [P, 3], F32)
        stat = sb("stat", [P, 16], F32)
        neg_half = sb("neg_half", [P, 1], F32)

        def const(name):
            a, b = C_AT[name]
            return cst[:, a:b]

        def bcol(name):
            a, b = B_AT[name]
            return bias[:, a:b]

        def w(name, part, k, n, first=0):
            a, size = W_AT[name]
            return wp[:, part, a + first:a + first + k * n].rearrange("p (k n) -> p k n", k=k)

        ident = const("ident")
        causal, mask8, quad, half = const("causal"), const("mask8"), const("quad"), const("half")
        eye4 = const("eye4").rearrange("p (b j) -> p b j", b=NB)

        ctx_tp = sb("ctx_tp", [P, 2, C, NB, KEYS], F16)
        ctx_lp = sb("ctx_lp", [P, 2, D], F16)

        x0 = sb("x0", [P, D], F32)
        x = sb("x", [P, D], F32)
        x_out = sb("x_out", [P, D], F32)
        xn = sb("xn", [P, D], F32)
        xt = sb("xt", [P, 2, C, P], F16)
        bn = sb("bn", [P, 6], F32)
        mv = sb("mv", [P, 2], F32)
        var_eps = sb("var_eps", [P, 1], F32)
        rstd = sb("rstd", [P, 1], F32)
        qk_f = sb("qk_f", [P, 4, P], F32)
        qk = sb("qk", [P, 2, 4, P], F16)
        op = sb("op", [P, 2, C, P], F16)
        last_cols = sb("last_cols", [P, GROUPS, P], F32)
        qb5 = sb("qb5", [P, 2, C, NB, 4, SEQ], F16)
        vl = sb("vl", [P, 2, D], F16)
        small = sb("small", [P, 96], F32)
        idx = sb("idx", [P, 8], U32)
        waited = sb("waited", [P, 1], F32)
        th_rm = sb("th_rm", [P, 16, 4], F32)
        gate_p = sb("gate_p", [P, 3, EXPERTS], F16)

        arena = sb("arena", [P, ARENA], F32)

        def carve(memory, at, words, dt=F32):
            a = memory[:, at:at + words]
            return a if dt == F32 else a.bitcast(dt)

        qbd = carve(arena, 0, 2048, F16).rearrange("p (l c b h q) -> p l c b h q", l=2, c=C, b=NB, h=8)
        ctx_np = carve(arena, 0, 2048, F16).rearrange("p (l b m d) -> p l b m d", l=2, b=NB, m=2)
        stage_t = carve(arena, 8198, 2 * C * KEYS).rearrange("p (s n) -> p s n", s=2)
        stage_n = carve(arena, 8198 + 2 * C * KEYS, 4 * D).rearrange("p (s n) -> p s n", s=2)
        stage_l = arena[0:NB, 8198 + 2 * C * KEYS + 4 * D:ARENA]
        probs = carve(arena, 2048, 1028)
        pt1 = carve(arena, 3076, 384, F16).rearrange("p (l n) -> p l n", l=2)
        s2 = carve(arena, 3584, 512)
        pt2 = carve(arena, 4096, 512, F16).rearrange("p (l g n) -> p l g n", l=2, g=GROUPS)
        vblk = carve(arena, 4608, 1024, F16).rearrange("p (l g b d) -> p l g b d", l=2, g=GROUPS, b=NB)
        v2 = carve(arena, 5632, 256, F16).rearrange("p (l n) -> p l n", l=2)
        om_f = carve(arena, 6144, 1024)
        om = carve(arena, 7168, 1024, F16).rearrange("p (l b n) -> p l b n", l=2, b=NB)
        th3 = carve(arena, 2048, 1024)
        r3 = carve(arena, 3072, 1024)
        rq3 = carve(arena, 4096, 1024)
        hq = carve(arena, 5120, 512, BF16)
        hqt = carve(arena, 5632, 512, BF16).rearrange("p (k n) -> p k n", k=8)
        xq_f = carve(arena, 6144, 256)
        xq = carve(arena, 6400, 128, BF16)
        xqt = carve(arena, 6528, 128, BF16).rearrange("p (c n) -> p c n", c=C)
        kp = carve(arena, 3076, 514, F16).rearrange("p (l c m) -> p l c m", l=2, c=C)
        vp = carve(arena, 3590, 1024, F16).rearrange("p (s l m n) -> p s l m n", s=2, l=2, m=2)
        pt4 = carve(arena, 4614, 3072, F16).rearrange("p (s l g n) -> p s l g n", s=2, l=2, g=GROUPS)
        om4_f = carve(arena, 7686, 256)
        om4 = carve(arena, 7942, 256, F16).rearrange("p (l g d) -> p l g d", l=2, g=GROUPS)
        v5 = carve(arena, 2048, 1024, F16).rearrange("p (l n) -> p l n", l=2)
        s5 = carve(arena, 3072, 512)
        pt5 = carve(arena, 3584, 512, F16).rearrange("p (l g n) -> p l g n", l=2, g=GROUPS)
        ptb = carve(arena, 4096, 2048, F16).rearrange("p (l g b n) -> p l g b n", l=2, g=GROUPS, b=NB)
        o5_f = carve(arena, 6144, 1024)
        o5 = carve(arena, 7168, 1024, F16).rearrange("p (l j n) -> p l j n", l=2, j=8)
        wb = carve(arena, 2048, 1024).rearrange("p (e n) -> p e n", e=EXPERTS)
        mb = carve(arena, 3072, 1024).rearrange("p (e n) -> p e n", e=EXPERTS)
        u4 = carve(arena, 4096, 1024).rearrange("p (s c n) -> p s c n", s=2, c=4)
        th6 = carve(arena, 5120, 512)
        v6 = carve(arena, 5632, 256)
        h_f = carve(arena, 5888, 512)
        hp = carve(arena, 6400, 512, F16)
        x2_f = carve(arena, 6912, 256)
        a3_f = carve(arena, 7168, 256)
        y = carve(arena, 7424, 256)
        prod = carve(arena, 7680, 256)

        ps = ctx.enter_context(nc.psum_tensor("ps", [P, 8, 512], F32))

        G = {}
        for n in SETUP_SIGNALS + list(PER_TRIP):
            G[n] = sem(n)
        s = G

        block = ctx.enter_context(nc.Block())

        def at(trip, name, n):
            return trip * PER_TRIP[name] + n + (1 if name in AHEAD else 0)

        @block.sync
        def _(sp):
            for name in AHEAD:
                sp.sem_inc(s[name], 1)
            sp.dma_start(cst[:, :], consts).then_inc(s["const_in"], 16)
            sp.dma_start(bias[:, :], biases).then_inc(s["const_in"], 16)
            sp.dma_start(row_bias[:, :, :], rows.rearrange("p (r n) -> p r n", r=4)).then_inc(s["const_in"], 16)
            for i in range(3):
                sp.dma_start(carve(arena, 2048 * i, 2048), ffn[i]).then_inc(s["ffn_in"], 16)
            with sp.Fori(0, W_COLS // (W_CHUNK * W_SLOTS)) as g:
                for j in range(W_SLOTS):
                    sp.wait_ge(s["w_split"], g * W_SLOTS + 1)
                    sp.dma_start(carve(arena, 6144 + W_CHUNK * j, W_CHUNK),
                                 weights[:, bass.ds((g * W_SLOTS + j) * W_CHUNK, W_CHUNK)]).then_inc(s[f"w_in{j}"], 16)
            sp.wait_ge(s["w_split"], W_COLS // W_CHUNK + 1)
            with sp.Fori(0, TILES) as t:
                sp.wait_ge(s["x_1"], at(t, "x_1", 0))
                sp.dma_start(x0[:, :], x_in[bass.ds(t, 1)].rearrange("t p d -> (t p) d")).then_inc(s["x_in"], 16)
                sp.wait_ge(s["ctx_done"], at(t, "ctx_done", 0))
                sp.dma_start(stage_l, ctx_l[bass.ds(t, 1)].rearrange("t p d -> (t p) d")).then_inc(s["last_in"], 16)
                for b in range(NB):
                    sp.wait_ge(s["ctx_done"], at(t, "ctx_done", 2 * b - 1 if b >= 2 else 0))
                    sp.dma_start(stage_t[:, b % 2, :], ctx_t[bass.ds(t, 1), b].rearrange("t p n -> (t p) n")).then_inc(s[f"ctx_in{b % 2}"], 16)
                    sp.dma_start(stage_n[:, b % 2, :], ctx_n[bass.ds(t, 1), b].rearrange("t p n -> (t p) n")).then_inc(s[f"ctx_in{b % 2}"], 16)

        @block.gpsimd
        def _(pool):
            pool.memset(ones[:, :], 1.0).then_inc(s["pool_set"], 1)
            pool.memset(neg_half[:, :], -0.5).then_inc(s["pool_set"], 1)
            pool.memset(last_cols[:, :, :], 0.0).then_inc(s["pool_set"], 1)
            pool.memset(qb5[:, :, :, :, :, :], 0.0).then_inc(s["pool_set"], 1)
            pool.memset(vl[:, :, :], 0.0).then_inc(s["pool_set"], 1)
            pool.memset(ctx_lp[:, :, :], 0.0).then_inc(s["pool_set"], 1)
            pool.wait_ge(s["const_in"], 48)
            pool.tensor_copy(ident16[:, :], ident).then_inc(s["pool_set"], 1)
            pool.tensor_copy(identb[:, :], ident).then_inc(s["pool_set"], 1)
            pool.tensor_copy(sel16[:, :], const("sel")).then_inc(s["pool_set"], 1)
            pool.wait_ge(s["pool_set"], 9)
            pool.wait_ge(s["dve_setup"], SETUP_STEPS)
            pool.wait_ge(s["w_split"], W_COLS // W_CHUNK + 1)
            with pool.Fori(0, TILES) as t:
                pool.wait_ge(s["last_hi"], t + 1)
                pool.tensor_tensor(ctx_lp[0:NB, 1, :], stage_l, ctx_lp[0:NB, 0, :], ALU.subtract).then_inc(s["ctx_done"], 1)
                for b in range(NB):
                    st = stage_t[:, b % 2, :].rearrange("p (c m) -> p c m", c=C)
                    sn = stage_n[:, b % 2, :].rearrange("p (m d) -> p m d", m=2)
                    pool.wait_ge(s["ctx_hi"], at(t, "ctx_hi", 2 * b + 2))
                    pool.tensor_tensor(ctx_tp[:, 1, :, b, :], st, ctx_tp[:, 0, :, b, :], ALU.subtract).then_inc(s["ctx_done"], 1)
                    pool.tensor_tensor(ctx_np[:, 1, b], sn, ctx_np[:, 0, b], ALU.subtract).then_inc(s["ctx_done"], 1)

                def power(n):
                    pool.wait_ge(s["ln_var"], at(t, "ln_var", n + 1))
                    pool.tensor_tensor(rstd[:, :], var_eps[:, :], neg_half[:, :], ALU.pow).then_inc(s["ln_rstd"], 1)

                power(0)
                power(1)
                pool.wait_ge(s["om_hi"], t + 1)
                pool.tensor_tensor(om[:, 1].rearrange("p b n -> p (b n)"), om_f,
                                   om[:, 0].rearrange("p b n -> p (b n)"), ALU.subtract).then_inc(s["om_lo"], 1)
                power(2)
                power(3)
                for b in range(NB):
                    pool.wait_ge(s["om4_hi"], at(t, "om4_hi", b + 1))
                    pool.tensor_tensor(om4[:, 1].rearrange("p g d -> p (g d)"), om4_f,
                                       om4[:, 0].rearrange("p g d -> p (g d)"), ALU.subtract).then_inc(s["om4_lo"], 1)
                power(4)
                for g in range(GROUPS):
                    pool.wait_ge(s["qk5_hi"], at(t, "qk5_hi", g + 1))
                    pool.tensor_tensor(qk[:, 1], qk_f[:, :, :], qk[:, 0], ALU.subtract).then_inc(s["qk5_lo"], 1)
                pool.wait_ge(s["o5_hi"], t + 1)
                pool.tensor_tensor(o5[:, 1].rearrange("p j n -> p (j n)"), o5_f,
                                   o5[:, 0].rearrange("p j n -> p (j n)"), ALU.subtract).then_inc(s["o5_lo"], 1)
                power(5)
                pool.wait_ge(s["sh_hi"], t + 1)
                pool.tensor_tensor(hp[:, 512:1024], h_f, hp[:, 0:512], ALU.subtract).then_inc(s["sh_lo"], 1)
                for e in range(EXPERTS):
                    if e == 0:
                        pool.wait_ge(s["y_0"], t + 1)
                    pool.wait_ge(s["he_hi"], at(t, "he_hi", e + 1))
                    pool.tensor_tensor(hp[:, 256:512], h_f[:, 0:256], hp[:, 0:256], ALU.subtract).then_inc(s["he_lo"], 1)
                    pool.wait_ge(s["a3"], at(t, "a3", e + 1))
                    pool.tensor_tensor(prod, x2_f, a3_f, ALU.mult).then_inc(s["prod"], 1)
                    pool.wait_ge(s["prod"], at(t, "prod", e + 1))
                    pool.tensor_tensor(y, y, prod, ALU.add).then_inc(s["y_add"], 1)
                    pool.wait_ge(s["y_add"], at(t, "y_add", e + 1))

        @block.scalar
        def _(act):
            with act.Fori(0, W_COLS // (W_CHUNK * W_SLOTS)) as g:
                for j in range(W_SLOTS):
                    act.wait_ge(s[f"w_in{j}"], g * 16 + 16)
                    act.activation(wp[:, 0, bass.ds((g * W_SLOTS + j) * W_CHUNK, W_CHUNK)],
                                   carve(arena, 6144 + W_CHUNK * j, W_CHUNK), ACT.Copy).then_inc(s["w_hi"], 1)
            with act.Fori(0, TILES) as t:
                def copy(dst, src, done, ready, n=1):
                    act.wait_ge(s[ready], at(t, ready, n))
                    act.activation(dst, src, ACT.Copy).then_inc(s[done], 1)

                def xt_hi(n):
                    copy(xt[:, 0].rearrange("p c n -> p (c n)"), ps[:, 0, 0:D], "xt_hi", "xt_ps", n + 1)

                act.wait_ge(s["pool_set"], 9)
                act.wait_ge(s["y4_ps"], at(t, "y4_ps", 0))
                act.wait_ge(s["last_in"], t * 16 + 16)
                act.activation(ctx_lp[0:NB, 0, :], stage_l, ACT.Copy).then_inc(s["last_hi"], 1)
                for b in range(NB):
                    act.wait_ge(s[f"ctx_in{b % 2}"], t * 64 + 32 * (b // 2) + 32)
                    act.activation(ctx_tp[:, 0, :, b, :], stage_t[:, b % 2, :].rearrange("p (c m) -> p c m", c=C), ACT.Copy).then_inc(s["ctx_hi"], 1)
                    act.activation(ctx_np[:, 0, b], stage_n[:, b % 2, :].rearrange("p (m d) -> p m d", m=2), ACT.Copy).then_inc(s["ctx_hi"], 1)

                xt_hi(0)
                act.wait_ge(s["q0_f"], t + 1)
                act.activation(qk[:, 0, 0:2], qk_f[:, 0:2], ACT.Copy).then_inc(s["q0_hi"], 1)
                copy(qk[:, 0, 2:4].rearrange("p c n -> p (c n)"), ps[:, 2, 0:D], "qp_hi", "qp_ps")
                act.wait_ge(s["s1_bias"], t + 1)
                act.activation(probs[:, 0:KEYS], ps[:, 4, 0:KEYS], ACT.Exp, bias=small[:, 3:4], scale=D ** -0.5,
                               accum_out=small[:, 4:5]).then_inc(s["p1"], 1)
                copy(pt1[:, 0, :], ps[:, 5, 0:384], "pt1_hi", "pt1_ps")
                copy(op[:, 0].rearrange("p c n -> p (c n)"), ps[:, 6, 0:D], "a1_hi", "a1_ps")
                xt_hi(1)
                act.wait_ge(s["qk2_f"], t + 1)
                act.activation(qk[:, 0], qk_f[:, :, :], ACT.Copy).then_inc(s["qk2_hi"], 1)
                copy(v2[:, 0, :], ps[:, 3, 0:D], "v2_hi", "v2_ps")
                act.wait_ge(s["s2_shift"], t + 1)
                act.activation(probs[:, 0:512], s2, ACT.Exp, scale=16 ** -0.5).then_inc(s["p2"], 1)
                copy(pt2[:, 0].rearrange("p g n -> p (g n)"), ps[:, 5, :], "pt2_hi", "pt2_ps")
                act.wait_ge(s["om_f"], at(t, "om_f", 4))
                act.activation(om[:, 0].rearrange("p b n -> p (b n)"), om_f, ACT.Copy).then_inc(s["om_hi"], 1)
                for c in range(C):
                    if c == 0:
                        act.wait_ge(s["o2_ps"], t + 1)
                    act.activation(op[:, 0, c], ps[:, 1, c * P:(c + 1) * P], ACT.Identity, bias=bcol("bv0")[:, c:c + 1]).then_inc(s["o2_hi"], 1)
                copy(xqt.rearrange("p c n -> p (c n)"), ps[:, 0, 0:P].bitcast(BF16), "xqt", "xq_ps")
                act.wait_ge(s["gate_ps"], t + 1)
                act.activation(th3, ps[:, 1:3, :].rearrange("p a n -> p (a n)"), ACT.Tanh, scale=small[:, 11:12]).then_inc(s["th3"], 1)
                copy(hqt.rearrange("p k n -> p (k n)"), ps[:, 5, :].bitcast(BF16), "hqt", "hq_ps")
                xt_hi(2)
                copy(qk[:, 0, 0:2].rearrange("p c n -> p (c n)"), ps[:, 1, 0:D], "q4_hi", "q4_ps")
                copy(vl[0:NB, 0, :], ps[0:NB, 3, 0:D], "vl_hi", "vl_ps")

                def k_hi(b):
                    copy(kp[:, 0], ps[:, 0:2, 0:KEYS], "k4_hi", "k4_ps", b + 1)

                def v_hi(b):
                    if b >= 2:
                        act.wait_ge(s["o4_ps"], at(t, "o4_ps", b - 1))
                    copy(vp[:, b % 2, 0].rearrange("p m n -> p (m n)"), ps[:, 2, :], "v4_hi", "v4_ps", b + 1)

                def om_hi(b):
                    act.wait_ge(s["om4_f"], at(t, "om4_f", b + 1))
                    act.activation(om4[:, 0].rearrange("p g d -> p (g d)"), om4_f, ACT.Copy).then_inc(s["om4_hi"], 1)

                def sel_hi(b):
                    copy(op[:, 0, :, SEQ * b:SEQ * (b + 1)], ps[:, 3, 256:320].rearrange("p (c n) -> p c n", c=C), "sel_hi", "sel_ps", b + 1)

                k_hi(0)
                v_hi(0)
                for b in range(NB):
                    act.wait_ge(s["s4_bias"], at(t, "s4_bias", b + 1))
                    for g in range(GROUPS):
                        act.activation(probs[:, KEYS * g:KEYS * (g + 1)], ps[:, 4 + g, 0:KEYS], ACT.Exp, bias=small[:, 24 + g:25 + g],
                                       scale=16 ** -0.5, accum_out=small[:, 28 + g:29 + g]).then_inc(s["p4"], 1)
                    if b >= 2:
                        sel_hi(b - 2)
                    if b + 1 < NB:
                        k_hi(b + 1)
                    copy(pt4[:, b % 2, 0], ps[:, 4:8, 0:384], "pt4_hi", "pt4_ps", b + 1)
                    if b + 1 < NB:
                        v_hi(b + 1)
                    if b >= 1:
                        om_hi(b - 1)
                sel_hi(NB - 2)
                om_hi(NB - 1)
                sel_hi(NB - 1)
                xt_hi(3)
                copy(v5[:, 0, :], ps[:, 2:4, :].rearrange("p a n -> p (a n)"), "v5_hi", "v5_ps")
                for g in range(GROUPS):
                    act.wait_ge(s["qk5_f"], at(t, "qk5_f", g + 1))
                    act.activation(qk[:, 0], qk_f[:, :, :], ACT.Copy).then_inc(s["qk5_hi"], 1)
                act.wait_ge(s["s5_shift"], t + 1)
                act.activation(s5, s5, ACT.Exp, scale=64 ** -0.5).then_inc(s["p5"], 1)
                copy(pt5[:, 0].rearrange("p g n -> p (g n)"), ps[:, 5, :], "pt5_hi", "pt5_ps")
                act.wait_ge(s["o5_f"], at(t, "o5_f", 8))
                act.activation(o5[:, 0].rearrange("p j n -> p (j n)"), o5_f, ACT.Copy).then_inc(s["o5_hi"], 1)
                xt_hi(4)
                act.wait_ge(s["gate_max"], t + 1)
                act.activation(small[:, 48:56], ps[:, 7, 0:EXPERTS], ACT.Exp, bias=small[:, 40:41], accum_out=small[:, 41:42]).then_inc(s["gate_exp"], 1)
                act.wait_ge(s["sh_ps"], t + 1)
                act.activation(th6, ps[:, 1, :], ACT.Tanh, scale=0.5).then_inc(s["th_sh"], 1)
                act.wait_ge(s["sh_f"], t + 1)
                act.activation(hp[:, 0:512], h_f, ACT.Copy).then_inc(s["sh_hi"], 1)
                act.wait_ge(s["wb_ps"], t + 1)
                act.activation(wb, ps[:, 3:5, :].rearrange("p a (e n) -> p (a e) n", n=P), ACT.Copy).then_inc(s["wb"], 1)
                act.activation(mb, ps[:, 5:7, :].rearrange("p a (e n) -> p (a e) n", n=P), ACT.Copy).then_inc(s["wb"], 1)
                for e in range(EXPERTS):
                    act.wait_ge(s["u4"], at(t, "u4", e + 1))
                    for c in range(C):
                        k = e * C + c
                        act.activation(th6[:, c * P:(c + 1) * P], u4[:, e % 2, c], ACT.Tanh, scale=0.5, bias=half_b1[:, k:k + 1]).then_inc(s["th_e"], 1)
                    for c in range(C):
                        k = e * C + c
                        act.activation(v6[:, c * P:(c + 1) * P], u4[:, e % 2, c], ACT.Identity, bias=bcol("b1")[:, k:k + 1]).then_inc(s["th_e"], 1)
                    act.wait_ge(s["he_f"], at(t, "he_f", e + 1))
                    if e >= 1:
                        act.wait_ge(s["e2_ps"], at(t, "e2_ps", e))
                    act.activation(hp[:, 0:256], h_f[:, 0:256], ACT.Copy).then_inc(s["he_hi"], 1)
                act.wait_ge(s["x_final"], t + 1)
                act.dma_start(out[bass.ds(t, 1)].rearrange("t p d -> (t p) d"), x_out[:, :]).then_inc(s["stored"], 16)
            act.wait_ge(s["stored"], 16 * TILES + 1)

        @block.tensor
        def _(pe):
            def product(dst, pairs, start=True, stop=True):
                n = len(pairs)
                last = None
                for i, ((lh, ll), (rh, rl)) in enumerate(pairs):
                    terms = [(lh, rh)]
                    if rl is not None:
                        terms.append((lh, rl))
                    if ll is not None:
                        terms.append((ll, rh))
                    for j, (a, b) in enumerate(terms):
                        last = pe.matmul(dst, a, b, start=start and i == 0 and j == 0,
                                         stop=stop and i == n - 1 and j == len(terms) - 1)
                return last

            def feature_major(dst, name, n, act_pair, chunks, first=0, k=C):
                for i, oc in enumerate(chunks):
                    last = product(dst[:, i * P:(i + 1) * P], [
                        ((w(name, 0, k, n, first)[:, kc, oc * P:(oc + 1) * P], w(name, 1, k, n, first)[:, kc, oc * P:(oc + 1) * P]),
                         (act_pair[:, 0, kc], act_pair[:, 1, kc])) for kc in range(k)])
                return last

            def token_major(dst, name, n, act_pair, lo, hi, k=C):
                return product(dst, [
                    ((act_pair[:, 0, kc], act_pair[:, 1, kc]), (w(name, 0, k, n)[:, kc, lo:hi], w(name, 1, k, n)[:, kc, lo:hi]))
                    for kc in range(k)])

            pe.wait_ge(s["pool_set"], 9)
            pe.wait_ge(s["ffn_abs"], 3)
            pe.matmul(ps[:, 0, 0:3], ones[:, :], stat[:, 0:3], start=True, stop=True).then_inc(s["ffn_sum"], 1)
            pe.wait_ge(s["w_split"], W_COLS // W_CHUNK + 1)
            pe.wait_ge(s["dve_setup"], SETUP_STEPS)
            with pe.Fori(0, TILES) as t:
                def need(name, n=1):
                    pe.wait_ge(s[name], at(t, name, n))

                def transpose_x(n):
                    need("xn", n + 1)
                    for c in range(C):
                        last = pe.transpose(ps[:, 0, c * P:(c + 1) * P], xn[:, c * P:(c + 1) * P], ident)
                    last.then_inc(s["xt_ps"], 1)
                    need("xt_lo", n + 1)

                transpose_x(0)
                feature_major(ps[:, 1], "q0", D, xt, range(C)).then_inc(s["q0_ps"], 1)
                need("q0_lo")
                feature_major(ps[:, 2], "k0t", D, qk[:, :, 0:2], range(C)).then_inc(s["qp_ps"], 1)
                product(ps[:, 3, 0:1], [((qk[:, 0, c], qk[:, 1, c]), (bk_pair[:, 0, c:c + 1], bk_pair[:, 1, c:c + 1]))
                                        for c in range(C)]).then_inc(s["qbk_ps"], 1)
                need("qp_lo")
                need("ctx_done", 9)
                for c in range(C):
                    for a, r in ((0, 0), (0, 1), (1, 0)):
                        for b in range(NB):
                            last = pe.matmul(ps[SEQ * b:SEQ * (b + 1), 4, 0:KEYS], qk[:, a, 2 + c, SEQ * b:SEQ * (b + 1)], ctx_tp[:, r, c, b, :],
                                             start=(c == 0 and a == 0 and r == 0), stop=(c == 1 and a == 1))
                last.then_inc(s["s1_ps"], 1)
                need("p1_last")
                for m in range(3):
                    src = probs[:, m * P:(m + 1) * P] if m < 2 else last_cols[:, 0, :]
                    last = pe.transpose(ps[:, 5, m * P:(m + 1) * P], src, ident)
                last.then_inc(s["pt1_ps"], 1)
                need("pt1_lo")
                for c in range(C):
                    cols = slice(c * P, (c + 1) * P)
                    product(ps[:, 6, cols], [((ctx_lp[:, 0, cols], ctx_lp[:, 1, cols]), (pt1[:, 0, 256:384], pt1[:, 1, 256:384]))], stop=False)
                    for b in range(NB):
                        for m in range(2):
                            toks = slice(m * P + SEQ * b, m * P + SEQ * (b + 1))
                            last = product(ps[:, 6, c * P + SEQ * b:c * P + SEQ * (b + 1)],
                                           [((ctx_np[:, 0, b, m, cols], ctx_np[:, 1, b, m, cols]), (pt1[:, 0, toks], pt1[:, 1, toks]))],
                                           start=False, stop=(b == NB - 1 and m == 1))
                last.then_inc(s["a1_ps"], 1)
                need("a1_lo")
                token_major(ps[:, 7, 0:D], "v0", D, op, 0, D).then_inc(s["y1_ps"], 1)

                transpose_x(1)
                feature_major(ps[:, 1], "qkv0", 3 * D, xt, range(4)).then_inc(s["qk2_ps"], 1)
                token_major(ps[:, 3, 0:D], "qkv0", 3 * D, xt, 2 * D, 3 * D).then_inc(s["v2_ps"], 1)
                need("qbd2")
                for g in range(GROUPS):
                    c, h = g // 2, 4 * (g % 2)
                    for b in range(NB):
                        q = [qbd[:, a, c, b, h:h + 4, :].rearrange("p h q -> p (h q)") for a in range(2)]
                        k = [qk[:, a, 2 + c, SEQ * b:SEQ * (b + 1)] for a in range(2)]
                        last = product(ps[:, 4, g * P + SEQ * b:g * P + SEQ * (b + 1)], [((q[0], q[1]), (k[0], k[1]))])
                last.then_inc(s["s2_ps"], 1)
                need("p2")
                for g in range(GROUPS):
                    last = pe.transpose(ps[:, 5, g * P:(g + 1) * P], probs[:, g * P:(g + 1) * P], ident)
                last.then_inc(s["pt2_ps"], 1)
                need("vblk")
                need("pt2_lo")
                for g in range(GROUPS):
                    v = [vblk[:, a, g].rearrange("p b d -> p (b d)") for a in range(2)]
                    last = product(ps[:, 6 + g // 2, (g % 2) * D:(g % 2 + 1) * D], [((pt2[:, 0, g], pt2[:, 1, g]), (v[0], v[1]))])
                last.then_inc(s["o2g_ps"], 1)
                need("om_lo")
                for c in range(C):
                    for b in range(NB):
                        for a in range(2):
                            last = pe.matmul(ps[:, 1, c * P + SEQ * b:c * P + SEQ * (b + 1)], om[:, a, b, c * P:(c + 1) * P], sel16[:, :],
                                             start=(a == 0), stop=(a == 1))
                last.then_inc(s["o2_ps"], 1)
                need("o2_lo", 2)
                token_major(ps[:, 2, 0:D], "o0", D, op, 0, D).then_inc(s["y2_ps"], 1)

                need("xq")
                for c in range(C):
                    last = pe.transpose(ps[:, 0, c * 64:(c + 1) * 64].bitcast(BF16), xq[:, c * P:(c + 1) * P], identb[:, :])
                last.then_inc(s["xq_ps"], 1)
                need("xqt")
                for i, name in ((0, "gate_ps"), (1, "up_ps")):
                    wt = ffn_w[:, i, :].rearrange("p (k n) -> p k n", k=C)
                    for j in range(2):
                        for kc in range(C):
                            last = pe.matmul(ps[:, 1 + 2 * i + j, :], xqt[:, kc], wt[:, kc, 512 * j:512 * (j + 1)], start=(kc == 0), stop=(kc == 1))
                    last.then_inc(s[name], 1)
                need("hq")
                for k in range(8):
                    last = pe.transpose(ps[:, 5, k * 64:(k + 1) * 64].bitcast(BF16), hq[:, k * P:(k + 1) * P], identb[:, :])
                last.then_inc(s["hq_ps"], 1)
                need("hqt")
                wt = ffn_w[:, 2, :].rearrange("p (k n) -> p k n", k=8)
                for k in range(8):
                    last = pe.matmul(ps[:, 6, 0:D], hqt[:, k], wt[:, k, :], start=(k == 0), stop=(k == 7))
                last.then_inc(s["y3_ps"], 1)

                transpose_x(2)
                feature_major(ps[:, 1], "xq", D, xt, range(C)).then_inc(s["q4_ps"], 1)
                product(ps[0:NB, 3, 0:D], [((ctx_tp[:, 0, c, :, KEYS - 1], ctx_tp[:, 1, c, :, KEYS - 1]),
                                            (w("xkv", 0, C, 2 * D)[:, c, D:2 * D], w("xkv", 1, C, 2 * D)[:, c, D:2 * D])) for c in range(C)]
                        ).then_inc(s["vl_ps"], 1)
                need("q4_lo")
                need("vl_lo")

                def keys_values(b):
                    if b >= 1:
                        need("k4_lo", b)
                    for oc in range(C):
                        last = product(ps[:, oc, 0:KEYS], [
                            ((w("xkv", 0, C, 2 * D)[:, kc, oc * P:(oc + 1) * P], w("xkv", 1, C, 2 * D)[:, kc, oc * P:(oc + 1) * P]),
                             (ctx_tp[:, 0, kc, b, :], ctx_tp[:, 1, kc, b, :])) for kc in range(C)])
                    last.then_inc(s["k4_ps"], 1)
                    if b >= 1:
                        need("v4_lo", b)
                    for m in range(2):
                        last = product(ps[:, 2, m * D:(m + 1) * D], [
                            ((ctx_tp[:, 0, kc, b, m * P:(m + 1) * P], ctx_tp[:, 1, kc, b, m * P:(m + 1) * P]),
                             (w("xkv", 0, C, 2 * D)[:, kc, D:2 * D], w("xkv", 1, C, 2 * D)[:, kc, D:2 * D])) for kc in range(C)])
                    last.then_inc(s["v4_ps"], 1)

                def scores(b):
                    need("k4_lo", b + 1)
                    if b == 0:
                        need("qbd4")
                    else:
                        need("pt4_lo", b)
                    for g in range(GROUPS):
                        c, h = g // 2, 4 * (g % 2)
                        q = [qbd[:, a, c, b, h:h + 4, :].rearrange("p h q -> p (h q)") for a in range(2)]
                        last = product(ps[:, 4 + g, 0:KEYS], [((q[0], q[1]), (kp[:, 0, c], kp[:, 1, c]))])
                    last.then_inc(s["s4_ps"], 1)

                def turn_probs(b):
                    need("p4_last", b + 1)
                    for g in range(GROUPS):
                        for m in range(3):
                            src = probs[:, KEYS * g + m * P:KEYS * g + (m + 1) * P] if m < 2 else last_cols[:, g, :]
                            last = pe.transpose(ps[:, 4 + g, m * P:(m + 1) * P], src, ident)
                    last.then_inc(s["pt4_ps"], 1)

                def values(b):
                    need("pt4_lo", b + 1)
                    need("v4_lo", b + 1)
                    if b >= 1:
                        need("sel_lo", b)
                    for g in range(GROUPS):
                        cols = slice(64 * g, 64 * (g + 1))
                        pt = [[pt4[:, b % 2, a, g, m * P:(m + 1) * P] for a in range(2)] for m in range(3)]
                        last = product(ps[:, 3, cols], [
                            ((pt[m][0], pt[m][1]), (vp[:, b % 2, 0, m, cols], vp[:, b % 2, 1, m, cols])) if m < 2 else
                            ((pt[m][0], pt[m][1]), (vl[:, 0, cols], vl[:, 1, cols])) for m in range(3)])
                    last.then_inc(s["o4_ps"], 1)

                def select(b):
                    need("om4_lo", b + 1)
                    for c in range(C):
                        for a in range(2):
                            last = pe.matmul(ps[:, 3, 256 + SEQ * c:256 + SEQ * (c + 1)], om4[:, a, 2 * c:2 * c + 2, :].rearrange("p g d -> p (g d)"), sel16[:, :],
                                             start=(a == 0), stop=(a == 1))
                    last.then_inc(s["sel_ps"], 1)

                keys_values(0)
                for b in range(NB):
                    scores(b)
                    if b >= 2:
                        select(b - 2)
                    if b + 1 < NB:
                        keys_values(b + 1)
                    turn_probs(b)
                    if b >= 1:
                        values(b - 1)
                select(NB - 2)
                values(NB - 1)
                select(NB - 1)
                need("sel_lo", NB)
                token_major(ps[:, 7, 0:D], "xo", D, op, 0, D).then_inc(s["y4_ps"], 1)

                def self_scores(g):
                    need("qb5", g + 1)
                    for b in range(NB):
                        last = product(ps[:, 4, g * P + SEQ * b:g * P + SEQ * (b + 1)], [
                            ((qb5[:, 0, c, b].rearrange("p h q -> p (h q)"), qb5[:, 1, c, b].rearrange("p h q -> p (h q)")),
                             (qk[:, 0, 2 + c, SEQ * b:SEQ * (b + 1)], qk[:, 1, 2 + c, SEQ * b:SEQ * (b + 1)])) for c in range(C)])
                    last.then_inc(s["s5_ps"], 1)

                transpose_x(3)
                for j in range(2):
                    last = token_major(ps[:, 2 + j, :], "av", WIDE, xt, 512 * j, 512 * (j + 1))
                last.then_inc(s["v5_ps"], 1)
                for g in range(GROUPS):
                    if g >= 2:
                        need("qk5_f", g - 1)
                    bank = ps[:, 6 + g % 2]
                    feature_major(bank[:, 0:D], "aq", WIDE, xt, range(2 * g, 2 * g + 2))
                    feature_major(bank[:, D:2 * D], "ak", WIDE, xt, range(2 * g, 2 * g + 2)).then_inc(s["qk5_ps"], 1)
                    if g >= 1:
                        self_scores(g - 1)
                self_scores(GROUPS - 1)
                need("p5_norm")
                for g in range(GROUPS):
                    last = pe.transpose(ps[:, 5, g * P:(g + 1) * P], s5[:, g * P:(g + 1) * P], ident)
                last.then_inc(s["pt5_ps"], 1)
                need("ptb")
                need("v5_lo")
                for j in range(8):
                    bank = (6, 7, 0, 1)[j // 2]
                    hh = (j % 2) * 64
                    pt = [ptb[:, a, j // 2, :, hh:hh + 64] for a in range(2)]
                    last = product(ps[:, bank, (j % 2) * D:(j % 2 + 1) * D],
                                   [((v5[:, 0, j * P:(j + 1) * P], v5[:, 1, j * P:(j + 1) * P]), (pt[0], pt[1]))])
                    if j % 2:
                        last.then_inc(s["o5_ps"], 1)
                need("o5_lo")
                token_major(ps[:, 2, 0:D], "ao", D, o5, 0, D, k=8).then_inc(s["y5_ps"], 1)

                transpose_x(4)
                token_major(ps[:, 7, 0:EXPERTS], "gate", EXPERTS, xt, 0, EXPERTS).then_inc(s["logit_ps"], 1)
                feature_major(ps[:, 1], "sw1", SHARED, xt, range(4))
                feature_major(ps[:, 2], "sw2", SHARED, xt, range(4)).then_inc(s["sh_ps"], 1)
                need("gate_p")
                for e in range(EXPERTS):
                    for a in range(2):
                        pe.matmul(ps[:, 3 + e // 4, (e % 4) * P:(e % 4 + 1) * P], gate_p[:, a, e:e + 1].to_broadcast([P, P]), ident16[:, :],
                                  start=(a == 0), stop=(a == 1))
                    last = pe.matmul(ps[:, 5 + e // 4, (e % 4) * P:(e % 4 + 1) * P], gate_p[:, 2, e:e + 1].to_broadcast([P, P]), ident16[:, :],
                                     start=True, stop=True)
                last.then_inc(s["wb_ps"], 1)
                need("sh_lo")
                sp_pair = hp.rearrange("p (l k n) -> p l k n", l=2, k=4)
                feature_major(ps[:, 0], "sw3", D, sp_pair, range(C), k=4).then_inc(s["z_ps"], 1)

                def expert_in(e):
                    if e < 2:
                        need("sh_f")
                    else:
                        need("u4", e - 1)
                    bank = ps[:, 1 + e % 2]
                    feature_major(bank[:, 0:D], "w1", D, xt, range(C), first=e * C * D)
                    feature_major(bank[:, D:2 * D], "w3", D, xt, range(C), first=e * C * D).then_inc(s["e13_ps"], 1)

                he = hp[:, 0:512].rearrange("p (l k n) -> p l k n", l=2, k=C)
                expert_in(0)
                for e in range(EXPERTS):
                    if e + 1 < EXPERTS:
                        expert_in(e + 1)
                    need("he_lo", e + 1)
                    if e == 0:
                        need("wb", 2)
                    if e >= 2:
                        need("x2", 2 * (e - 1))
                    feature_major(ps[:, 3 + e % 2], "w2", D, he, range(C), first=e * C * D).then_inc(s["e2_ps"], 1)
                need("y_add", EXPERTS)
                for c in range(C):
                    last = pe.transpose(ps[:, 0, c * P:(c + 1) * P], y[:, c * P:(c + 1) * P], ident)
                last.then_inc(s["y6_ps"], 1)

        @block.vector
        def _(dve):
            made = [0]
            dve.wait_ge(s["ffn_in"], 48)
            n0 = [0]

            def first(ins):
                n0[0] += 1
                ins.then_inc(s["dve_setup"], 1)
                dve.wait_ge(s["dve_setup"], n0[0])

            for i in range(3):
                dve.tensor_reduce(stat[:, i:i + 1], carve(arena, 2048 * i, 2048), X, ALU.add, apply_absolute_value=True).then_inc(s["ffn_abs"], 1)
            dve.wait_ge(s["ffn_sum"], 1)
            first(dve.tensor_scalar(ffn_inv[:, :], ps[:, 0, 0:3], 1.0 / (WIDE * D), 1e-5, ALU.mult, ALU.max))
            first(dve.reciprocal(stat[:, 4:7], ffn_inv[:, :]))
            for i in range(3):
                wf = carve(arena, 2048 * i, 2048)
                first(dve.tensor_scalar(wf, wf, stat[:, 4 + i:5 + i], 2.0, ALU.mult, ALU.min))
                first(dve.tensor_scalar(wf, wf, -2.0, ROUND, ALU.max, ALU.add))
                first(dve.tensor_scalar(wf, wf, ROUND, 1.0, ALU.subtract, ALU.min))
                first(dve.tensor_scalar(ffn_w[:, i, :], wf, -1.0, None, ALU.max))
            dve.wait_ge(s["const_in"], 48)
            first(dve.tensor_copy(bk_pair[:, 0, :], bcol("bk0")))
            first(dve.tensor_tensor(bk_pair[:, 1, :], bcol("bk0"), bk_pair[:, 0, :], ALU.subtract))
            first(dve.tensor_scalar(half_b1[:, :], bcol("b1"), 0.5, None, ALU.mult))
            with dve.Fori(0, W_COLS // (W_CHUNK * W_SLOTS)) as g:
                for j in range(W_SLOTS):
                    dve.wait_ge(s["w_hi"], g * W_SLOTS + j + 1)
                    cols = bass.ds((g * W_SLOTS + j) * W_CHUNK, W_CHUNK)
                    dve.tensor_tensor(wp[:, 1, cols], carve(arena, 6144 + W_CHUNK * j, W_CHUNK), wp[:, 0, cols], ALU.subtract).then_inc(s["w_split"], 1)
            assert n0[0] == SETUP_STEPS
            with dve.Fori(0, TILES) as t:
                def need(name, n=1):
                    dve.wait_ge(s[name], at(t, name, n))

                def then(ins):
                    made[0] += 1
                    ins.then_inc(s["dve_order"], 1)
                    dve.wait_ge(s["dve_order"], at(t, "dve_order", made[0]))

                def alone():
                    made[0] += 1
                    dve.memset(waited[:, :], 0.0).then_inc(s["dve_order"], 1)

                def lo(dst, src, hi, done, ready, n=1):
                    need(ready, n)
                    dve.tensor_tensor(dst, src, hi, ALU.subtract).then_inc(s[done], 1)

                def normalise(n, src):
                    then(dve.bn_stats(bn[:, :], src))
                    alone()
                    then(dve.bn_aggr(mv[:, :], bn[:, :]))
                    dve.tensor_scalar(var_eps[:, :], mv[:, 1:2], EPS, None, ALU.add).then_inc(s["ln_var"], 1)
                    need("ln_rstd", n + 1)
                    return dve.tensor_scalar(xn[:, :], src, mv[:, 0:1], rstd[:, 0:1], ALU.subtract, ALU.mult)

                def normalised_t(k, n, src):
                    normalise(n, src).then_inc(s["xn"], 1)
                    lo(xt[:, 1].rearrange("p c n -> p (c n)"), ps[:, 0, 0:D], xt[:, 0].rearrange("p c n -> p (c n)"), "xt_lo", "xt_hi", k + 1)

                def add_block(ready, bank, row, src=None):
                    need(ready)
                    then(dve.tensor_tensor(x[:, :], ps[:, bank, 0:D], x[:, :], ALU.add))
                    then(dve.tensor_tensor(x[:, :], x[:, :], row_bias[:, row, :], ALU.add))

                def mask_queries(done):
                    src = qk[:, :, 0:2].rearrange("p l c (b q) -> p l (c b) q", b=NB)
                    dst = qbd.rearrange("p l c b h q -> p l (c b) h q")
                    for h in range(8):
                        ins = dve.tensor_scalar(dst[:, :, :, h, :], src, mask8[:, h:h + 1], None, ALU.mult)
                        if h < 7:
                            then(ins)
                    ins.then_inc(s[done], 1)

                dve.wait_ge(s["x_in"], t * 16 + 16)
                normalised_t(0, 0, x0[:, :])
                need("q0_ps")
                dve.tensor_tensor(qk_f[:, 0:2], ps[:, 1, 0:D].rearrange("p (c n) -> p c n", c=C),
                                  bcol("bq0").unsqueeze(2).to_broadcast([P, C, P]), ALU.add).then_inc(s["q0_f"], 1)
                lo(qk[:, 1, 0:2], qk_f[:, 0:2], qk[:, 0, 0:2], "q0_lo", "q0_hi")
                lo(qk[:, 1, 2:4].rearrange("p c n -> p (c n)"), ps[:, 2, 0:D], qk[:, 0, 2:4].rearrange("p c n -> p (c n)"), "qp_lo", "qp_hi")
                need("qbk_ps")
                then(dve.tensor_copy(small[:, 0:1], ps[:, 3, 0:1]))
                need("s1_ps")
                then(dve.tensor_reduce(small[:, 1:2], ps[:, 4, 0:KEYS], X, ALU.max))
                then(dve.tensor_tensor(small[:, 2:3], small[:, 1:2], small[:, 0:1], ALU.add))
                then(dve.tensor_tensor(small[:, 2:3], small[:, 0:1], small[:, 2:3], ALU.subtract))
                dve.tensor_scalar(small[:, 3:4], small[:, 2:3], D ** -0.5, None, ALU.mult).then_inc(s["s1_bias"], 1)
                need("p1")
                dve.tensor_scalar(last_cols[:, 0, 0:NB], quad, probs[:, KEYS - 1:KEYS], None, ALU.mult).then_inc(s["p1_last"], 1)
                then(dve.reciprocal(small[:, 5:6], small[:, 4:5]))
                lo(pt1[:, 1, :], ps[:, 5, 0:384], pt1[:, 0, :], "pt1_lo", "pt1_hi")
                lo(op[:, 1].rearrange("p c n -> p (c n)"), ps[:, 6, 0:D], op[:, 0].rearrange("p c n -> p (c n)"), "a1_lo", "a1_hi")
                need("y1_ps")
                then(dve.scalar_tensor_tensor(x[:, :], ps[:, 7, 0:D], small[:, 5:6], x0[:, :], ALU.mult, ALU.add))
                dve.tensor_tensor(x[:, :], x[:, :], row_bias[:, 0, :], ALU.add).then_inc(s["x_1"], 1)
                need("x_1")

                normalised_t(1, 1, x[:, :])
                need("qk2_ps")
                dve.tensor_tensor(qk_f[:, :, :], ps[:, 1].rearrange("p (c n) -> p c n", c=4),
                                  bcol("bqk0").unsqueeze(2).to_broadcast([P, 4, P]), ALU.add).then_inc(s["qk2_f"], 1)
                need("qk2_hi")
                then(dve.tensor_tensor(qk[:, 1], qk_f[:, :, :], qk[:, 0], ALU.subtract))
                mask_queries("qbd2")
                need("v2_hi")
                then(dve.tensor_tensor(v2[:, 1, :], ps[:, 3, 0:D], v2[:, 0, :], ALU.subtract))
                for b in range(NB):
                    ins = dve.tensor_scalar(vblk.rearrange("p l g b d -> p (l g) b d")[:, :, b, :],
                                            v2.rearrange("p l (g d) -> p (l g) d", g=GROUPS), quad[:, b:b + 1], None, ALU.mult)
                    if b < NB - 1:
                        then(ins)
                ins.then_inc(s["vblk"], 1)
                need("s2_ps")
                s2v = s2.rearrange("p (n k) -> p n k", k=SEQ)
                then(dve.tensor_tensor(s2v, ps[:, 4, :].rearrange("p (n k) -> p n k", k=SEQ),
                                       causal.unsqueeze(1).to_broadcast([P, 16, SEQ]), ALU.add))
                then(dve.tensor_reduce(small[:, 64:80], s2v, X, ALU.max))
                dve.tensor_tensor(s2v, s2v, small[:, 64:80].unsqueeze(2).to_broadcast([P, 16, SEQ]), ALU.subtract).then_inc(s["s2_shift"], 1)
                need("p2")
                then(dve.tensor_reduce(small[:, 64:80], probs[:, 0:512].rearrange("p (n k) -> p n k", k=SEQ), X, ALU.add))
                then(dve.reciprocal(small[:, 80:96], small[:, 64:80]))
                rm = th_rm[:, :, :]
                then(dve.tensor_tensor(rm, small[:, 80:96].unsqueeze(2).to_broadcast([P, 16, 4]),
                                       quad.unsqueeze(1).to_broadcast([P, 16, 4]), ALU.mult))
                lo(pt2[:, 1].rearrange("p g n -> p (g n)"), ps[:, 5, :], pt2[:, 0].rearrange("p g n -> p (g n)"), "pt2_lo", "pt2_hi")
                need("o2g_ps")
                for g in range(GROUPS):
                    dst = om_f.rearrange("p (b g h d) -> p g b h d", b=NB, g=GROUPS, h=4)[:, g]
                    src = ps[:, 6 + g // 2, (g % 2) * D:(g % 2 + 1) * D].rearrange("p (b h d) -> p b h d", b=NB, h=4)
                    dve.tensor_tensor(dst, src, rm[:, NB * g:NB * (g + 1), :].unsqueeze(3).to_broadcast([P, NB, 4, 16]),
                                      ALU.mult).then_inc(s["om_f"], 1)
                need("o2_hi", 2)
                for c in range(C):
                    dve.scalar_tensor_tensor(op[:, 1, c], ps[:, 1, c * P:(c + 1) * P], bcol("bv0")[:, c:c + 1], op[:, 0, c],
                                             ALU.add, ALU.subtract).then_inc(s["o2_lo"], 1)
                add_block("y2_ps", 2, 1)

                then(normalise(2, x[:, :]))
                then(dve.tensor_reduce(small[:, 8:9], xn[:, :], X, ALU.max, apply_absolute_value=True))
                then(dve.tensor_scalar(small[:, 8:9], small[:, 8:9], 1e-5, None, ALU.max))
                then(dve.reciprocal(small[:, 9:10], small[:, 8:9]))
                then(dve.tensor_scalar(small[:, 9:10], small[:, 9:10], 127.0, None, ALU.mult))
                then(dve.tensor_scalar(xq_f, xn[:, :], small[:, 9:10], ROUND, ALU.mult, ALU.add))
                then(dve.tensor_scalar(xq_f, xq_f, ROUND, 127.0, ALU.subtract, ALU.min))
                then(dve.tensor_scalar(small[:, 10:11], small[:, 8:9], 1.0 / 127.0, None, ALU.mult))
                then(dve.tensor_scalar(small[:, 11:12], small[:, 10:11], ffn_inv[:, 0:1], 0.5, ALU.mult, ALU.mult))
                then(dve.tensor_scalar(small[:, 12:13], small[:, 10:11], ffn_inv[:, 1:2], small[:, 11:12], ALU.mult, ALU.mult))
                dve.tensor_scalar(xq, xq_f, -128.0, None, ALU.max).then_inc(s["xq"], 1)
                need("th3")
                gate_v = ps[:, 1:3, :].rearrange("p a n -> p (a n)")
                then(dve.scalar_tensor_tensor(r3, th3, 1.0, gate_v, ALU.add, ALU.mult))
                need("up_ps")
                then(dve.tensor_tensor(r3, r3, ps[:, 3:5, :].rearrange("p a n -> p (a n)"), ALU.mult))
                then(dve.tensor_reduce(small[:, 13:14], r3, X, ALU.max, apply_absolute_value=True))
                then(dve.tensor_scalar(small[:, 13:14], small[:, 13:14], small[:, 12:13], 1e-5, ALU.mult, ALU.max))
                then(dve.reciprocal(small[:, 14:15], small[:, 13:14]))
                then(dve.tensor_scalar(small[:, 15:16], small[:, 14:15], small[:, 12:13], 127.0, ALU.mult, ALU.mult))
                then(dve.tensor_scalar(rq3, r3, small[:, 15:16], ROUND, ALU.mult, ALU.add))
                then(dve.tensor_scalar(rq3, rq3, ROUND, 127.0, ALU.subtract, ALU.min))
                dve.tensor_scalar(hq, rq3, -128.0, None, ALU.max).then_inc(s["hq"], 1)
                then(dve.tensor_scalar(small[:, 16:17], small[:, 13:14], ffn_inv[:, 2:3], 1.0 / 127.0, ALU.mult, ALU.mult))
                need("y3_ps")
                then(dve.scalar_tensor_tensor(x[:, :], ps[:, 6, 0:D], small[:, 16:17], x[:, :], ALU.mult, ALU.add))

                normalised_t(2, 3, x[:, :])
                need("q4_hi")
                dve.tensor_tensor(qk[:, 1, 0:2].rearrange("p c n -> p (c n)"), ps[:, 1, 0:D], qk[:, 0, 0:2].rearrange("p c n -> p (c n)"),
                                  ALU.subtract).then_inc(s["q4_lo"], 1)
                need("q4_lo")
                mask_queries("qbd4")
                lo(vl[0:NB, 1, :], ps[0:NB, 3, 0:D], vl[0:NB, 0, :], "vl_lo", "vl_hi")

                def k_lo(b):
                    lo(kp[:, 1], ps[:, 0:2, 0:KEYS], kp[:, 0], "k4_lo", "k4_hi", b + 1)

                def v_lo(b):
                    lo(vp[:, b % 2, 1].rearrange("p m n -> p (m n)"), ps[:, 2, :], vp[:, b % 2, 0].rearrange("p m n -> p (m n)"), "v4_lo", "v4_hi", b + 1)

                rm4 = [th_rm[:, 4 * i:4 * i + 4, :] for i in range(2)]

                def om_mask(b):
                    need("o4_ps", b + 1)
                    dve.tensor_tensor(om4_f.rearrange("p (n d) -> p n d", d=16), ps[:, 3, 0:256].rearrange("p (n d) -> p n d", d=16),
                                      rm4[b % 2].rearrange("p n h -> p (n h)").unsqueeze(2).to_broadcast([P, 16, 16]), ALU.mult).then_inc(s["om4_f"], 1)

                def sel_lo(b):
                    toks = slice(SEQ * b, SEQ * (b + 1))
                    lo(op[:, 1, :, toks], ps[:, 3, 256:320].rearrange("p (c n) -> p c n", c=C), op[:, 0, :, toks], "sel_lo", "sel_hi", b + 1)

                k_lo(0)
                v_lo(0)
                for b in range(NB):
                    need("s4_ps", b + 1)
                    then(dve.tensor_reduce(small[:, 20:24], ps[:, 4:8, 0:KEYS], X, ALU.max))
                    dve.tensor_scalar(small[:, 24:28], small[:, 20:24], -(16 ** -0.5), None, ALU.mult).then_inc(s["s4_bias"], 1)
                    if b >= 2:
                        sel_lo(b - 2)
                    if b + 1 < NB:
                        k_lo(b + 1)
                    need("p4", GROUPS * (b + 1))
                    pv = probs[:, 0:GROUPS * KEYS].rearrange("p (g m) -> p g m", g=GROUPS)
                    dve.tensor_tensor(last_cols[:, :, 0:NB], pv[:, :, KEYS - 1:KEYS].to_broadcast([P, GROUPS, NB]),
                                      eye4[:, b, :].unsqueeze(1).to_broadcast([P, GROUPS, NB]), ALU.mult).then_inc(s["p4_last"], 1)
                    then(dve.reciprocal(small[:, 32:36], small[:, 28:32]))
                    then(dve.tensor_tensor(rm4[b % 2], small[:, 32:36].unsqueeze(2).to_broadcast([P, 4, 4]),
                                           quad.unsqueeze(1).to_broadcast([P, 4, 4]), ALU.mult))
                    lo(pt4[:, b % 2, 1], ps[:, 4:8, 0:384], pt4[:, b % 2, 0], "pt4_lo", "pt4_hi", b + 1)
                    if b + 1 < NB:
                        v_lo(b + 1)
                    if b >= 1:
                        om_mask(b - 1)
                sel_lo(NB - 2)
                om_mask(NB - 1)
                sel_lo(NB - 1)
                add_block("y4_ps", 7, 2)

                normalised_t(3, 4, x[:, :])
                lo(v5[:, 1, :], ps[:, 2:4, :].rearrange("p a n -> p (a n)"), v5[:, 0, :], "v5_lo", "v5_hi")
                for g in range(GROUPS):
                    need("qk5_ps", g + 1)
                    if g >= 1:
                        need("qk5_lo", g)
                    dve.tensor_tensor(qk_f[:, :, :], ps[:, 6 + g % 2].rearrange("p (c n) -> p c n", c=4),
                                      bcol("bqk1")[:, 4 * g:4 * g + 4].unsqueeze(2).to_broadcast([P, 4, P]), ALU.add).then_inc(s["qk5_f"], 1)
                    need("qk5_lo", g + 1)
                    for h in range(4):
                        c = h // 2
                        ins = dve.tensor_scalar(qb5[:, :, c, :, h, :], qk[:, :, c].rearrange("p l (b q) -> p l b q", b=NB),
                                                half[:, h % 2:h % 2 + 1], None, ALU.mult)
                        if h < 3:
                            then(ins)
                    ins.then_inc(s["qb5"], 1)
                    need("s5_ps", g + 1)
                s5v = s5.rearrange("p (n k) -> p n k", k=SEQ)
                psv = ps[:, 4, :].rearrange("p (n k) -> p n k", k=SEQ)
                then(dve.tensor_reduce(small[:, 64:80], psv, X, ALU.max))
                dve.tensor_tensor(s5v, psv, small[:, 64:80].unsqueeze(2).to_broadcast([P, 16, SEQ]), ALU.subtract).then_inc(s["s5_shift"], 1)
                need("p5")
                then(dve.tensor_reduce(small[:, 64:80], s5v, X, ALU.add))
                then(dve.reciprocal(small[:, 80:96], small[:, 64:80]))
                dve.tensor_tensor(s5v, s5v, small[:, 80:96].unsqueeze(2).to_broadcast([P, 16, SEQ]), ALU.mult).then_inc(s["p5_norm"], 1)
                need("pt5_hi")
                then(dve.tensor_tensor(pt5[:, 1].rearrange("p g n -> p (g n)"), ps[:, 5, :], pt5[:, 0].rearrange("p g n -> p (g n)"), ALU.subtract))
                for b in range(NB):
                    ins = dve.tensor_scalar(ptb.rearrange("p l g b n -> p (l g) b n")[:, :, b, :],
                                            pt5.rearrange("p l g n -> p (l g) n"), quad[:, b:b + 1], None, ALU.mult)
                    if b < NB - 1:
                        then(ins)
                ins.then_inc(s["ptb"], 1)
                for i in range(4):
                    need("o5_ps", i + 1)
                    bank = (6, 7, 0, 1)[i]
                    for hh in range(2):
                        pr = slice(64 * hh, 64 * hh + 64)
                        src = ps[pr, bank, :].rearrange("p (j b h q) -> p j b h q", j=2, b=NB, h=2)[:, :, :, hh, :]
                        dst = o5_f[pr, 256 * i:256 * (i + 1)].rearrange("p (j b q) -> p j b q", j=2, b=NB)
                        a0 = B_AT["bv1"][0] + 2 * i
                        dve.tensor_tensor(dst, src, bias[pr, a0:a0 + 2].unsqueeze(2).unsqueeze(3).to_broadcast([64, 2, NB, SEQ]),
                                          ALU.add).then_inc(s["o5_f"], 1)
                add_block("y5_ps", 2, 3)

                normalised_t(4, 5, x[:, :])
                need("logit_ps")
                then(dve.tensor_reduce(small[:, 42:43], ps[:, 7, 0:EXPERTS], X, ALU.max))
                dve.tensor_scalar(small[:, 40:41], small[:, 42:43], -1.0, None, ALU.mult).then_inc(s["gate_max"], 1)
                need("gate_exp")
                then(dve.reciprocal(small[:, 43:44], small[:, 41:42]))
                then(dve.tensor_scalar(small[:, 48:56], small[:, 48:56], small[:, 43:44], None, ALU.mult))
                alone()
                then(dve.max(small[:, 56:64], small[:, 48:56]))
                alone()
                then(dve.max_index(idx[:, :], small[:, 56:64], small[:, 48:56]))
                then(dve.tensor_copy(small[:, 56:64], idx[:, :]))
                then(dve.tensor_scalar(small[:, 80:88], const("iota8"), small[:, 56:57], None, ALU.is_equal))
                then(dve.scalar_tensor_tensor(gate_p[:, 2, :], const("iota8"), small[:, 57:58], small[:, 80:88], ALU.is_equal, ALU.add))
                then(dve.tensor_copy(gate_p[:, 0, :], small[:, 48:56]))
                dve.tensor_tensor(gate_p[:, 1, :], small[:, 48:56], gate_p[:, 0, :], ALU.subtract).then_inc(s["gate_p"], 1)
                need("th_sh")
                then(dve.scalar_tensor_tensor(h_f, th6, 1.0, ps[:, 1, :], ALU.add, ALU.mult))
                dve.scalar_tensor_tensor(h_f, h_f, 0.5, ps[:, 2, :], ALU.mult, ALU.mult).then_inc(s["sh_f"], 1)
                need("z_ps")
                dve.tensor_copy(y, ps[:, 0, 0:D]).then_inc(s["y_0"], 1)

                def scale_in(e):
                    need("e13_ps", e + 1)
                    if e == 0:
                        need("wb", 2)
                    dve.tensor_tensor(u4[:, e % 2], ps[:, 1 + e % 2].rearrange("p (c n) -> p c n", c=4),
                                      wb[:, e].unsqueeze(1).to_broadcast([P, 4, P]), ALU.mult).then_inc(s["u4"], 1)

                scale_in(0)
                for e in range(EXPERTS):
                    need("th_e", 4 * (e + 1))
                    if e >= 1:
                        need("he_lo", e)
                    dve.scalar_tensor_tensor(h_f[:, 0:256], th6[:, 0:256], 1.0, v6, ALU.add, ALU.mult).then_inc(s["he_f"], 1)
                    if e + 1 < EXPERTS:
                        if e >= 1:
                            need("a3", e)
                        scale_in(e + 1)
                    if e >= 1:
                        need("prod", e)
                    need("e2_ps", e + 1)
                    for c in range(C):
                        k = e * C + c
                        dve.tensor_scalar(x2_f[:, c * P:(c + 1) * P], ps[:, 3 + e % 2, c * P:(c + 1) * P], 0.5, bcol("b2")[:, k:k + 1],
                                          ALU.mult, ALU.add).then_inc(s["x2"], 1)
                    for c in range(C):
                        k = e * C + c
                        ins = dve.scalar_tensor_tensor(a3_f[:, c * P:(c + 1) * P], u4[:, e % 2, 2 + c], bcol("b3")[:, k:k + 1], mb[:, e],
                                                       ALU.add, ALU.mult)
                        if c == 0:
                            then(ins)
                    ins.then_inc(s["a3"], 1)
                need("y6_ps")
                dve.wait_ge(s["stored"], t * 16 + 1)
                dve.tensor_tensor(x_out[:, :], ps[:, 0, 0:D], x[:, :], ALU.add).then_inc(s["x_final"], 1)
            assert made[0] == PER_TRIP["dve_order"], made[0]


def _stacked(m, k):
    import numpy as np

    return np.ascontiguousarray(m.reshape(k, P, -1).transpose(1, 0, 2).reshape(P, -1))


def _columns(v):
    return v.reshape(-1, P).T


def _constants():
    import numpy as np

    p = np.arange(P)
    parts = {
        "ident": np.eye(P), "sel": p[:, None] % SEQ == np.arange(SEQ)[None], "causal": np.where(np.arange(SEQ)[None] <= p[:, None] % SEQ, 0.0, FAR),
        "mask8": p[:, None] // 16 == np.arange(8)[None], "quad": p[:, None] // SEQ == np.arange(4)[None],
        "half": p[:, None] // 64 == np.arange(2)[None], "eye4": np.tile(np.eye(4).reshape(1, 16), (P, 1)),
        "iota8": np.tile(np.arange(8)[None], (P, 1)),
    }
    return np.concatenate([parts[n] for n, _ in _CONSTS], axis=1).astype(np.float32)


def kernel(**inputs):
    import numpy as np
    from concourse import bacc
    from concourse.bass_utils import run_bass_kernel_spmd

    a = {k: np.asarray(v) for k, v in inputs.items()}
    c = a["ctx_1024"]
    qkv_b, h = a["L0_attn_qkv_b"], a["L1_attn_W_Q"].shape[0]
    flat = {n: a["L1_attn_W_" + n].reshape(WIDE, D).T for n in "QKV"}
    experts = {n: np.concatenate([_stacked(a["L1_ffn_" + n][e].T, C) for e in range(EXPERTS)], axis=1) for n in ("w1", "w2", "w3")}
    packed = {
        "q0": _stacked(a["L0_xattn_Wq"], C), "k0t": _stacked(a["L0_xattn_Wk"].T, C), "v0": _stacked(a["L0_xattn_Wv"], C),
        "qkv0": _stacked(a["L0_attn_qkv_w"].T, C), "o0": _stacked(a["L0_attn_o_w"].T, C),
        "xq": _stacked(a["L1_xattn_w_q"].T, C), "xkv": _stacked(a["L1_xattn_w_kv"].T, C), "xo": _stacked(a["L1_xattn_w_out"].T, C),
        "aq": _stacked(flat["Q"], C), "ak": _stacked(flat["K"], C), "av": _stacked(flat["V"], C),
        "ao": _stacked(a["L1_attn_W_O"].transpose(0, 2, 1).reshape(WIDE, D), WIDE // P),
        "gate": _stacked(a["L1_ffn_gate_w"].T, C), **experts,
        "sw1": _stacked(a["L1_ffn_sw1"].T, C), "sw2": _stacked(a["L1_ffn_sw2"].T, C), "sw3": _stacked(a["L1_ffn_sw3"].T, SHARED // P),
    }
    bq, bk = _columns(a["L1_attn_b_Q"].reshape(-1)), _columns(a["L1_attn_b_K"].reshape(-1))
    columns = {
        "bq0": _columns(a["L0_xattn_bq"]), "bk0": _columns(a["L0_xattn_bk"]),
        "bqk0": _columns(qkv_b[0:2 * D]), "bv0": _columns(qkv_b[2 * D:3 * D]),
        "bqk1": np.concatenate([m[:, 2 * g:2 * g + 2] for g in range(GROUPS) for m in (bq, bk)], axis=1),
        "bv1": _columns(a["L1_attn_b_V"].reshape(-1)),
        **{n: _columns(a["L1_ffn_" + n].reshape(-1)) for n in ("b1", "b2", "b3")},
    }
    rows = np.stack([a["L0_xattn_bv"], a["L0_attn_o_b"], a["L1_xattn_b_out"], a["L1_attn_b_O"]])
    arrays = {
        "x_tok": a["x"].reshape(TILES, P, D),
        "ctx_t": c.reshape(TILES, NB, KEYS, C, P).transpose(0, 1, 4, 3, 2).reshape(TILES, NB, P, C * KEYS),
        "ctx_n": c[:, 0:2 * P].reshape(TILES, NB, 2, P, D).transpose(0, 1, 3, 2, 4).reshape(TILES, NB, P, 2 * D),
        "ctx_l": c[:, KEYS - 1].reshape(TILES, NB, D),
        "weights": np.concatenate([packed[n] for n, _ in _SIZES], axis=1),
        "ffn": np.stack([_stacked(a["L0_ffn_w_gate"].T, C), _stacked(a["L0_ffn_w_up"].T, C), _stacked(a["L0_ffn_w_down"].T, 8)]),
        "consts": _constants(),
        "biases": np.concatenate([columns[n] for n, _ in _BIASES], axis=1),
        "rows": np.tile(rows.reshape(1, -1), (P, 1)),
    }
    arrays = {"in_" + k: np.ascontiguousarray(v) for k, v in arrays.items()}
    nc = bacc.Bacc("TRN2", target_bir_lowering=False, num_devices=1)
    args = [nc.dram_tensor(k, v.shape, mybir.dt.from_np(v.dtype), kind="ExternalInput").ap() for k, v in arrays.items()]
    out = nc.dram_tensor("y_tok", (TILES, P, D), F32, kind="ExternalOutput").ap()
    build(nc, *args, out)
    r = run_bass_kernel_spmd(nc, [arrays], core_ids=[0])
    return r.results[0]["y_tok"].reshape(SEQS, SEQ, D)
```

```python
from contextlib import ExitStack

import concourse.bass as bass
from concourse import mybir

F32 = mybir.dt.float32
F16 = mybir.dt.float16
BF16 = mybir.dt.bfloat16
U32 = mybir.dt.uint32
ALU = mybir.AluOpType
ACT = mybir.ActivationFunctionType
X = mybir.AxisListType.X

P = 128
D = 256
C = D // P
SEQ = 32
SEQS = 128
KEYS = 257
NB = P // SEQ
TILES = SEQS // NB
LANES = 2
TRIPS = TILES // LANES
HEADS = 16
GROUPS = HEADS // 4
WIDE = 1024
EXPERTS = 8
SHARED = 512
EPS = 1e-5
ROUND = 1.5 * 2.0**23
FAR = -1.0e30

_SIZES = [
    [("q0", C * D), ("k0t", C * D), ("v0", C * D), ("qkv0", C * 3 * D), ("o0", C * D),
     ("xq", C * D), ("xkv", C * 2 * D), ("xo", C * D)],
    [("aq", C * WIDE), ("ak", C * WIDE), ("av", C * WIDE), ("ao", WIDE // P * D),
     ("gate", C * EXPERTS), ("w1", EXPERTS * C * D), ("w2", EXPERTS * C * D), ("w3", EXPERTS * C * D),
     ("sw1", C * SHARED), ("sw2", C * SHARED), ("sw3", SHARED // P * D)],
]
W_AT, W_COLS = [{}, {}], [0, 0]
for _half in range(2):
    for _name, _n in _SIZES[_half]:
        W_AT[_half][_name] = W_COLS[_half]
        W_COLS[_half] += _n
W_SLOTS = 4
W_CHUNK = [1408, 1473]
W_GROUPS = [W_COLS[h] // (W_CHUNK[h] * W_SLOTS) for h in range(2)]
assert all(W_GROUPS[h] * W_CHUNK[h] * W_SLOTS == W_COLS[h] for h in range(2))

FRONT = 8198
LANE_1 = FRONT + 2 * C * KEYS + 4 * D + D + 2 * NB * D + 2 * C * NB * KEYS // 2 + D
LANE_2 = 6144 + 1024
MEM = max(LANES * LANE_1 + W_COLS[0] + 3072, W_COLS[1] + LANES * LANE_2)

_CONSTS = [("ident", P), ("sel", SEQ), ("causal", SEQ), ("mask8", 8), ("quad", 4), ("half", 2), ("eye4", 16), ("iota8", 8)]
C_AT, C_COLS = {}, 0
for _name, _n in _CONSTS:
    C_AT[_name] = (C_COLS, C_COLS + _n)
    C_COLS += _n
_BIASES = [("bq0", 2), ("bk0", 2), ("bqk0", 4), ("bv0", 2), ("bqk1", 16), ("bv1", 8), ("b1", 16), ("b2", 16), ("b3", 16)]
B_AT, B_COLS = {}, 0
for _name, _n in _BIASES:
    B_AT[_name] = (B_COLS, B_COLS + _n)
    B_COLS += _n

SETUP_STEPS = 17
POOL_SETUP = 5 + 3 * LANES

FIRST = {
    "ln_var": 4, "ln_rstd": 4, "xn": 3, "xt_ps": 3, "xt_hi": 3, "xt_lo": 3,
    "tp_hi": 4, "tp_lo": 4, "np_hi": 4, "np_lo": 4, "cl_hi": 1, "cl_lo": 1,
    "q0_ps": 1, "q0_f": 1, "q0_hi": 1, "q0_lo": 1, "qp_ps": 1, "qp_hi": 1, "qp_lo": 1, "qbk_ps": 1, "s1_ps": 1,
    "s1_bias": 1, "p1": 1, "p1_last": 1, "pt1_ps": 1, "pt1_hi": 1, "pt1_lo": 1, "a1_ps": 1, "a1_hi": 1, "a1_lo": 1,
    "y1_ps": 1, "x_1": 1, "qk_ps": 1, "qk_f": 1, "qk_hi": 1, "v_ps": 1, "v_hi": 1, "qbd2": 1, "self_v": 1,
    "self_s": 1, "self_shift": 1, "self_p": 1, "self_pt": 1, "self_pt_hi": 1, "pt2_lo": 1, "o2g_ps": 1, "o_f": 4, "o_hi": 1,
    "o_lo": 1, "o2_ps": 1, "o2_hi": 2, "o2_lo": 2, "self_y": 1, "xq": 1, "xq_ps": 1, "xqt": 1, "gate_ps": 1,
    "up_ps": 1, "th3": 1, "hq": 1, "hq_ps": 1, "hqt": 1, "y3_ps": 1, "q4_ps": 1, "q4_hi": 1, "q4_lo": 1, "qbd4": 1,
    "vl_ps": 1, "vl_hi": 1, "vl_lo": 1, "k4_ps": 4, "k4_hi": 4, "k4_lo": 4, "v4_ps": 4, "v4_hi": 4, "v4_lo": 4,
    "s4_ps": 4, "s4_bias": 4, "p4": 16, "p4_last": 4, "pt4_ps": 4, "pt4_hi": 4, "pt4_lo": 4, "o4_ps": 4, "om4_f": 4,
    "om4_hi": 4, "om4_lo": 4, "sel_ps": 4, "sel_hi": 4, "sel_lo": 4, "y4_ps": 1, "x_4": 1, "dve_order": 77,
}
SECOND = {
    "ln_var": 2, "ln_rstd": 2, "xn": 2, "xt_ps": 2, "xt_hi": 2, "xt_lo": 2, "v_ps": 1, "v_hi": 1, "self_v": 1,
    "qk_ps": 4, "qk_f": 4, "qk_hi": 4, "qk5_lo": 4, "qb5": 4, "self_s": 4, "self_shift": 1, "self_p": 1, "p5_norm": 1,
    "self_pt": 1, "self_pt_hi": 1, "ptb": 1, "o5_ps": 4, "o_f": 8, "o_hi": 1, "o_lo": 1, "self_y": 1, "x_5": 1, "gate_ps": 1,
    "s1_bias": 1, "p1": 1, "gate_p": 1, "sh_ps": 1, "th_sh": 1, "sh_f": 1, "sh_hi": 1, "sh_lo": 1, "wb_ps": 1,
    "mb_ps": 1, "wb": 1, "mb": 2, "y4_ps": 1, "y_0": 1, "e13_ps": 8, "u4": 8, "th_e": 32, "he_f": 8, "he_hi": 8, "he_lo": 8,
    "e2_ps": 8, "x2": 16, "a3": 8, "prod": 8, "y_add": 8, "y3_ps": 1, "x_final": 1, "dve_order": 46,
}
EARLY = ("tp_hi", "tp_lo", "np_hi", "np_lo", "cl_hi", "cl_lo")
AHEAD = ("x_5",)
LANE_SIGNALS = ("x_in", "stored", "l_in", "n_in0_", "n_in1_", "t_in0_", "t_in1_")
SETUP_SIGNALS = ["const_in", "ffn_in", "pool_set", "ffn_abs", "ffn_sum", "dve_setup", "w_hi", "w_split", "first_over"] + [
    f"w_in{j}" for j in range(W_SLOTS)] + [f"{n}{lane}" for n in LANE_SIGNALS for lane in range(LANES)]


def counter(table, done, lane):
    def at(trip, name, n):
        ahead = (2 if name in AHEAD else 0) + (LANES * table[name] if name in EARLY else 0)
        return trip * (LANES * table[name]) + (LANES * n - 1 + lane + ahead + LANES * TRIPS * done.get(name, 0))
    return at


def in_turns(first, second):
    for _ in first:
        next(second)
    for _ in second:
        pass


def carve(memory, at, words, dt=F32):
    a = memory[:, at:at + words]
    return a if dt == F32 else a.bitcast(dt)


def build(nc, x_in, ctx_t, ctx_n, ctx_l, weights, ffn, consts, biases, rows, mid, out):
    ctx = ExitStack()
    with ctx:
        def sb(name, shape, dt):
            return ctx.enter_context(nc.sbuf_tensor(name, shape, dt))

        def sem(name):
            return ctx.enter_context(nc.semaphore(name))

        cst = sb("cst", [P, C_COLS], F32)
        bias = sb("bias", [P, B_COLS], F32)
        row_bias = sb("row_bias", [P, 4, D], F32)
        ident16 = sb("ident16", [P, P], F16)
        identb = sb("identb", [P, P], BF16)
        sel16 = sb("sel16", [P, SEQ], F16)
        ones = sb("ones", [P, P], F32)
        bk_pair = sb("bk_pair", [P, 2, C], F16)
        half_b1 = sb("half_b1", [P, EXPERTS * C], F32)
        ffn_inv = sb("ffn_inv", [P, 3], F32)
        stat = sb("stat", [P, 16], F32)
        neg_half = sb("neg_half", [P, 1], F32)
        mem = sb("mem", [P, MEM], F32)

        def pairs(at, cols):
            return carve(mem, at, cols, F16).rearrange("p (l n) -> p l n", l=2)

        wp = [pairs(LANES * LANE_1, W_COLS[0]), pairs(0, W_COLS[1])]
        ffn_w = carve(mem, LANES * LANE_1 + W_COLS[0], 3072, BF16).rearrange("p (i n) -> p i n", i=3)
        ffn_stage = [carve(mem, 2048 * i, 2048) for i in range(3)]
        w_stage = [[carve(mem, (LANE_1, W_COLS[1])[h] + W_CHUNK[h] * j, W_CHUNK[h]) for j in range(W_SLOTS)] for h in range(2)]

        def const(name):
            a, b = C_AT[name]
            return cst[:, a:b]

        def bcol(name):
            a, b = B_AT[name]
            return bias[:, a:b]

        def w(name, part, k, n, first=0):
            h = 0 if name in W_AT[0] else 1
            a = W_AT[h][name] + first
            return wp[h][:, part, a:a + k * n].rearrange("p (k n) -> p k n", k=k)

        ident = const("ident")
        causal, mask8, quad, half = const("causal"), const("mask8"), const("quad"), const("half")
        eye4 = const("eye4").rearrange("p (b j) -> p b j", b=NB)
        psum = ctx.enter_context(nc.psum_tensor("ps", [P, 8, 512], F32))

        def lane_buffers(k):
            def own(name, shape, dt):
                return sb(f"{name}_{k}", shape, dt)

            return dict(
                x0=own("x0", [P, D], F32), x=own("x", [P, D], F32), x_out=own("x_out", [P, D], F32), xn=own("xn", [P, D], F32),
                xt=own("xt", [P, 2, C, P], F16), bn=own("bn", [P, 6], F32), mv=own("mv", [P, 2], F32), var_eps=own("var_eps", [P, 1], F32),
                rstd=own("rstd", [P, 1], F32), qk_f=own("qk_f", [P, 4, P], F32), qk=own("qk", [P, 2, 4, P], F16),
                op=own("op", [P, 2, C, P], F16), last_cols=own("last_cols", [P, GROUPS, P], F32), vl=own("vl", [P, 2, D], F16),
                small=own("small", [P, 96], F32), idx=own("idx", [P, 8], U32), waited=own("waited", [P, 1], F32),
                th_rm=own("th_rm", [P, 16, 4], F32), gate_p=own("gate_p", [P, 3, EXPERTS], F16))

        own = [lane_buffers(k) for k in range(LANES)]

        s = {}
        for n in SETUP_SIGNALS + list(dict.fromkeys([*FIRST, *SECOND])):
            s[n] = sem(n)

        def product(pe, dst, pairs, start=True, stop=True):
            n = len(pairs)
            last = None
            for i, ((lh, ll), (rh, rl)) in enumerate(pairs):
                for j, (a, b) in enumerate([(lh, rh), (lh, rl), (ll, rh)]):
                    last = pe.matmul(dst, a, b, start=start and i == 0 and j == 0, stop=stop and i == n - 1 and j == 2)
            return last

        def feature_major(pe, dst, name, n, act_pair, chunks, first=0, k=C):
            for i, oc in enumerate(chunks):
                last = product(pe, dst[:, i * P:(i + 1) * P], [
                    ((w(name, 0, k, n, first)[:, kc, oc * P:(oc + 1) * P], w(name, 1, k, n, first)[:, kc, oc * P:(oc + 1) * P]),
                     (act_pair[:, 0, kc], act_pair[:, 1, kc])) for kc in range(k)])
            return last

        def token_major(pe, dst, name, n, act_pair, lo, hi, k=C):
            return product(pe, dst, [
                ((act_pair[:, 0, kc], act_pair[:, 1, kc]), (w(name, 0, k, n)[:, kc, lo:hi], w(name, 1, k, n)[:, kc, lo:hi]))
                for kc in range(k)])

        def first_half(lane):
            me = own[lane]
            x0, x, xn, xt, bn, mv, var_eps, rstd = me["x0"], me["x"], me["xn"], me["xt"], me["bn"], me["mv"], me["var_eps"], me["rstd"]
            qk_f, qk, op, last_cols, vl, small, waited, th_rm = me["qk_f"], me["qk"], me["op"], me["last_cols"], me["vl"], me["small"], me["waited"], me["th_rm"]
            at = counter(FIRST, {}, lane)
            ps = psum[:, 4 * lane:4 * lane + 4, :]
            arena = mem[:, LANE_1 * lane:LANE_1 * (lane + 1)]

            stage_t = carve(arena, FRONT, 2 * C * KEYS).rearrange("p (s n) -> p s n", s=2)
            stage_n = carve(arena, FRONT + 2 * C * KEYS, 4 * D).rearrange("p (s n) -> p s n", s=2)
            after = FRONT + 2 * C * KEYS + 4 * D
            stage_l = arena[0:NB, after:after + D]
            ctx_np = carve(arena, after + D, 2 * NB * D, F16).rearrange("p (l b m d) -> p l b m d", l=2, b=NB, m=2)
            after += D + 2 * NB * D
            ctx_tp = carve(arena, after, C * NB * KEYS, F16).rearrange("p (l c b m) -> p l c b m", l=2, c=C, b=NB)
            ctx_lp = carve(arena, after + C * NB * KEYS, D, F16).rearrange("p (l n) -> p l n", l=2)
            qbd = carve(arena, 0, 2048, F16).rearrange("p (l c b h q) -> p l c b h q", l=2, c=C, b=NB, h=8)
            probs = carve(arena, 2048, 1028)
            pt1 = carve(arena, 3076, 384, F16).rearrange("p (l n) -> p l n", l=2)
            s2 = carve(arena, 3584, 512)
            pt2 = carve(arena, 4096, 512, F16).rearrange("p (l g n) -> p l g n", l=2, g=GROUPS)
            vblk = carve(arena, 4608, 1024, F16).rearrange("p (l g b d) -> p l g b d", l=2, g=GROUPS, b=NB)
            v2 = carve(arena, 5632, 256, F16).rearrange("p (l n) -> p l n", l=2)
            om_f = carve(arena, 6144, 1024)
            om = carve(arena, 7168, 1024, F16).rearrange("p (l b n) -> p l b n", l=2, b=NB)
            th3 = carve(arena, 2048, 1024)
            r3 = carve(arena, 3072, 1024)
            rq3 = carve(arena, 4096, 1024)
            hq = carve(arena, 5120, 512, BF16)
            hqt = carve(arena, 5632, 512, BF16).rearrange("p (k n) -> p k n", k=8)
            xq_f = carve(arena, 6144, 256)
            xq = carve(arena, 6400, 128, BF16)
            xqt = carve(arena, 6528, 128, BF16).rearrange("p (c n) -> p c n", c=C)
            kp = carve(arena, 3076, 514, F16).rearrange("p (l c m) -> p l c m", l=2, c=C)
            vp = carve(arena, 3590, 1024, F16).rearrange("p (s l m n) -> p s l m n", s=2, l=2, m=2)
            pt4 = carve(arena, 4614, 3072, F16).rearrange("p (s l g n) -> p s l g n", s=2, l=2, g=GROUPS)
            om4_f = carve(arena, 7686, 256)
            om4 = carve(arena, 7942, 256, F16).rearrange("p (l g d) -> p l g d", l=2, g=GROUPS)

            def tp_hi(act, trip, b):
                act.wait_ge(s[f"t_in{b % 2}_{lane}"], trip * 32 + 32 + 16 * (b // 2) + 16)
                if not isinstance(trip, int):
                    act.wait_ge(s["v4_ps"], at(trip, "v4_ps", b + 1))
                act.activation(ctx_tp[:, 0, :, b, :], stage_t[:, b % 2, :].rearrange("p (c m) -> p c m", c=C), ACT.Copy).then_inc(s["tp_hi"], 1)
                yield

            def tp_lo(pool, trip, b):
                pool.wait_ge(s["tp_hi"], at(trip, "tp_hi", b + 1))
                pool.tensor_tensor(ctx_tp[:, 1, :, b, :], stage_t[:, b % 2, :].rearrange("p (c m) -> p c m", c=C), ctx_tp[:, 0, :, b, :],
                                   ALU.subtract).then_inc(s["tp_lo"], 1)
                yield

            def np_hi(act, trip, b):
                act.wait_ge(s[f"n_in{b % 2}_{lane}"], trip * 32 + 32 + 16 * (b // 2) + 16)
                if not isinstance(trip, int) and b == 0:
                    act.wait_ge(s["a1_ps"], at(trip, "a1_ps", 1))
                act.activation(ctx_np[:, 0, b], stage_n[:, b % 2, :].rearrange("p (m d) -> p m d", m=2), ACT.Copy).then_inc(s["np_hi"], 1)
                yield

            def np_lo(pool, trip, b):
                pool.wait_ge(s["np_hi"], at(trip, "np_hi", b + 1))
                pool.tensor_tensor(ctx_np[:, 1, b], stage_n[:, b % 2, :].rearrange("p (m d) -> p m d", m=2), ctx_np[:, 0, b],
                                   ALU.subtract).then_inc(s["np_lo"], 1)
                yield

            def last_hi(act, trip):
                act.wait_ge(s[f"l_in{lane}"], trip * 16 + 32)
                act.activation(ctx_lp[0:NB, 0, :], stage_l, ACT.Copy).then_inc(s["cl_hi"], 1)
                yield

            def last_lo(pool, trip):
                pool.wait_ge(s["cl_hi"], at(trip, "cl_hi", 1))
                pool.tensor_tensor(ctx_lp[0:NB, 1, :], stage_l, ctx_lp[0:NB, 0, :], ALU.subtract).then_inc(s["cl_lo"], 1)
                yield

            def scalar_before(act):
                for b in range(NB):
                    yield from np_hi(act, -1, b)
                    yield from tp_hi(act, -1, b)
                yield from last_hi(act, -1)

            def gpsimd_before(pool):
                for b in range(NB):
                    yield from np_lo(pool, -1, b)
                    yield from tp_lo(pool, -1, b)
                yield from last_lo(pool, -1)

            def load_n(sp, trip, b):
                if b >= 2 or not isinstance(trip, int):
                    sp.wait_ge(s["np_lo"], at(trip, "np_lo", b - 1))
                source = (TRIPS - 1 if isinstance(trip, int) else trip) * LANES + lane
                sp.dma_start(stage_n[:, b % 2, :], ctx_n[bass.ds(source, 1), b].rearrange("t p n -> (t p) n")).then_inc(s[f"n_in{b % 2}_{lane}"], 16)

            def load_t(sp, trip, b):
                if b >= 2 or not isinstance(trip, int):
                    sp.wait_ge(s["tp_lo"], at(trip, "tp_lo", b - 1))
                source = (TRIPS - 1 if isinstance(trip, int) else trip) * LANES + lane
                sp.dma_start(stage_t[:, b % 2, :], ctx_t[bass.ds(source, 1), b].rearrange("t p n -> (t p) n")).then_inc(s[f"t_in{b % 2}_{lane}"], 16)

            def load_l(sp, trip):
                if not isinstance(trip, int):
                    sp.wait_ge(s["cl_lo"], at(trip, "cl_lo", 0))
                source = (TRIPS - 1 if isinstance(trip, int) else trip) * LANES + lane
                sp.dma_start(stage_l, ctx_l[bass.ds(source, 1)].rearrange("t p d -> (t p) d")).then_inc(s[f"l_in{lane}"], 16)

            def load_x(sp, trip):
                if not isinstance(trip, int):
                    sp.wait_ge(s["x_1"], at(trip, "x_1", 1))
                source = (TRIPS - 1 if isinstance(trip, int) else trip) * LANES + lane
                sp.dma_start(x0[:, :], x_in[bass.ds(source, 1)].rearrange("t p d -> (t p) d")).then_inc(s[f"x_in{lane}"], 16)

            def store_x(sp, trip):
                sp.wait_ge(s["x_4"], at(trip, "x_4", 1))
                sp.dma_start(mid[bass.ds(trip * LANES + lane, 1)].rearrange("t p d -> (t p) d"), x[:, :]).then_inc(s[f"stored{lane}"], 16)

            def tensor(pe, t):
                def need(name, n=1):
                    pe.wait_ge(s[name], at(t, name, n))

                def transpose_x(n):
                    need("xn", n + 1)
                    for c in range(C):
                        last = pe.transpose(ps[:, 0, c * P:(c + 1) * P], xn[:, c * P:(c + 1) * P], ident)
                    last.then_inc(s["xt_ps"], 1)
                    yield
                    need("xt_lo", n + 1)

                yield from transpose_x(0)
                feature_major(pe, ps[:, 1], "q0", D, xt, range(C)).then_inc(s["q0_ps"], 1)
                yield
                need("q0_lo")
                feature_major(pe, ps[:, 2], "k0t", D, qk[:, :, 0:2], range(C)).then_inc(s["qp_ps"], 1)
                yield
                product(pe, ps[:, 3, 0:1], [((qk[:, 0, c], qk[:, 1, c]), (bk_pair[:, 0, c:c + 1], bk_pair[:, 1, c:c + 1]))
                                        for c in range(C)]).then_inc(s["qbk_ps"], 1)
                yield
                need("qp_lo")
                need("tp_lo", 0)
                for c in range(C):
                    for a, r in ((0, 0), (0, 1), (1, 0)):
                        for b in range(NB):
                            last = pe.matmul(ps[SEQ * b:SEQ * (b + 1), 0, 0:KEYS], qk[:, a, 2 + c, SEQ * b:SEQ * (b + 1)], ctx_tp[:, r, c, b, :],
                                             start=(c == 0 and a == 0 and r == 0), stop=(c == 1 and a == 1))
                last.then_inc(s["s1_ps"], 1)
                yield
                need("p1_last")
                for m in range(3):
                    src = probs[:, m * P:(m + 1) * P] if m < 2 else last_cols[:, 0, :]
                    last = pe.transpose(ps[:, 1, m * P:(m + 1) * P], src, ident)
                last.then_inc(s["pt1_ps"], 1)
                yield
                need("pt1_lo")
                need("cl_lo", 0)
                need("np_lo", 0)
                for c in range(C):
                    cols = slice(c * P, (c + 1) * P)
                    product(pe, ps[:, 2, cols], [((ctx_lp[:, 0, cols], ctx_lp[:, 1, cols]), (pt1[:, 0, 256:384], pt1[:, 1, 256:384]))], stop=False)
                    for b in range(NB):
                        for m in range(2):
                            toks = slice(m * P + SEQ * b, m * P + SEQ * (b + 1))
                            last = product(pe, ps[:, 2, c * P + SEQ * b:c * P + SEQ * (b + 1)],
                                           [((ctx_np[:, 0, b, m, cols], ctx_np[:, 1, b, m, cols]), (pt1[:, 0, toks], pt1[:, 1, toks]))],
                                           start=False, stop=(b == NB - 1 and m == 1))
                last.then_inc(s["a1_ps"], 1)
                yield
                need("a1_lo")
                token_major(pe, ps[:, 3, 0:D], "v0", D, op, 0, D).then_inc(s["y1_ps"], 1)
                yield

                yield from transpose_x(1)
                feature_major(pe, ps[:, 1], "qkv0", 3 * D, xt, range(4)).then_inc(s["qk_ps"], 1)
                yield
                token_major(pe, ps[:, 2, 0:D], "qkv0", 3 * D, xt, 2 * D, 3 * D).then_inc(s["v_ps"], 1)
                yield
                need("qbd2")
                for g in range(GROUPS):
                    c, h = g // 2, 4 * (g % 2)
                    for b in range(NB):
                        q = [qbd[:, a, c, b, h:h + 4, :].rearrange("p h q -> p (h q)") for a in range(2)]
                        k = [qk[:, a, 2 + c, SEQ * b:SEQ * (b + 1)] for a in range(2)]
                        last = product(pe, ps[:, 3, g * P + SEQ * b:g * P + SEQ * (b + 1)], [((q[0], q[1]), (k[0], k[1]))])
                last.then_inc(s["self_s"], 1)
                yield
                need("self_p")
                for g in range(GROUPS):
                    last = pe.transpose(ps[:, 0, g * P:(g + 1) * P], probs[:, g * P:(g + 1) * P], ident)
                last.then_inc(s["self_pt"], 1)
                yield
                need("self_v")
                need("pt2_lo")
                for g in range(GROUPS):
                    v = [vblk[:, a, g].rearrange("p b d -> p (b d)") for a in range(2)]
                    last = product(pe, ps[:, 1 + g // 2, (g % 2) * D:(g % 2 + 1) * D], [((pt2[:, 0, g], pt2[:, 1, g]), (v[0], v[1]))])
                last.then_inc(s["o2g_ps"], 1)
                yield
                need("o_lo")
                for c in range(C):
                    for b in range(NB):
                        for a in range(2):
                            last = pe.matmul(ps[:, 3, c * P + SEQ * b:c * P + SEQ * (b + 1)], om[:, a, b, c * P:(c + 1) * P], sel16[:, :],
                                             start=(a == 0), stop=(a == 1))
                last.then_inc(s["o2_ps"], 1)
                yield
                need("o2_lo", 2)
                token_major(pe, ps[:, 0, 0:D], "o0", D, op, 0, D).then_inc(s["self_y"], 1)
                yield

                need("xq")
                for c in range(C):
                    last = pe.transpose(ps[:, 3, c * 64:(c + 1) * 64].bitcast(BF16), xq[:, c * P:(c + 1) * P], identb[:, :])
                last.then_inc(s["xq_ps"], 1)
                yield
                need("xqt")
                for i, name in ((0, "gate_ps"), (1, "up_ps")):
                    wt = ffn_w[:, i, :].rearrange("p (k n) -> p k n", k=C)
                    for j in range(2):
                        for kc in range(C):
                            last = pe.matmul(ps[:, 2 * i + j, :], xqt[:, kc], wt[:, kc, 512 * j:512 * (j + 1)], start=(kc == 0), stop=(kc == 1))
                    last.then_inc(s[name], 1)
                    yield
                need("hq")
                for k in range(8):
                    last = pe.transpose(ps[:, 0, k * 64:(k + 1) * 64].bitcast(BF16), hq[:, k * P:(k + 1) * P], identb[:, :])
                last.then_inc(s["hq_ps"], 1)
                yield
                need("hqt")
                wt = ffn_w[:, 2, :].rearrange("p (k n) -> p k n", k=8)
                for k in range(8):
                    last = pe.matmul(ps[:, 1, 0:D], hqt[:, k], wt[:, k, :], start=(k == 0), stop=(k == 7))
                last.then_inc(s["y3_ps"], 1)
                yield

                yield from transpose_x(2)
                feature_major(pe, ps[:, 2], "xq", D, xt, range(C)).then_inc(s["q4_ps"], 1)
                yield
                product(pe, ps[0:NB, 3, 0:D], [((ctx_tp[:, 0, c, :, KEYS - 1], ctx_tp[:, 1, c, :, KEYS - 1]),
                                            (w("xkv", 0, C, 2 * D)[:, c, D:2 * D], w("xkv", 1, C, 2 * D)[:, c, D:2 * D])) for c in range(C)]
                        ).then_inc(s["vl_ps"], 1)
                yield
                need("q4_lo")
                need("vl_lo")

                def keys_values(b):
                    if b >= 1:
                        need("pt4_lo", b)
                    for oc in range(C):
                        last = product(pe, ps[:, oc, 0:KEYS], [
                            ((w("xkv", 0, C, 2 * D)[:, kc, oc * P:(oc + 1) * P], w("xkv", 1, C, 2 * D)[:, kc, oc * P:(oc + 1) * P]),
                             (ctx_tp[:, 0, kc, b, :], ctx_tp[:, 1, kc, b, :])) for kc in range(C)])
                    last.then_inc(s["k4_ps"], 1)
                    yield
                    for m in range(2):
                        last = product(pe, ps[:, 2, m * D:(m + 1) * D], [
                            ((ctx_tp[:, 0, kc, b, m * P:(m + 1) * P], ctx_tp[:, 1, kc, b, m * P:(m + 1) * P]),
                             (w("xkv", 0, C, 2 * D)[:, kc, D:2 * D], w("xkv", 1, C, 2 * D)[:, kc, D:2 * D])) for kc in range(C)])
                    last.then_inc(s["v4_ps"], 1)
                    yield

                def scores(b):
                    need("k4_lo", b + 1)
                    need("v4_lo", b + 1)
                    if b == 0:
                        need("qbd4")
                    else:
                        need("sel_lo", b)
                    for g in range(GROUPS):
                        c, h = g // 2, 4 * (g % 2)
                        q = [qbd[:, a, c, b, h:h + 4, :].rearrange("p h q -> p (h q)") for a in range(2)]
                        last = product(pe, ps[:, g, 0:KEYS], [((q[0], q[1]), (kp[:, 0, c], kp[:, 1, c]))])
                    last.then_inc(s["s4_ps"], 1)
                    yield

                def turn_probs(b):
                    need("p4_last", b + 1)
                    for g in range(GROUPS):
                        for m in range(3):
                            src = probs[:, KEYS * g + m * P:KEYS * g + (m + 1) * P] if m < 2 else last_cols[:, g, :]
                            k = 3 * g + m
                            last = pe.transpose(ps[:, k // 4, (k % 4) * P:(k % 4 + 1) * P], src, ident)
                    last.then_inc(s["pt4_ps"], 1)
                    yield

                def values(b):
                    need("pt4_lo", b + 1)
                    for g in range(GROUPS):
                        cols = slice(64 * g, 64 * (g + 1))
                        pt = [[pt4[:, b % 2, a, g, m * P:(m + 1) * P] for a in range(2)] for m in range(3)]
                        last = product(pe, ps[:, 3, cols], [
                            ((pt[m][0], pt[m][1]), (vp[:, b % 2, 0, m, cols], vp[:, b % 2, 1, m, cols])) if m < 2 else
                            ((pt[m][0], pt[m][1]), (vl[:, 0, cols], vl[:, 1, cols])) for m in range(3)])
                    last.then_inc(s["o4_ps"], 1)
                    yield

                def select(b):
                    need("om4_lo", b + 1)
                    for c in range(C):
                        for a in range(2):
                            last = pe.matmul(ps[:, 3, 256 + SEQ * c:256 + SEQ * (c + 1)], om4[:, a, 2 * c:2 * c + 2, :].rearrange("p g d -> p (g d)"), sel16[:, :],
                                             start=(a == 0), stop=(a == 1))
                    last.then_inc(s["sel_ps"], 1)
                    yield

                yield from keys_values(0)
                for b in range(NB):
                    yield from scores(b)
                    yield from turn_probs(b)
                    yield from values(b)
                    if b + 1 < NB:
                        yield from keys_values(b + 1)
                    yield from select(b)
                need("sel_lo", NB)
                token_major(pe, ps[:, 0, 0:D], "xo", D, op, 0, D).then_inc(s["y4_ps"], 1)
                yield

            def scalar(act, t):
                def copy(dst, src, done, ready, n=1):
                    act.wait_ge(s[ready], at(t, ready, n))
                    act.activation(dst, src, ACT.Copy).then_inc(s[done], 1)
                    yield

                def xt_hi(n):
                    yield from copy(xt[:, 0].rearrange("p c n -> p (c n)"), ps[:, 0, 0:D], "xt_hi", "xt_ps", n + 1)

                yield from xt_hi(0)
                act.wait_ge(s["q0_f"], at(t, "q0_f", 1))
                act.activation(qk[:, 0, 0:2], qk_f[:, 0:2], ACT.Copy).then_inc(s["q0_hi"], 1)
                yield
                yield from copy(qk[:, 0, 2:4].rearrange("p c n -> p (c n)"), ps[:, 2, 0:D], "qp_hi", "qp_ps")
                act.wait_ge(s["s1_bias"], at(t, "s1_bias", 1))
                act.activation(probs[:, 0:KEYS], ps[:, 0, 0:KEYS], ACT.Exp, bias=small[:, 3:4], scale=D ** -0.5,
                               accum_out=small[:, 4:5]).then_inc(s["p1"], 1)
                yield
                yield from copy(pt1[:, 0, :], ps[:, 1, 0:384], "pt1_hi", "pt1_ps")
                yield from copy(op[:, 0].rearrange("p c n -> p (c n)"), ps[:, 2, 0:D], "a1_hi", "a1_ps")
                yield from last_hi(act, t)
                yield from xt_hi(1)
                act.wait_ge(s["qk_f"], at(t, "qk_f", 1))
                act.activation(qk[:, 0], qk_f[:, :, :], ACT.Copy).then_inc(s["qk_hi"], 1)
                yield
                yield from copy(v2[:, 0, :], ps[:, 2, 0:D], "v_hi", "v_ps")
                act.wait_ge(s["self_shift"], at(t, "self_shift", 1))
                act.activation(probs[:, 0:512], s2, ACT.Exp, scale=16 ** -0.5).then_inc(s["self_p"], 1)
                yield
                yield from copy(pt2[:, 0].rearrange("p g n -> p (g n)"), ps[:, 0, :], "self_pt_hi", "self_pt")
                act.wait_ge(s["o_f"], at(t, "o_f", 4))
                act.activation(om[:, 0].rearrange("p b n -> p (b n)"), om_f, ACT.Copy).then_inc(s["o_hi"], 1)
                yield
                for c in range(C):
                    if c == 0:
                        act.wait_ge(s["o2_ps"], at(t, "o2_ps", 1))
                    act.activation(op[:, 0, c], ps[:, 3, c * P:(c + 1) * P], ACT.Identity, bias=bcol("bv0")[:, c:c + 1]).then_inc(s["o2_hi"], 1)
                    yield
                for b in range(NB):
                    yield from np_hi(act, t, b)
                yield from copy(xqt.rearrange("p c n -> p (c n)"), ps[:, 3, 0:P].bitcast(BF16), "xqt", "xq_ps")
                act.wait_ge(s["gate_ps"], at(t, "gate_ps", 1))
                act.activation(th3, ps[:, 0:2, :].rearrange("p a n -> p (a n)"), ACT.Tanh, scale=small[:, 11:12]).then_inc(s["th3"], 1)
                yield
                yield from copy(hqt.rearrange("p k n -> p (k n)"), ps[:, 0, :].bitcast(BF16), "hqt", "hq_ps")
                yield from xt_hi(2)
                yield from copy(qk[:, 0, 0:2].rearrange("p c n -> p (c n)"), ps[:, 2, 0:D], "q4_hi", "q4_ps")
                yield from copy(vl[0:NB, 0, :], ps[0:NB, 3, 0:D], "vl_hi", "vl_ps")

                def k_hi(b):
                    yield from copy(kp[:, 0], ps[:, 0:2, 0:KEYS], "k4_hi", "k4_ps", b + 1)

                def v_hi(b):
                    if b >= 2:
                        act.wait_ge(s["o4_ps"], at(t, "o4_ps", b - 1))
                    yield from copy(vp[:, b % 2, 0].rearrange("p m n -> p (m n)"), ps[:, 2, :], "v4_hi", "v4_ps", b + 1)

                def om_hi(b):
                    act.wait_ge(s["om4_f"], at(t, "om4_f", b + 1))
                    act.activation(om4[:, 0].rearrange("p g d -> p (g d)"), om4_f, ACT.Copy).then_inc(s["om4_hi"], 1)
                    yield

                def sel_hi(b):
                    yield from copy(op[:, 0, :, SEQ * b:SEQ * (b + 1)], ps[:, 3, 256:320].rearrange("p (c n) -> p c n", c=C), "sel_hi", "sel_ps", b + 1)

                yield from k_hi(0)
                yield from v_hi(0)
                for b in range(NB):
                    act.wait_ge(s["s4_bias"], at(t, "s4_bias", b + 1))
                    for g in range(GROUPS):
                        act.activation(probs[:, KEYS * g:KEYS * (g + 1)], ps[:, g, 0:KEYS], ACT.Exp, bias=small[:, 24 + g:25 + g],
                                       scale=16 ** -0.5, accum_out=small[:, 28 + g:29 + g]).then_inc(s["p4"], 1)
                        yield
                    yield from tp_hi(act, t, b)
                    yield from copy(pt4[:, b % 2, 0].rearrange("p g n -> p (g n)"), ps[:, 0:3, :].rearrange("p a n -> p (a n)"), "pt4_hi", "pt4_ps", b + 1)
                    yield from om_hi(b)
                    if b + 1 < NB:
                        yield from k_hi(b + 1)
                        yield from v_hi(b + 1)
                    yield from sel_hi(b)

            def vector(dve, t):
                made = [0]

                def need(name, n=1):
                    dve.wait_ge(s[name], at(t, name, n))

                def then(ins):
                    made[0] += 1
                    ins.then_inc(s["dve_order"], 1)
                    yield
                    dve.wait_ge(s["dve_order"], at(t, "dve_order", made[0]))

                def alone():
                    made[0] += 1
                    dve.memset(waited[:, :], 0.0).then_inc(s["dve_order"], 1)
                    yield

                def lo(dst, src, hi, done, ready, n=1):
                    need(ready, n)
                    dve.tensor_tensor(dst, src, hi, ALU.subtract).then_inc(s[done], 1)
                    yield

                def normalise(n, src):
                    yield from then(dve.bn_stats(bn[:, :], src))
                    yield from alone()
                    yield from then(dve.bn_aggr(mv[:, :], bn[:, :]))
                    dve.tensor_scalar(var_eps[:, :], mv[:, 1:2], EPS, None, ALU.add).then_inc(s["ln_var"], 1)
                    yield
                    need("ln_rstd", n + 1)
                    return dve.tensor_scalar(xn[:, :], src, mv[:, 0:1], rstd[:, 0:1], ALU.subtract, ALU.mult)

                def normalised_t(k, n, src):
                    ins = yield from normalise(n, src)
                    ins.then_inc(s["xn"], 1)
                    yield
                    yield from lo(xt[:, 1].rearrange("p c n -> p (c n)"), ps[:, 0, 0:D], xt[:, 0].rearrange("p c n -> p (c n)"), "xt_lo", "xt_hi", k + 1)

                def add_block(ready, bank, row, src):
                    need(ready)
                    yield from then(dve.tensor_tensor(x[:, :], ps[:, bank, 0:D], x[:, :], ALU.add))
                    yield from then(dve.tensor_tensor(x[:, :], x[:, :], row_bias[:, row, :], ALU.add))

                def mask_queries(done):
                    src = qk[:, :, 0:2].rearrange("p l c (b q) -> p l (c b) q", b=NB)
                    dst = qbd.rearrange("p l c b h q -> p l (c b) h q")
                    for h in range(8):
                        ins = dve.tensor_scalar(dst[:, :, :, h, :], src, mask8[:, h:h + 1], None, ALU.mult)
                        if h < 7:
                            yield from then(ins)
                    ins.then_inc(s[done], 1)
                    yield

                dve.wait_ge(s[f"x_in{lane}"], t * 16 + 16)
                yield from normalised_t(0, 0, x0[:, :])
                need("q0_ps")
                dve.tensor_tensor(qk_f[:, 0:2], ps[:, 1, 0:D].rearrange("p (c n) -> p c n", c=C),
                                  bcol("bq0").unsqueeze(2).to_broadcast([P, C, P]), ALU.add).then_inc(s["q0_f"], 1)
                yield
                yield from lo(qk[:, 1, 0:2], qk_f[:, 0:2], qk[:, 0, 0:2], "q0_lo", "q0_hi")
                yield from lo(qk[:, 1, 2:4].rearrange("p c n -> p (c n)"), ps[:, 2, 0:D], qk[:, 0, 2:4].rearrange("p c n -> p (c n)"), "qp_lo", "qp_hi")
                need("qbk_ps")
                yield from then(dve.tensor_copy(small[:, 0:1], ps[:, 3, 0:1]))
                need("s1_ps")
                yield from then(dve.tensor_reduce(small[:, 1:2], ps[:, 0, 0:KEYS], X, ALU.max))
                yield from then(dve.tensor_tensor(small[:, 2:3], small[:, 1:2], small[:, 0:1], ALU.add))
                yield from then(dve.tensor_tensor(small[:, 2:3], small[:, 0:1], small[:, 2:3], ALU.subtract))
                dve.tensor_scalar(small[:, 3:4], small[:, 2:3], D ** -0.5, None, ALU.mult).then_inc(s["s1_bias"], 1)
                yield
                need("p1")
                dve.tensor_scalar(last_cols[:, 0, 0:NB], quad, probs[:, KEYS - 1:KEYS], None, ALU.mult).then_inc(s["p1_last"], 1)
                yield
                yield from then(dve.reciprocal(small[:, 5:6], small[:, 4:5]))
                yield from lo(pt1[:, 1, :], ps[:, 1, 0:384], pt1[:, 0, :], "pt1_lo", "pt1_hi")
                yield from lo(op[:, 1].rearrange("p c n -> p (c n)"), ps[:, 2, 0:D], op[:, 0].rearrange("p c n -> p (c n)"), "a1_lo", "a1_hi")
                need("y1_ps")
                dve.wait_ge(s[f"stored{lane}"], t * 16 + 1)
                yield from then(dve.scalar_tensor_tensor(x[:, :], ps[:, 3, 0:D], small[:, 5:6], x0[:, :], ALU.mult, ALU.add))
                dve.tensor_tensor(x[:, :], x[:, :], row_bias[:, 0, :], ALU.add).then_inc(s["x_1"], 1)
                yield
                need("x_1")

                yield from normalised_t(1, 1, x[:, :])
                need("qk_ps")
                dve.tensor_tensor(qk_f[:, :, :], ps[:, 1].rearrange("p (c n) -> p c n", c=4),
                                  bcol("bqk0").unsqueeze(2).to_broadcast([P, 4, P]), ALU.add).then_inc(s["qk_f"], 1)
                yield
                need("qk_hi")
                yield from then(dve.tensor_tensor(qk[:, 1], qk_f[:, :, :], qk[:, 0], ALU.subtract))
                yield from mask_queries("qbd2")
                need("v_hi")
                yield from then(dve.tensor_tensor(v2[:, 1, :], ps[:, 2, 0:D], v2[:, 0, :], ALU.subtract))
                for b in range(NB):
                    ins = dve.tensor_scalar(vblk.rearrange("p l g b d -> p (l g) b d")[:, :, b, :],
                                            v2.rearrange("p l (g d) -> p (l g) d", g=GROUPS), quad[:, b:b + 1], None, ALU.mult)
                    if b < NB - 1:
                        yield from then(ins)
                ins.then_inc(s["self_v"], 1)
                yield
                need("self_s")
                s2v = s2.rearrange("p (n k) -> p n k", k=SEQ)
                yield from then(dve.tensor_tensor(s2v, ps[:, 3, :].rearrange("p (n k) -> p n k", k=SEQ),
                                       causal.unsqueeze(1).to_broadcast([P, 16, SEQ]), ALU.add))
                yield from then(dve.tensor_reduce(small[:, 64:80], s2v, X, ALU.max))
                dve.tensor_tensor(s2v, s2v, small[:, 64:80].unsqueeze(2).to_broadcast([P, 16, SEQ]), ALU.subtract).then_inc(s["self_shift"], 1)
                yield
                need("self_p")
                yield from then(dve.tensor_reduce(small[:, 64:80], probs[:, 0:512].rearrange("p (n k) -> p n k", k=SEQ), X, ALU.add))
                yield from then(dve.reciprocal(small[:, 80:96], small[:, 64:80]))
                rm = th_rm[:, :, :]
                yield from then(dve.tensor_tensor(rm, small[:, 80:96].unsqueeze(2).to_broadcast([P, 16, 4]),
                                       quad.unsqueeze(1).to_broadcast([P, 16, 4]), ALU.mult))
                yield from lo(pt2[:, 1].rearrange("p g n -> p (g n)"), ps[:, 0, :], pt2[:, 0].rearrange("p g n -> p (g n)"), "pt2_lo", "self_pt_hi")
                need("o2g_ps")
                for g in range(GROUPS):
                    dst = om_f.rearrange("p (b g h d) -> p g b h d", b=NB, g=GROUPS, h=4)[:, g]
                    src = ps[:, 1 + g // 2, (g % 2) * D:(g % 2 + 1) * D].rearrange("p (b h d) -> p b h d", b=NB, h=4)
                    dve.tensor_tensor(dst, src, rm[:, NB * g:NB * (g + 1), :].unsqueeze(3).to_broadcast([P, NB, 4, 16]),
                                      ALU.mult).then_inc(s["o_f"], 1)
                    yield
                need("o2_hi", 2)
                for c in range(C):
                    dve.scalar_tensor_tensor(op[:, 1, c], ps[:, 3, c * P:(c + 1) * P], bcol("bv0")[:, c:c + 1], op[:, 0, c],
                                             ALU.add, ALU.subtract).then_inc(s["o2_lo"], 1)
                    yield
                yield from add_block("self_y", 0, 1, x)

                ins = yield from normalise(2, x[:, :])
                yield from then(ins)
                yield from then(dve.tensor_reduce(small[:, 8:9], xn[:, :], X, ALU.max, apply_absolute_value=True))
                yield from then(dve.tensor_scalar(small[:, 8:9], small[:, 8:9], 1e-5, None, ALU.max))
                yield from then(dve.reciprocal(small[:, 9:10], small[:, 8:9]))
                yield from then(dve.tensor_scalar(small[:, 9:10], small[:, 9:10], 127.0, None, ALU.mult))
                yield from then(dve.tensor_scalar(xq_f, xn[:, :], small[:, 9:10], ROUND, ALU.mult, ALU.add))
                yield from then(dve.tensor_scalar(xq_f, xq_f, ROUND, 127.0, ALU.subtract, ALU.min))
                yield from then(dve.tensor_scalar(small[:, 10:11], small[:, 8:9], 1.0 / 127.0, None, ALU.mult))
                yield from then(dve.tensor_scalar(small[:, 11:12], small[:, 10:11], ffn_inv[:, 0:1], 0.5, ALU.mult, ALU.mult))
                yield from then(dve.tensor_scalar(small[:, 12:13], small[:, 10:11], ffn_inv[:, 1:2], small[:, 11:12], ALU.mult, ALU.mult))
                dve.tensor_scalar(xq, xq_f, -128.0, None, ALU.max).then_inc(s["xq"], 1)
                yield
                need("th3")
                gate_v = ps[:, 0:2, :].rearrange("p a n -> p (a n)")
                yield from then(dve.scalar_tensor_tensor(r3, th3, 1.0, gate_v, ALU.add, ALU.mult))
                need("up_ps")
                yield from then(dve.tensor_tensor(r3, r3, ps[:, 2:4, :].rearrange("p a n -> p (a n)"), ALU.mult))
                yield from then(dve.tensor_reduce(small[:, 13:14], r3, X, ALU.max, apply_absolute_value=True))
                yield from then(dve.tensor_scalar(small[:, 13:14], small[:, 13:14], small[:, 12:13], 1e-5, ALU.mult, ALU.max))
                yield from then(dve.reciprocal(small[:, 14:15], small[:, 13:14]))
                yield from then(dve.tensor_scalar(small[:, 15:16], small[:, 14:15], small[:, 12:13], 127.0, ALU.mult, ALU.mult))
                yield from then(dve.tensor_scalar(rq3, r3, small[:, 15:16], ROUND, ALU.mult, ALU.add))
                yield from then(dve.tensor_scalar(rq3, rq3, ROUND, 127.0, ALU.subtract, ALU.min))
                dve.tensor_scalar(hq, rq3, -128.0, None, ALU.max).then_inc(s["hq"], 1)
                yield
                yield from then(dve.tensor_scalar(small[:, 16:17], small[:, 13:14], ffn_inv[:, 2:3], 1.0 / 127.0, ALU.mult, ALU.mult))
                need("y3_ps")
                yield from then(dve.scalar_tensor_tensor(x[:, :], ps[:, 1, 0:D], small[:, 16:17], x[:, :], ALU.mult, ALU.add))

                yield from normalised_t(2, 3, x[:, :])
                need("q4_hi")
                dve.tensor_tensor(qk[:, 1, 0:2].rearrange("p c n -> p (c n)"), ps[:, 2, 0:D], qk[:, 0, 0:2].rearrange("p c n -> p (c n)"),
                                  ALU.subtract).then_inc(s["q4_lo"], 1)
                yield
                need("q4_lo")
                yield from mask_queries("qbd4")
                yield from lo(vl[0:NB, 1, :], ps[0:NB, 3, 0:D], vl[0:NB, 0, :], "vl_lo", "vl_hi")

                def k_lo(b):
                    yield from lo(kp[:, 1], ps[:, 0:2, 0:KEYS], kp[:, 0], "k4_lo", "k4_hi", b + 1)

                def v_lo(b):
                    yield from lo(vp[:, b % 2, 1].rearrange("p m n -> p (m n)"), ps[:, 2, :], vp[:, b % 2, 0].rearrange("p m n -> p (m n)"), "v4_lo", "v4_hi", b + 1)

                rm4 = [th_rm[:, 4 * i:4 * i + 4, :] for i in range(2)]

                def om_mask(b):
                    need("o4_ps", b + 1)
                    dve.tensor_tensor(om4_f.rearrange("p (n d) -> p n d", d=16), ps[:, 3, 0:256].rearrange("p (n d) -> p n d", d=16),
                                      rm4[b % 2].rearrange("p n h -> p (n h)").unsqueeze(2).to_broadcast([P, 16, 16]), ALU.mult).then_inc(s["om4_f"], 1)
                    yield

                def sel_lo(b):
                    toks = slice(SEQ * b, SEQ * (b + 1))
                    yield from lo(op[:, 1, :, toks], ps[:, 3, 256:320].rearrange("p (c n) -> p c n", c=C), op[:, 0, :, toks], "sel_lo", "sel_hi", b + 1)

                yield from k_lo(0)
                yield from v_lo(0)
                for b in range(NB):
                    need("s4_ps", b + 1)
                    yield from then(dve.tensor_reduce(small[:, 20:24], ps[:, 0:4, 0:KEYS], X, ALU.max))
                    dve.tensor_scalar(small[:, 24:28], small[:, 20:24], -(16 ** -0.5), None, ALU.mult).then_inc(s["s4_bias"], 1)
                    yield
                    need("p4", GROUPS * (b + 1))
                    pv = probs[:, 0:GROUPS * KEYS].rearrange("p (g m) -> p g m", g=GROUPS)
                    dve.tensor_tensor(last_cols[:, :, 0:NB], pv[:, :, KEYS - 1:KEYS].to_broadcast([P, GROUPS, NB]),
                                      eye4[:, b, :].unsqueeze(1).to_broadcast([P, GROUPS, NB]), ALU.mult).then_inc(s["p4_last"], 1)
                    yield
                    yield from then(dve.reciprocal(small[:, 32:36], small[:, 28:32]))
                    yield from then(dve.tensor_tensor(rm4[b % 2], small[:, 32:36].unsqueeze(2).to_broadcast([P, 4, 4]),
                                           quad.unsqueeze(1).to_broadcast([P, 4, 4]), ALU.mult))
                    yield from lo(pt4[:, b % 2, 1].rearrange("p g n -> p (g n)"), ps[:, 0:3, :].rearrange("p a n -> p (a n)"), pt4[:, b % 2, 0].rearrange("p g n -> p (g n)"),
                                  "pt4_lo", "pt4_hi", b + 1)
                    yield from om_mask(b)
                    if b + 1 < NB:
                        yield from k_lo(b + 1)
                        yield from v_lo(b + 1)
                    yield from sel_lo(b)
                need("y4_ps")
                yield from then(dve.tensor_tensor(x[:, :], ps[:, 0, 0:D], x[:, :], ALU.add))
                dve.tensor_tensor(x[:, :], x[:, :], row_bias[:, 2, :], ALU.add).then_inc(s["x_4"], 1)
                yield
                assert made[0] == FIRST["dve_order"], made[0]

            def gpsimd(pool, t):
                def power(n):
                    pool.wait_ge(s["ln_var"], at(t, "ln_var", n + 1))
                    pool.tensor_tensor(rstd[:, :], var_eps[:, :], neg_half[:, :], ALU.pow).then_inc(s["ln_rstd"], 1)
                    yield

                yield from power(0)
                yield from power(1)
                yield from last_lo(pool, t)
                pool.wait_ge(s["o_hi"], at(t, "o_hi", 1))
                pool.tensor_tensor(om[:, 1].rearrange("p b n -> p (b n)"), om_f,
                                   om[:, 0].rearrange("p b n -> p (b n)"), ALU.subtract).then_inc(s["o_lo"], 1)
                yield
                for b in range(NB):
                    yield from np_lo(pool, t, b)
                yield from power(2)
                yield from power(3)
                for b in range(NB):
                    pool.wait_ge(s["om4_hi"], at(t, "om4_hi", b + 1))
                    pool.tensor_tensor(om4[:, 1].rearrange("p g d -> p (g d)"), om4_f,
                                       om4[:, 0].rearrange("p g d -> p (g d)"), ALU.subtract).then_inc(s["om4_lo"], 1)
                    yield
                    yield from tp_lo(pool, t, b)

            return dict(ctx_lp=ctx_lp, tensor=tensor, scalar=scalar, vector=vector, gpsimd=gpsimd, scalar_before=scalar_before,
                                   gpsimd_before=gpsimd_before, load_n=load_n, load_t=load_t, load_l=load_l, load_x=load_x,
                                   store_x=store_x, at=at)

        def second_half(lane):
            me = own[lane]
            x0, x, x_out, xn, xt, bn, mv, var_eps, rstd = me["x0"], me["x"], me["x_out"], me["xn"], me["xt"], me["bn"], me["mv"], me["var_eps"], me["rstd"]
            qk_f, qk, small, idx, waited, gate_p = me["qk_f"], me["qk"], me["small"], me["idx"], me["waited"], me["gate_p"]
            at = counter(SECOND, FIRST, lane)
            ps = psum[:, 4 * lane:4 * lane + 4, :]
            arena = mem[:, W_COLS[1] + LANE_2 * lane:W_COLS[1] + LANE_2 * (lane + 1)]
            qb5 = carve(arena, 6144, 1024, F16).rearrange("p (l c b h q) -> p l c b h q", l=2, c=C, b=NB, h=4)
            v5 = carve(arena, 0, 1024, F16).rearrange("p (l n) -> p l n", l=2)
            s5 = carve(arena, 1024, 512)
            pt5 = carve(arena, 1536, 512, F16).rearrange("p (l g n) -> p l g n", l=2, g=GROUPS)
            ptb = carve(arena, 2048, 2048, F16).rearrange("p (l g b n) -> p l g b n", l=2, g=GROUPS, b=NB)
            o5_f = carve(arena, 4096, 1024)
            o5 = carve(arena, 5120, 1024, F16).rearrange("p (l j n) -> p l j n", l=2, j=8)
            wb = carve(arena, 0, 1024).rearrange("p (e n) -> p e n", e=EXPERTS)
            mb = carve(arena, 1024, 1024).rearrange("p (e n) -> p e n", e=EXPERTS)
            u4 = carve(arena, 2048, 1024).rearrange("p (s c n) -> p s c n", s=2, c=4)
            th6 = carve(arena, 3072, 512)
            v6 = carve(arena, 3584, 256)
            h_f = carve(arena, 3840, 512)
            hp = carve(arena, 4352, 512, F16)
            x2_f = carve(arena, 4864, 256)
            a3_f = carve(arena, 5120, 256)
            y = carve(arena, 5376, 256)
            prod = carve(arena, 5632, 256)

            def load_x(sp, trip):
                sp.wait_ge(s["x_5"], at(trip, "x_5", 0))
                sp.dma_start(x0[:, :], mid[bass.ds(trip * LANES + lane, 1)].rearrange("t p d -> (t p) d")).then_inc(s[f"x_in{lane}"], 16)

            def store_out(act, trip):
                act.wait_ge(s["x_final"], at(trip, "x_final", 1))
                act.dma_start(out[bass.ds(trip * LANES + lane, 1)].rearrange("t p d -> (t p) d"), x_out[:, :]).then_inc(s[f"stored{lane}"], 16)

            def tensor(pe, t):
                def need(name, n=1):
                    pe.wait_ge(s[name], at(t, name, n))

                def transpose_x(n):
                    need("xn", n + 1)
                    for c in range(C):
                        last = pe.transpose(ps[:, 0, c * P:(c + 1) * P], xn[:, c * P:(c + 1) * P], ident)
                    last.then_inc(s["xt_ps"], 1)
                    yield
                    need("xt_lo", n + 1)

                def self_scores(g):
                    need("qb5", g + 1)
                    if g == 0:
                        need("self_v")
                    for b in range(NB):
                        last = product(pe, ps[:, 2, g * P + SEQ * b:g * P + SEQ * (b + 1)], [
                            ((qb5[:, 0, c, b].rearrange("p h q -> p (h q)"), qb5[:, 1, c, b].rearrange("p h q -> p (h q)")),
                             (qk[:, 0, 2 + c, SEQ * b:SEQ * (b + 1)], qk[:, 1, 2 + c, SEQ * b:SEQ * (b + 1)])) for c in range(C)])
                    last.then_inc(s["self_s"], 1)
                    yield

                yield from transpose_x(0)
                for j in range(2):
                    last = token_major(pe, ps[:, 2 + j, :], "av", WIDE, xt, 512 * j, 512 * (j + 1))
                last.then_inc(s["v_ps"], 1)
                yield
                for g in range(GROUPS):
                    if g >= 2:
                        need("qk_f", g - 1)
                    bank = ps[:, g % 2]
                    feature_major(pe, bank[:, 0:D], "aq", WIDE, xt, range(2 * g, 2 * g + 2))
                    feature_major(pe, bank[:, D:2 * D], "ak", WIDE, xt, range(2 * g, 2 * g + 2)).then_inc(s["qk_ps"], 1)
                    yield
                    if g >= 1:
                        yield from self_scores(g - 1)
                yield from self_scores(GROUPS - 1)
                need("p5_norm")
                for g in range(GROUPS):
                    last = pe.transpose(ps[:, 3, g * P:(g + 1) * P], s5[:, g * P:(g + 1) * P], ident)
                last.then_inc(s["self_pt"], 1)
                yield
                need("ptb")
                for j in range(8):
                    hh = (j % 2) * 64
                    pt = [ptb[:, a, j // 2, :, hh:hh + 64] for a in range(2)]
                    last = product(pe, ps[:, j // 2, (j % 2) * D:(j % 2 + 1) * D],
                                   [((v5[:, 0, j * P:(j + 1) * P], v5[:, 1, j * P:(j + 1) * P]), (pt[0], pt[1]))])
                    if j % 2:
                        last.then_inc(s["o5_ps"], 1)
                        yield
                need("o_lo")
                token_major(pe, ps[:, 0, 0:D], "ao", D, o5, 0, D, k=8).then_inc(s["self_y"], 1)
                yield

                yield from transpose_x(1)
                token_major(pe, ps[:, 3, 0:EXPERTS], "gate", EXPERTS, xt, 0, EXPERTS).then_inc(s["gate_ps"], 1)
                yield
                feature_major(pe, ps[:, 1], "sw1", SHARED, xt, range(4))
                feature_major(pe, ps[:, 2], "sw2", SHARED, xt, range(4)).then_inc(s["sh_ps"], 1)
                yield
                need("gate_p")
                need("sh_f")
                for e in range(EXPERTS):
                    for a in range(2):
                        last = pe.matmul(ps[:, 1 + e // 4, (e % 4) * P:(e % 4 + 1) * P], gate_p[:, a, e:e + 1].to_broadcast([P, P]), ident16[:, :],
                                         start=(a == 0), stop=(a == 1))
                last.then_inc(s["wb_ps"], 1)
                yield
                for e in range(EXPERTS):
                    last = pe.matmul(ps[:, (3, 0)[e // 4], (e % 4) * P:(e % 4 + 1) * P], gate_p[:, 2, e:e + 1].to_broadcast([P, P]), ident16[:, :],
                                     start=True, stop=True)
                last.then_inc(s["mb_ps"], 1)
                yield
                need("sh_lo")
                need("mb", 2)
                sp_pair = hp.rearrange("p (l k n) -> p l k n", l=2, k=4)
                feature_major(pe, ps[:, 0], "sw3", D, sp_pair, range(C), k=4).then_inc(s["y4_ps"], 1)
                yield

                def expert_in(e):
                    if e < 2:
                        need("wb")
                    else:
                        need("u4", e - 1)
                    bank = ps[:, 1 + e % 2]
                    feature_major(pe, bank[:, 0:D], "w1", D, xt, range(C), first=e * C * D)
                    feature_major(pe, bank[:, D:2 * D], "w3", D, xt, range(C), first=e * C * D).then_inc(s["e13_ps"], 1)
                    yield

                he = hp[:, 0:512].rearrange("p (l k n) -> p l k n", l=2, k=C)
                yield from expert_in(0)
                for e in range(EXPERTS):
                    if e + 1 < EXPERTS:
                        yield from expert_in(e + 1)
                    need("he_lo", e + 1)
                    if e == 1:
                        need("y_0")
                    if e >= 2:
                        need("x2", 2 * (e - 1))
                    feature_major(pe, ps[:, (3, 0)[e % 2]], "w2", D, he, range(C), first=e * C * D).then_inc(s["e2_ps"], 1)
                    yield
                need("y_add", EXPERTS)
                for c in range(C):
                    last = pe.transpose(ps[:, 0, c * P:(c + 1) * P], y[:, c * P:(c + 1) * P], ident)
                last.then_inc(s["y3_ps"], 1)
                yield

            def scalar(act, t):
                def copy(dst, src, done, ready, n=1):
                    act.wait_ge(s[ready], at(t, ready, n))
                    act.activation(dst, src, ACT.Copy).then_inc(s[done], 1)
                    yield

                def xt_hi(n):
                    yield from copy(xt[:, 0].rearrange("p c n -> p (c n)"), ps[:, 0, 0:D], "xt_hi", "xt_ps", n + 1)

                yield from xt_hi(0)
                yield from copy(v5[:, 0, :], ps[:, 2:4, :].rearrange("p a n -> p (a n)"), "v_hi", "v_ps")
                for g in range(GROUPS):
                    act.wait_ge(s["qk_f"], at(t, "qk_f", g + 1))
                    act.activation(qk[:, 0], qk_f[:, :, :], ACT.Copy).then_inc(s["qk_hi"], 1)
                    yield
                act.wait_ge(s["self_shift"], at(t, "self_shift", 1))
                act.activation(s5, s5, ACT.Exp, scale=64 ** -0.5).then_inc(s["self_p"], 1)
                yield
                yield from copy(pt5[:, 0].rearrange("p g n -> p (g n)"), ps[:, 3, :], "self_pt_hi", "self_pt")
                act.wait_ge(s["o_f"], at(t, "o_f", 8))
                act.activation(o5[:, 0].rearrange("p j n -> p (j n)"), o5_f, ACT.Copy).then_inc(s["o_hi"], 1)
                yield
                yield from xt_hi(1)
                act.wait_ge(s["s1_bias"], at(t, "s1_bias", 1))
                act.activation(small[:, 48:56], ps[:, 3, 0:EXPERTS], ACT.Exp, bias=small[:, 40:41], accum_out=small[:, 41:42]).then_inc(s["p1"], 1)
                yield
                act.wait_ge(s["sh_ps"], at(t, "sh_ps", 1))
                act.activation(th6, ps[:, 1, :], ACT.Tanh, scale=0.5).then_inc(s["th_sh"], 1)
                yield
                act.wait_ge(s["sh_f"], at(t, "sh_f", 1))
                act.activation(hp[:, 0:512], h_f, ACT.Copy).then_inc(s["sh_hi"], 1)
                yield
                yield from copy(wb, ps[:, 1:3, :].rearrange("p a (e n) -> p (a e) n", n=P), "wb", "wb_ps")
                for i in range(2):
                    yield from copy(mb[:, 4 * i:4 * i + 4], ps[:, (3, 0)[i], :].rearrange("p (e n) -> p e n", n=P), "mb", "mb_ps")
                for e in range(EXPERTS):
                    act.wait_ge(s["u4"], at(t, "u4", e + 1))
                    for c in range(C):
                        k = e * C + c
                        act.activation(th6[:, c * P:(c + 1) * P], u4[:, e % 2, c], ACT.Tanh, scale=0.5, bias=half_b1[:, k:k + 1]).then_inc(s["th_e"], 1)
                        yield
                    for c in range(C):
                        k = e * C + c
                        act.activation(v6[:, c * P:(c + 1) * P], u4[:, e % 2, c], ACT.Identity, bias=bcol("b1")[:, k:k + 1]).then_inc(s["th_e"], 1)
                        yield
                    act.wait_ge(s["he_f"], at(t, "he_f", e + 1))
                    if e >= 1:
                        act.wait_ge(s["e2_ps"], at(t, "e2_ps", e))
                    act.activation(hp[:, 0:256], h_f[:, 0:256], ACT.Copy).then_inc(s["he_hi"], 1)
                    yield
                store_out(act, t)
                yield

            def vector(dve, t):
                made = [0]

                def need(name, n=1):
                    dve.wait_ge(s[name], at(t, name, n))

                def then(ins):
                    made[0] += 1
                    ins.then_inc(s["dve_order"], 1)
                    yield
                    dve.wait_ge(s["dve_order"], at(t, "dve_order", made[0]))

                def alone():
                    made[0] += 1
                    dve.memset(waited[:, :], 0.0).then_inc(s["dve_order"], 1)
                    yield

                def lo(dst, src, hi, done, ready, n=1):
                    need(ready, n)
                    dve.tensor_tensor(dst, src, hi, ALU.subtract).then_inc(s[done], 1)
                    yield

                def normalise(n, src):
                    yield from then(dve.bn_stats(bn[:, :], src))
                    yield from alone()
                    yield from then(dve.bn_aggr(mv[:, :], bn[:, :]))
                    dve.tensor_scalar(var_eps[:, :], mv[:, 1:2], EPS, None, ALU.add).then_inc(s["ln_var"], 1)
                    yield
                    need("ln_rstd", n + 1)
                    return dve.tensor_scalar(xn[:, :], src, mv[:, 0:1], rstd[:, 0:1], ALU.subtract, ALU.mult)

                def normalised_t(k, n, src):
                    ins = yield from normalise(n, src)
                    ins.then_inc(s["xn"], 1)
                    yield
                    yield from lo(xt[:, 1].rearrange("p c n -> p (c n)"), ps[:, 0, 0:D], xt[:, 0].rearrange("p c n -> p (c n)"), "xt_lo", "xt_hi", k + 1)

                dve.wait_ge(s[f"x_in{lane}"], (TRIPS + t) * 16 + 32)
                yield from normalised_t(0, 0, x0[:, :])
                yield from lo(v5[:, 1, :], ps[:, 2:4, :].rearrange("p a n -> p (a n)"), v5[:, 0, :], "self_v", "v_hi")
                for g in range(GROUPS):
                    need("qk_ps", g + 1)
                    if g >= 1:
                        need("qk5_lo", g)
                    dve.tensor_tensor(qk_f[:, :, :], ps[:, g % 2].rearrange("p (c n) -> p c n", c=4),
                                      bcol("bqk1")[:, 4 * g:4 * g + 4].unsqueeze(2).to_broadcast([P, 4, P]), ALU.add).then_inc(s["qk_f"], 1)
                    yield
                    need("qk5_lo", g + 1)
                    for h in range(4):
                        c = h // 2
                        ins = dve.tensor_scalar(qb5[:, :, c, :, h, :], qk[:, :, c].rearrange("p l (b q) -> p l b q", b=NB),
                                                half[:, h % 2:h % 2 + 1], None, ALU.mult)
                        if h < 3:
                            yield from then(ins)
                    ins.then_inc(s["qb5"], 1)
                    yield
                    need("self_s", g + 1)
                s5v = s5.rearrange("p (n k) -> p n k", k=SEQ)
                psv = ps[:, 2, :].rearrange("p (n k) -> p n k", k=SEQ)
                yield from then(dve.tensor_reduce(small[:, 64:80], psv, X, ALU.max))
                dve.tensor_tensor(s5v, psv, small[:, 64:80].unsqueeze(2).to_broadcast([P, 16, SEQ]), ALU.subtract).then_inc(s["self_shift"], 1)
                yield
                need("self_p")
                yield from then(dve.tensor_reduce(small[:, 64:80], s5v, X, ALU.add))
                yield from then(dve.reciprocal(small[:, 80:96], small[:, 64:80]))
                dve.tensor_tensor(s5v, s5v, small[:, 80:96].unsqueeze(2).to_broadcast([P, 16, SEQ]), ALU.mult).then_inc(s["p5_norm"], 1)
                yield
                need("self_pt_hi")
                yield from then(dve.tensor_tensor(pt5[:, 1].rearrange("p g n -> p (g n)"), ps[:, 3, :], pt5[:, 0].rearrange("p g n -> p (g n)"), ALU.subtract))
                for b in range(NB):
                    ins = dve.tensor_scalar(ptb.rearrange("p l g b n -> p (l g) b n")[:, :, b, :],
                                            pt5.rearrange("p l g n -> p (l g) n"), quad[:, b:b + 1], None, ALU.mult)
                    if b < NB - 1:
                        yield from then(ins)
                ins.then_inc(s["ptb"], 1)
                yield
                for i in range(4):
                    need("o5_ps", i + 1)
                    for hh in range(2):
                        pr = slice(64 * hh, 64 * hh + 64)
                        src = ps[pr, i, :].rearrange("p (j b h q) -> p j b h q", j=2, b=NB, h=2)[:, :, :, hh, :]
                        dst = o5_f[pr, 256 * i:256 * (i + 1)].rearrange("p (j b q) -> p j b q", j=2, b=NB)
                        a0 = B_AT["bv1"][0] + 2 * i
                        dve.tensor_tensor(dst, src, bias[pr, a0:a0 + 2].unsqueeze(2).unsqueeze(3).to_broadcast([64, 2, NB, SEQ]),
                                          ALU.add).then_inc(s["o_f"], 1)
                        yield
                need("self_y")
                dve.tensor_tensor(x[:, :], ps[:, 0, 0:D], x0[:, :], ALU.add).then_inc(s["x_5"], 1)
                yield
                need("x_5")
                yield from then(dve.tensor_tensor(x[:, :], x[:, :], row_bias[:, 3, :], ALU.add))

                yield from normalised_t(1, 1, x[:, :])
                need("gate_ps")
                yield from then(dve.tensor_reduce(small[:, 42:43], ps[:, 3, 0:EXPERTS], X, ALU.max))
                dve.tensor_scalar(small[:, 40:41], small[:, 42:43], -1.0, None, ALU.mult).then_inc(s["s1_bias"], 1)
                yield
                need("p1")
                yield from then(dve.reciprocal(small[:, 43:44], small[:, 41:42]))
                yield from then(dve.tensor_scalar(small[:, 48:56], small[:, 48:56], small[:, 43:44], None, ALU.mult))
                yield from alone()
                yield from then(dve.max(small[:, 56:64], small[:, 48:56]))
                yield from alone()
                yield from then(dve.max_index(idx[:, :], small[:, 56:64], small[:, 48:56]))
                yield from then(dve.tensor_copy(small[:, 56:64], idx[:, :]))
                yield from then(dve.tensor_scalar(small[:, 80:88], const("iota8"), small[:, 56:57], None, ALU.is_equal))
                yield from then(dve.scalar_tensor_tensor(gate_p[:, 2, :], const("iota8"), small[:, 57:58], small[:, 80:88], ALU.is_equal, ALU.add))
                yield from then(dve.tensor_copy(gate_p[:, 0, :], small[:, 48:56]))
                dve.tensor_tensor(gate_p[:, 1, :], small[:, 48:56], gate_p[:, 0, :], ALU.subtract).then_inc(s["gate_p"], 1)
                yield
                need("th_sh")
                yield from then(dve.scalar_tensor_tensor(h_f, th6, 1.0, ps[:, 1, :], ALU.add, ALU.mult))
                dve.scalar_tensor_tensor(h_f, h_f, 0.5, ps[:, 2, :], ALU.mult, ALU.mult).then_inc(s["sh_f"], 1)
                yield
                need("y4_ps")
                dve.tensor_copy(y, ps[:, 0, 0:D]).then_inc(s["y_0"], 1)
                yield

                def scale_in(e):
                    need("e13_ps", e + 1)
                    if e == 0:
                        need("mb", 2)
                    dve.tensor_tensor(u4[:, e % 2], ps[:, 1 + e % 2].rearrange("p (c n) -> p c n", c=4),
                                      wb[:, e].unsqueeze(1).to_broadcast([P, 4, P]), ALU.mult).then_inc(s["u4"], 1)
                    yield

                yield from scale_in(0)
                for e in range(EXPERTS):
                    need("th_e", 4 * (e + 1))
                    if e >= 1:
                        need("he_lo", e)
                    dve.scalar_tensor_tensor(h_f[:, 0:256], th6[:, 0:256], 1.0, v6, ALU.add, ALU.mult).then_inc(s["he_f"], 1)
                    yield
                    if e + 1 < EXPERTS:
                        if e >= 1:
                            need("a3", e)
                        yield from scale_in(e + 1)
                    if e >= 1:
                        need("prod", e)
                    need("e2_ps", e + 1)
                    for c in range(C):
                        k = e * C + c
                        dve.tensor_scalar(x2_f[:, c * P:(c + 1) * P], ps[:, (3, 0)[e % 2], c * P:(c + 1) * P], 0.5, bcol("b2")[:, k:k + 1],
                                          ALU.mult, ALU.add).then_inc(s["x2"], 1)
                        yield
                    for c in range(C):
                        k = e * C + c
                        ins = dve.scalar_tensor_tensor(a3_f[:, c * P:(c + 1) * P], u4[:, e % 2, 2 + c], bcol("b3")[:, k:k + 1], mb[:, e],
                                                       ALU.add, ALU.mult)
                        if c == 0:
                            yield from then(ins)
                    ins.then_inc(s["a3"], 1)
                    yield
                need("y3_ps")
                dve.wait_ge(s[f"stored{lane}"], (TRIPS + t) * 16 + 1)
                dve.tensor_tensor(x_out[:, :], ps[:, 0, 0:D], x[:, :], ALU.add).then_inc(s["x_final"], 1)
                yield
                assert made[0] == SECOND["dve_order"], made[0]

            def gpsimd(pool, t):
                def power(n):
                    pool.wait_ge(s["ln_var"], at(t, "ln_var", n + 1))
                    pool.tensor_tensor(rstd[:, :], var_eps[:, :], neg_half[:, :], ALU.pow).then_inc(s["ln_rstd"], 1)
                    yield

                yield from power(0)
                for g in range(GROUPS):
                    pool.wait_ge(s["qk_hi"], at(t, "qk_hi", g + 1))
                    pool.tensor_tensor(qk[:, 1], qk_f[:, :, :], qk[:, 0], ALU.subtract).then_inc(s["qk5_lo"], 1)
                    yield
                pool.wait_ge(s["o_hi"], at(t, "o_hi", 1))
                pool.tensor_tensor(o5[:, 1].rearrange("p j n -> p (j n)"), o5_f,
                                   o5[:, 0].rearrange("p j n -> p (j n)"), ALU.subtract).then_inc(s["o_lo"], 1)
                yield
                yield from power(1)
                pool.wait_ge(s["sh_hi"], at(t, "sh_hi", 1))
                pool.tensor_tensor(hp[:, 512:1024], h_f, hp[:, 0:512], ALU.subtract).then_inc(s["sh_lo"], 1)
                yield
                for e in range(EXPERTS):
                    if e == 0:
                        pool.wait_ge(s["y_0"], at(t, "y_0", 1))
                    pool.wait_ge(s["he_hi"], at(t, "he_hi", e + 1))
                    pool.tensor_tensor(hp[:, 256:512], h_f[:, 0:256], hp[:, 0:256], ALU.subtract).then_inc(s["he_lo"], 1)
                    yield
                    pool.wait_ge(s["a3"], at(t, "a3", e + 1))
                    pool.tensor_tensor(prod, x2_f, a3_f, ALU.mult).then_inc(s["prod"], 1)
                    yield
                    pool.wait_ge(s["prod"], at(t, "prod", e + 1))
                    pool.tensor_tensor(y, y, prod, ALU.add).then_inc(s["y_add"], 1)
                    yield
                    pool.wait_ge(s["y_add"], at(t, "y_add", e + 1))

            return dict(tensor=tensor, scalar=scalar, vector=vector, gpsimd=gpsimd, load_x=load_x, store_out=store_out, qb5=qb5)

        first = [first_half(k) for k in range(LANES)]
        second = [second_half(k) for k in range(LANES)]
        chunks = [0, W_GROUPS[0] * W_SLOTS, (W_GROUPS[0] + W_GROUPS[1]) * W_SLOTS]
        block = ctx.enter_context(nc.Block())

        @block.sync
        def _(sp):
            sp.sem_inc(s["x_5"], 2)
            for lane in range(LANES):
                sp.sem_inc(s[f"stored{lane}"], 1)
            sp.dma_start(cst[:, :], consts).then_inc(s["const_in"], 16)
            sp.dma_start(bias[:, :], biases).then_inc(s["const_in"], 16)
            sp.dma_start(row_bias[:, :, :], rows.rearrange("p (r n) -> p r n", r=4)).then_inc(s["const_in"], 16)
            for i in range(3):
                sp.dma_start(ffn_stage[i], ffn[i]).then_inc(s["ffn_in"], 16)
            for j in range(W_SLOTS):
                sp.dma_start(w_stage[0][j], weights[:, W_CHUNK[0] * j:W_CHUNK[0] * (j + 1)]).then_inc(s[f"w_in{j}"], 16)
            for lane in first:
                lane["load_x"](sp, -1)
                lane["load_l"](sp, -1)
            for b in range(NB):
                for lane in first:
                    lane["load_n"](sp, -1, b)
                    lane["load_t"](sp, -1, b)
            with sp.Fori(0, TRIPS) as t:
                for b in range(2):
                    for lane in first:
                        lane["load_n"](sp, t, b)
                for b in range(2):
                    for lane in first:
                        lane["load_t"](sp, t, b)
                for lane in first:
                    lane["load_l"](sp, t)
                    lane["load_x"](sp, t)
                for b in range(2, NB):
                    for lane in first:
                        lane["load_n"](sp, t, b)
                for b in range(2, NB):
                    for lane in first:
                        lane["load_t"](sp, t, b)
                for lane in first:
                    lane["store_x"](sp, t)
            for lane in range(LANES):
                sp.wait_ge(s[f"stored{lane}"], 16 * TRIPS + 1)
                for name in ("tp_lo", "np_lo", "cl_lo"):
                    sp.wait_ge(s[name], first[lane]["at"](TRIPS, name, 0))
            sp.sem_inc(s["first_over"], 1)
            for lane in second:
                lane["load_x"](sp, 0)
            with sp.Fori(0, W_GROUPS[1]) as g:
                for j in range(W_SLOTS):
                    sp.wait_ge(s["w_split"], g * W_SLOTS + j + 1)
                    sp.dma_start(w_stage[1][j], weights[:, bass.ds(W_COLS[0] + (g * W_SLOTS + j) * W_CHUNK[1], W_CHUNK[1])]).then_inc(s[f"w_in{j}"], 16)
            with sp.Fori(1, TRIPS) as t:
                for lane in second:
                    lane["load_x"](sp, t)
            for lane in range(LANES):
                sp.wait_ge(s[f"stored{lane}"], 32 * TRIPS + 1)

        @block.gpsimd
        def _(pool):
            pool.memset(ones[:, :], 1.0).then_inc(s["pool_set"], 1)
            pool.memset(neg_half[:, :], -0.5).then_inc(s["pool_set"], 1)
            for lane in range(LANES):
                pool.memset(own[lane]["last_cols"][:, :, :], 0.0).then_inc(s["pool_set"], 1)
                pool.memset(own[lane]["vl"][:, :, :], 0.0).then_inc(s["pool_set"], 1)
                pool.memset(first[lane]["ctx_lp"][:, :, :], 0.0).then_inc(s["pool_set"], 1)
            pool.wait_ge(s["const_in"], 48)
            pool.tensor_copy(ident16[:, :], ident).then_inc(s["pool_set"], 1)
            pool.tensor_copy(identb[:, :], ident).then_inc(s["pool_set"], 1)
            pool.tensor_copy(sel16[:, :], const("sel")).then_inc(s["pool_set"], 1)
            pool.wait_ge(s["pool_set"], POOL_SETUP)
            in_turns(*(lane["gpsimd_before"](pool) for lane in first))
            with pool.Fori(0, TRIPS) as t:
                in_turns(*(lane["gpsimd"](pool, t) for lane in first))
            pool.wait_ge(s["first_over"], 1)
            for lane in second:
                pool.memset(lane["qb5"][:, :, :, :, :, :], 0.0).then_inc(s["pool_set"], 1)
            with pool.Fori(0, TRIPS) as t:
                in_turns(*(lane["gpsimd"](pool, t) for lane in second))

        @block.scalar
        def _(act):
            for j in range(W_SLOTS):
                act.wait_ge(s[f"w_in{j}"], 16)
                act.activation(wp[0][:, 0, W_CHUNK[0] * j:W_CHUNK[0] * (j + 1)], w_stage[0][j], ACT.Copy).then_inc(s["w_hi"], 1)
            act.wait_ge(s["pool_set"], POOL_SETUP)
            in_turns(*(lane["scalar_before"](act) for lane in first))
            with act.Fori(0, TRIPS) as t:
                in_turns(*(lane["scalar"](act, t) for lane in first))
            with act.Fori(0, W_GROUPS[1]) as g:
                for j in range(W_SLOTS):
                    act.wait_ge(s[f"w_in{j}"], g * 16 + 32)
                    act.activation(wp[1][:, 0, bass.ds((g * W_SLOTS + j) * W_CHUNK[1], W_CHUNK[1])], w_stage[1][j], ACT.Copy).then_inc(s["w_hi"], 1)
            act.wait_ge(s["w_split"], chunks[2])
            with act.Fori(0, TRIPS) as t:
                in_turns(*(lane["scalar"](act, t) for lane in second))

        @block.tensor
        def _(pe):
            pe.wait_ge(s["pool_set"], POOL_SETUP)
            pe.wait_ge(s["ffn_abs"], 3)
            pe.matmul(psum[:, 0, 0:3], ones[:, :], stat[:, 0:3], start=True, stop=True).then_inc(s["ffn_sum"], 1)
            pe.wait_ge(s["w_split"], chunks[1])
            pe.wait_ge(s["dve_setup"], SETUP_STEPS)
            with pe.Fori(0, TRIPS) as t:
                in_turns(*(lane["tensor"](pe, t) for lane in first))
            pe.wait_ge(s["w_split"], chunks[2])
            with pe.Fori(0, TRIPS) as t:
                in_turns(*(lane["tensor"](pe, t) for lane in second))

        @block.vector
        def _(dve):
            dve.wait_ge(s["ffn_in"], 48)
            n0 = [0]

            def step(ins):
                n0[0] += 1
                ins.then_inc(s["dve_setup"], 1)
                dve.wait_ge(s["dve_setup"], n0[0])

            for i in range(3):
                dve.tensor_reduce(stat[:, i:i + 1], ffn_stage[i], X, ALU.add, apply_absolute_value=True).then_inc(s["ffn_abs"], 1)
            dve.wait_ge(s["ffn_sum"], 1)
            step(dve.tensor_scalar(ffn_inv[:, :], psum[:, 0, 0:3], 1.0 / (WIDE * D), 1e-5, ALU.mult, ALU.max))
            step(dve.reciprocal(stat[:, 4:7], ffn_inv[:, :]))
            for i in range(3):
                wf = ffn_stage[i]
                step(dve.tensor_scalar(wf, wf, stat[:, 4 + i:5 + i], 2.0, ALU.mult, ALU.min))
                step(dve.tensor_scalar(wf, wf, -2.0, ROUND, ALU.max, ALU.add))
                step(dve.tensor_scalar(wf, wf, ROUND, 1.0, ALU.subtract, ALU.min))
                step(dve.tensor_scalar(ffn_w[:, i, :], wf, -1.0, None, ALU.max))
            dve.wait_ge(s["const_in"], 48)
            step(dve.tensor_copy(bk_pair[:, 0, :], bcol("bk0")))
            step(dve.tensor_tensor(bk_pair[:, 1, :], bcol("bk0"), bk_pair[:, 0, :], ALU.subtract))
            step(dve.tensor_scalar(half_b1[:, :], bcol("b1"), 0.5, None, ALU.mult))
            assert n0[0] == SETUP_STEPS
            for j in range(W_SLOTS):
                dve.wait_ge(s["w_hi"], j + 1)
                cols = slice(W_CHUNK[0] * j, W_CHUNK[0] * (j + 1))
                dve.tensor_tensor(wp[0][:, 1, cols], w_stage[0][j], wp[0][:, 0, cols], ALU.subtract).then_inc(s["w_split"], 1)
            dve.wait_ge(s["w_split"], chunks[1])
            with dve.Fori(0, TRIPS) as t:
                in_turns(*(lane["vector"](dve, t) for lane in first))
            with dve.Fori(0, W_GROUPS[1]) as g:
                for j in range(W_SLOTS):
                    dve.wait_ge(s["w_hi"], g * W_SLOTS + j + chunks[1] + 1)
                    cols = bass.ds((g * W_SLOTS + j) * W_CHUNK[1], W_CHUNK[1])
                    dve.tensor_tensor(wp[1][:, 1, cols], w_stage[1][j], wp[1][:, 0, cols], ALU.subtract).then_inc(s["w_split"], 1)
            dve.wait_ge(s["w_split"], chunks[2])
            dve.wait_ge(s["pool_set"], POOL_SETUP + LANES)
            with dve.Fori(0, TRIPS) as t:
                in_turns(*(lane["vector"](dve, t) for lane in second))


def _stacked(m, k):
    import numpy as np

    return np.ascontiguousarray(m.reshape(k, P, -1).transpose(1, 0, 2).reshape(P, -1))


def _columns(v):
    return v.reshape(-1, P).T


def _constants():
    import numpy as np

    p = np.arange(P)
    parts = {
        "ident": np.eye(P), "sel": p[:, None] % SEQ == np.arange(SEQ)[None], "causal": np.where(np.arange(SEQ)[None] <= p[:, None] % SEQ, 0.0, FAR),
        "mask8": p[:, None] // 16 == np.arange(8)[None], "quad": p[:, None] // SEQ == np.arange(4)[None],
        "half": p[:, None] // 64 == np.arange(2)[None], "eye4": np.tile(np.eye(4).reshape(1, 16), (P, 1)),
        "iota8": np.tile(np.arange(8)[None], (P, 1)),
    }
    return np.concatenate([parts[n] for n, _ in _CONSTS], axis=1).astype(np.float32)


def kernel(**inputs):
    import numpy as np
    from concourse import bacc
    from concourse.bass_utils import run_bass_kernel_spmd

    a = {k: np.asarray(v) for k, v in inputs.items()}
    c = a["ctx_1024"]
    qkv_b, h = a["L0_attn_qkv_b"], a["L1_attn_W_Q"].shape[0]
    flat = {n: a["L1_attn_W_" + n].reshape(WIDE, D).T for n in "QKV"}
    experts = {n: np.concatenate([_stacked(a["L1_ffn_" + n][e].T, C) for e in range(EXPERTS)], axis=1) for n in ("w1", "w2", "w3")}

    def rolled(m):
        return np.roll(m, -LANES, axis=0)

    packed = {
        "q0": _stacked(a["L0_xattn_Wq"], C), "k0t": _stacked(a["L0_xattn_Wk"].T, C), "v0": _stacked(a["L0_xattn_Wv"], C),
        "qkv0": _stacked(a["L0_attn_qkv_w"].T, C), "o0": _stacked(a["L0_attn_o_w"].T, C),
        "xq": _stacked(a["L1_xattn_w_q"].T, C), "xkv": _stacked(a["L1_xattn_w_kv"].T, C), "xo": _stacked(a["L1_xattn_w_out"].T, C),
        "aq": _stacked(flat["Q"], C), "ak": _stacked(flat["K"], C), "av": _stacked(flat["V"], C),
        "ao": _stacked(a["L1_attn_W_O"].transpose(0, 2, 1).reshape(WIDE, D), WIDE // P),
        "gate": _stacked(a["L1_ffn_gate_w"].T, C), **experts,
        "sw1": _stacked(a["L1_ffn_sw1"].T, C), "sw2": _stacked(a["L1_ffn_sw2"].T, C), "sw3": _stacked(a["L1_ffn_sw3"].T, SHARED // P),
    }
    bq, bk = _columns(a["L1_attn_b_Q"].reshape(-1)), _columns(a["L1_attn_b_K"].reshape(-1))
    columns = {
        "bq0": _columns(a["L0_xattn_bq"]), "bk0": _columns(a["L0_xattn_bk"]),
        "bqk0": _columns(qkv_b[0:2 * D]), "bv0": _columns(qkv_b[2 * D:3 * D]),
        "bqk1": np.concatenate([m[:, 2 * g:2 * g + 2] for g in range(GROUPS) for m in (bq, bk)], axis=1),
        "bv1": _columns(a["L1_attn_b_V"].reshape(-1)),
        **{n: _columns(a["L1_ffn_" + n].reshape(-1)) for n in ("b1", "b2", "b3")},
    }
    rows = np.stack([a["L0_xattn_bv"], a["L0_attn_o_b"], a["L1_xattn_b_out"], a["L1_attn_b_O"]])
    arrays = {
        "x_tok": rolled(a["x"].reshape(TILES, P, D)),
        "ctx_t": rolled(c.reshape(TILES, NB, KEYS, C, P).transpose(0, 1, 4, 3, 2).reshape(TILES, NB, P, C * KEYS)),
        "ctx_n": rolled(c[:, 0:2 * P].reshape(TILES, NB, 2, P, D).transpose(0, 1, 3, 2, 4).reshape(TILES, NB, P, 2 * D)),
        "ctx_l": rolled(c[:, KEYS - 1].reshape(TILES, NB, D)),
        "weights": np.concatenate([packed[n] for half in _SIZES for n, _ in half], axis=1),
        "ffn": np.stack([_stacked(a["L0_ffn_w_gate"].T, C), _stacked(a["L0_ffn_w_up"].T, C), _stacked(a["L0_ffn_w_down"].T, 8)]),
        "consts": _constants(),
        "biases": np.concatenate([columns[n] for n, _ in _BIASES], axis=1),
        "rows": np.tile(rows.reshape(1, -1), (P, 1)),
    }
    arrays = {"in_" + k: np.ascontiguousarray(v) for k, v in arrays.items()}
    nc = bacc.Bacc("TRN2", target_bir_lowering=False, num_devices=1)
    args = [nc.dram_tensor(k, v.shape, mybir.dt.from_np(v.dtype), kind="ExternalInput").ap() for k, v in arrays.items()]
    mid = nc.dram_tensor("x_mid", (TILES, P, D), F32, kind="Internal").ap()
    out = nc.dram_tensor("y_tok", (TILES, P, D), F32, kind="ExternalOutput").ap()
    build(nc, *args, mid, out)
    r = run_bass_kernel_spmd(nc, [arrays], core_ids=[0])
    return r.results[0]["y_tok"].reshape(SEQS, SEQ, D)
```

```python
from contextlib import ExitStack

import concourse.bass as bass
from concourse import mybir

F32 = mybir.dt.float32
F16 = mybir.dt.float16
BF16 = mybir.dt.bfloat16
U32 = mybir.dt.uint32
ALU = mybir.AluOpType
ACT = mybir.ActivationFunctionType
X = mybir.AxisListType.X

P = 128
D = 256
C = D // P
SEQ = 32
SEQS = 128
KEYS = 257
NB = P // SEQ
TILES = SEQS // NB
LANES = 2
TRIPS = TILES // LANES
UNITS = 2 * NB
HEADS = 16
GROUPS = HEADS // 4
WIDE = 1024
EXPERTS = 8
SHARED = 512
EPS = 1e-5
ROUND = 1.5 * 2.0**23
FAR = -1.0e30

_SIZES = [
    [("q0t", C * D), ("k0t", C * D), ("v0", C * D), ("qkv0", C * 3 * D), ("o0", C * D),
     ("xq", C * D), ("xkv", C * 2 * D), ("xo", C * D)],
    [("aq", C * WIDE), ("ak", C * WIDE), ("av", C * WIDE), ("ao", WIDE // P * D),
     ("gate", C * EXPERTS), ("w1", EXPERTS * C * D), ("w2", EXPERTS * C * D), ("w3", EXPERTS * C * D),
     ("sw1", C * SHARED), ("sw2", C * SHARED), ("sw3", SHARED // P * D)],
]
W_AT, W_COLS = [{}, {}], [0, 0]
for _half in range(2):
    for _name, _n in _SIZES[_half]:
        W_AT[_half][_name] = W_COLS[_half]
        W_COLS[_half] += _n
W_SLOTS = 4
W_CHUNK = [1408, 1473]
W_GROUPS = [W_COLS[h] // (W_CHUNK[h] * W_SLOTS) for h in range(2)]
assert all(W_GROUPS[h] * W_CHUNK[h] * W_SLOTS == W_COLS[h] for h in range(2))

FRONT = 9228
LANE_1 = FRONT + 2 * C * KEYS + 4 * D + D + 2 * NB * D + 2 * C * NB * KEYS // 2 + D
LANE_2 = 6144 + 1024 + 1024
MEM = max(LANES * LANE_1 + W_COLS[0] + 3072, W_COLS[1] + LANES * LANE_2)

_CONSTS = [("ident", P), ("sel", SEQ), ("causal", SEQ), ("mask8", 8), ("quad", 4), ("half", 2), ("eye4", 16), ("iota8", 8)]
C_AT, C_COLS = {}, 0
for _name, _n in _CONSTS:
    C_AT[_name] = (C_COLS, C_COLS + _n)
    C_COLS += _n
_BIASES = [("bq0", 2), ("bk0", 2), ("bqk0", 4), ("bv0", 2), ("bqk1", 16), ("bv1", 8), ("b1", 16), ("b2", 16), ("b3", 16)]
B_AT, B_COLS = {}, 0
for _name, _n in _BIASES:
    B_AT[_name] = (B_COLS, B_COLS + _n)
    B_COLS += _n

SETUP_STEPS = 19
POOL_SETUP = 5 + 3 * LANES

FIRST = {
    "ln_var": 4, "ln_rstd": 4, "xn": 3, "biased": 3, "xt_ps": 3, "xt_hi": 3, "xt_lo": 3,
    "tp_hi": 4, "tp_lo": 4, "np_hi": 4, "np_lo": 4, "cl_hi": 1, "cl_lo": 1,
    "q0_ps": 1, "q0_f": 1, "q0_hi": 1, "q0_lo": 1, "qbk_ps": 1, "s1_ps": 1,
    "exp_bias": 1, "exps": 1, "p1_last": 1, "pt1_ps": 1, "pt1_hi": 1, "pt1_lo": 1, "a1_ps": 1, "a1_hi": 1, "a1_lo": 1,
    "y1_ps": 1, "x_1": 1, "qk_ps": 1, "qk_f": 1, "qk_hi": 1, "v_ps": 1, "v_hi": 1, "qbd2": 1, "qk2_lo": 1, "qbd2_act": 3, "self_v": 1,
    "self_s": 1, "self_shift": 1, "self_p": 1, "self_pt": 1, "self_pt_hi": 1, "pt2_lo": 1, "o2g_ps": 1, "o_f": 4, "o_hi": 2, "o_lo_v": 1,
    "o_lo": 1, "o2_ps": 1, "o2_hi": 2, "o2_lo": 2, "self_y": 1, "xq": 1, "xq_ps": 1, "xqt": 1, "gate_ps": 2,
    "up_ps": 2, "tanh": 2, "hq": 1, "hq_ps": 1, "hqt": 1, "ffn_y": 1, "q4_ps": 1, "q4_hi": 1, "q4_lo": 1, "qbd4": 4,
    "vl_ps": 1, "vl_hi": 1, "vl_lo": 1, "k4_ps": 4, "k4_hi": 4, "k4_lo": 4, "v4_ps": 4, "v4_hi": 4, "v4_lo": 4,
    "s4_ps": 8, "s4_bias": 8, "p4": 16, "p4_last": 8, "pt4_ps": 8, "pt4_hi": 8, "pt4_lo": 8, "o4_ps": 8, "om4_f": 8,
    "om4_hi": 8, "om4_lo": 8, "sel_ps": 1, "sel_hi": 1, "sel_lo": 1, "y4_ps": 1, "x_4": 1, "dve_order": 81,
}
SECOND = {
    "ln_var": 2, "ln_rstd": 2, "xn": 2, "biased": 1, "xt_ps": 2, "xt_hi": 2, "xt_lo": 2, "v_ps": 1, "v_hi": 1, "self_v": 1,
    "qk_ps": 4, "qk_f": 4, "qk_hi": 4, "qk5_lo": 4, "qb5": 4, "self_s": 4, "self_shift": 1, "self_p": 1, "p5_norm": 1,
    "self_pt": 1, "self_pt_hi": 1, "ptb": 1, "pt5_lo": 1, "ptb_act": 1, "o5_ps": 4, "o_f": 8, "o_hi": 2, "o_lo_v": 1, "o_lo": 1, "self_y": 2, "x_5": 1, "gate_ps": 1,
    "exp_bias": 1, "exps": 1, "gate_p": 1, "sh_ps": 1, "tanh": 1, "sh_f": 1, "sh_hi": 1, "sh_lo": 1, "wb_ps": 1,
    "mb_ps": 1, "wb": 2, "mb": 1, "z_ps": 1, "y_0": 1, "e13_ps": 8, "u4": 8, "th_e": 32, "he_f": 8, "he_hi": 8, "he_lo": 8,
    "e2_ps": 8, "x2": 16, "a3": 16, "prod": 8, "y_add": 8, "ffn_y": 1, "x_final": 1, "dve_order": 35,
}
EARLY = ("tp_hi", "tp_lo", "np_hi", "np_lo", "cl_hi", "cl_lo")
AHEAD = ("x_5",)
LANE_SIGNALS = ("x_in", "stored", "l_in", "n_in0_", "n_in1_", "t_in0_", "t_in1_")
SETUP_SIGNALS = ["const_in", "ffn_in", "pool_set", "ffn_abs", "ffn_sum", "dve_setup", "w_hi", "w_split", "first_over", "wqk_ps", "wqk"] + [
    f"w_in{j}" for j in range(W_SLOTS)] + [f"{n}{lane}" for n in LANE_SIGNALS for lane in range(LANES)]


def counter(table, done, lane):
    def at(trip, name, n):
        ahead = (2 if name in AHEAD else 0) + (LANES * table[name] if name in EARLY else 0)
        return trip * (LANES * table[name]) + (LANES * n - 1 + lane + ahead + LANES * TRIPS * done.get(name, 0))
    return at


def in_turns(first, second):
    for _ in first:
        next(second)
    for _ in second:
        pass


def carve(memory, at, words, dt=F32):
    a = memory[:, at:at + words]
    return a if dt == F32 else a.bitcast(dt)


def build(nc, x_in, ctx_t, ctx_n, ctx_l, weights, ffn, consts, biases, rows, mid, out):
    ctx = ExitStack()
    with ctx:
        def sb(name, shape, dt):
            return ctx.enter_context(nc.sbuf_tensor(name, shape, dt))

        def sem(name):
            return ctx.enter_context(nc.semaphore(name))

        cst = sb("cst", [P, C_COLS], F32)
        bias = sb("bias", [P, B_COLS], F32)
        row_bias = sb("row_bias", [P, 4, D], F32)
        ident16 = sb("ident16", [P, P], F16)
        identb = sb("identb", [P, P], BF16)
        sel16 = sb("sel16", [P, SEQ], F16)
        ones = sb("ones", [P, P], F32)
        bq_pair = sb("bq_pair", [P, 2, C], F16)
        bk_pair = sb("bk_pair", [P, 2, C], F16)
        qk_bias = sb("qk_bias", [P, 5], F32)
        wbk_pair = sb("wbk_pair", [P, 2, C], F16)
        half_b1 = sb("half_b1", [P, EXPERTS * C], F32)
        ffn_inv = sb("ffn_inv", [P, 3], F32)
        stat = sb("stat", [P, 16], F32)
        neg_half = sb("neg_half", [P, 1], F32)
        mem = sb("mem", [P, MEM], F32)

        def pairs(at, cols):
            return carve(mem, at, cols, F16).rearrange("p (l n) -> p l n", l=2)

        wp = [pairs(LANES * LANE_1, W_COLS[0]), pairs(0, W_COLS[1])]
        ffn_w = carve(mem, LANES * LANE_1 + W_COLS[0], 3072, BF16).rearrange("p (i n) -> p i n", i=3)
        ffn_stage = [carve(mem, 2048 * i, 2048) for i in range(3)]
        w_stage = [[carve(mem, (LANE_1, W_COLS[1])[h] + W_CHUNK[h] * j, W_CHUNK[h]) for j in range(W_SLOTS)] for h in range(2)]

        def const(name):
            a, b = C_AT[name]
            return cst[:, a:b]

        def bcol(name):
            a, b = B_AT[name]
            return bias[:, a:b]

        def w(name, part, k, n, first=0):
            h = 0 if name in W_AT[0] else 1
            a = W_AT[h][name] + first
            return wp[h][:, part, a:a + k * n].rearrange("p (k n) -> p k n", k=k)

        ident = const("ident")
        causal, mask8, quad, half = const("causal"), const("mask8"), const("quad"), const("half")
        eye4 = const("eye4").rearrange("p (b j) -> p b j", b=NB)
        psum = ctx.enter_context(nc.psum_tensor("ps", [P, 8, 512], F32))

        def lane_buffers(k):
            def own(name, shape, dt):
                return sb(f"{name}_{k}", shape, dt)

            return dict(
                x0=own("x0", [P, D], F32), x=own("x", [P, D], F32), x_out=own("x_out", [P, D], F32), xn=own("xn", [P, D], F32),
                xt=own("xt", [P, 2, C, P], F16), bn=own("bn", [P, 6], F32), mv=own("mv", [P, 2], F32), var_eps=own("var_eps", [P, 1], F32),
                rstd=own("rstd", [P, 1], F32), qk_f=own("qk_f", [P, 4, P], F32), qk=own("qk", [P, 2, 4, P], F16),
                op=own("op", [P, 2, C, P], F16), last_cols=own("last_cols", [P, GROUPS, P], F32), vl=own("vl", [P, 2, D], F16),
                small=own("small", [P, 96], F32), idx=own("idx", [P, 8], U32), waited=own("waited", [P, 1], F32),
                th_rm=own("th_rm", [P, 16, 4], F32), gate_p=own("gate_p", [P, 3, EXPERTS], F16))

        own = [lane_buffers(k) for k in range(LANES)]

        s = {}
        for n in SETUP_SIGNALS + list(dict.fromkeys([*FIRST, *SECOND])):
            s[n] = sem(n)

        def product(pe, dst, pairs, start=True, stop=True):
            n = len(pairs)
            last = None
            for i, ((lh, ll), (rh, rl)) in enumerate(pairs):
                for j, (a, b) in enumerate([(lh, rh), (lh, rl), (ll, rh)]):
                    last = pe.matmul(dst, a, b, start=start and i == 0 and j == 0, stop=stop and i == n - 1 and j == 2)
            return last

        def feature_major(pe, dst, name, n, act_pair, chunks, first=0, k=C):
            for i, oc in enumerate(chunks):
                last = product(pe, dst[:, i * P:(i + 1) * P], [
                    ((w(name, 0, k, n, first)[:, kc, oc * P:(oc + 1) * P], w(name, 1, k, n, first)[:, kc, oc * P:(oc + 1) * P]),
                     (act_pair[:, 0, kc], act_pair[:, 1, kc])) for kc in range(k)])
            return last

        def token_major(pe, dst, name, n, act_pair, lo, hi, k=C):
            return product(pe, dst, [
                ((act_pair[:, 0, kc], act_pair[:, 1, kc]), (w(name, 0, k, n)[:, kc, lo:hi], w(name, 1, k, n)[:, kc, lo:hi]))
                for kc in range(k)])

        def first_half(lane):
            me = own[lane]
            x0, x, xn, xt, bn, mv, var_eps, rstd = me["x0"], me["x"], me["xn"], me["xt"], me["bn"], me["mv"], me["var_eps"], me["rstd"]
            qk_f, qk, op, last_cols, vl, small, waited, th_rm = me["qk_f"], me["qk"], me["op"], me["last_cols"], me["vl"], me["small"], me["waited"], me["th_rm"]
            at = counter(FIRST, {}, lane)
            ps = psum[:, 4 * lane:4 * lane + 4, :]
            arena = mem[:, LANE_1 * lane:LANE_1 * (lane + 1)]

            stage_t = carve(arena, FRONT, 2 * C * KEYS).rearrange("p (s n) -> p s n", s=2)
            stage_n = carve(arena, FRONT + 2 * C * KEYS, 4 * D).rearrange("p (s n) -> p s n", s=2)
            after = FRONT + 2 * C * KEYS + 4 * D
            stage_l = arena[0:NB, after:after + D]
            ctx_np = carve(arena, after + D, 2 * NB * D, F16).rearrange("p (l b m d) -> p l b m d", l=2, b=NB, m=2)
            after += D + 2 * NB * D
            ctx_tp = carve(arena, after, C * NB * KEYS, F16).rearrange("p (l c b m) -> p l c b m", l=2, c=C, b=NB)
            ctx_lp = carve(arena, after + C * NB * KEYS, D, F16).rearrange("p (l n) -> p l n", l=2)
            qbd = carve(arena, 0, 2048, F16).rearrange("p (l c b h q) -> p l c b h q", l=2, c=C, b=NB, h=8)
            probs = carve(arena, 2048, 1028)
            pt1 = carve(arena, 3076, 384, F16).rearrange("p (l n) -> p l n", l=2)
            s2 = carve(arena, 3584, 512)
            pt2 = carve(arena, 4096, 512, F16).rearrange("p (l g n) -> p l g n", l=2, g=GROUPS)
            vblk = carve(arena, 4608, 1024, F16).rearrange("p (l g b d) -> p l g b d", l=2, g=GROUPS, b=NB)
            v2 = carve(arena, 5632, 256, F16).rearrange("p (l n) -> p l n", l=2)
            om_f = carve(arena, 6144, 1024)
            om = carve(arena, 7168, 1024, F16).rearrange("p (l b n) -> p l b n", l=2, b=NB)
            th3 = carve(arena, 2048, 1024)
            r3 = carve(arena, 3072, 1024)
            rq3 = carve(arena, 4096, 1024)
            hq = carve(arena, 5120, 512, BF16)
            hqt = carve(arena, 5632, 512, BF16).rearrange("p (k n) -> p k n", k=8)
            xq_f = carve(arena, 6144, 256)
            xq = carve(arena, 6400, 128, BF16)
            xqt = carve(arena, 6528, 128, BF16).rearrange("p (c n) -> p c n", c=C)
            kp = carve(arena, 3076, 2056, F16).rearrange("p (l c b m) -> p l c b m", l=2, c=C, b=NB)
            vp = carve(arena, 5132, 2048, F16).rearrange("p (l b m n) -> p l b m n", l=2, b=NB, m=2)
            pt4 = carve(arena, 7180, 1536, F16).rearrange("p (s l n) -> p s l n", s=2, l=2)
            om4_f = carve(arena, 8716, 256).rearrange("p (s n) -> p s n", s=2)
            om4 = carve(arena, 8972, 256, F16).rearrange("p (s l n) -> p s l n", s=2, l=2)

            def tp_hi(act, trip, b):
                act.wait_ge(s[f"t_in{b % 2}_{lane}"], trip * 32 + 32 + 16 * (b // 2) + 16)
                if not isinstance(trip, int):
                    act.wait_ge(s["v4_ps"], at(trip, "v4_ps", b + 1))
                act.activation(ctx_tp[:, 0, :, b, :], stage_t[:, b % 2, :].rearrange("p (c m) -> p c m", c=C), ACT.Copy).then_inc(s["tp_hi"], 1)
                yield

            def tp_lo(pool, trip, b):
                pool.wait_ge(s["tp_hi"], at(trip, "tp_hi", b + 1))
                pool.tensor_tensor(ctx_tp[:, 1, :, b, :], stage_t[:, b % 2, :].rearrange("p (c m) -> p c m", c=C), ctx_tp[:, 0, :, b, :],
                                   ALU.subtract).then_inc(s["tp_lo"], 1)
                yield

            def np_hi(act, trip, b):
                act.wait_ge(s[f"n_in{b % 2}_{lane}"], trip * 32 + 32 + 16 * (b // 2) + 16)
                if not isinstance(trip, int) and b == 0:
                    act.wait_ge(s["a1_ps"], at(trip, "a1_ps", 1))
                act.activation(ctx_np[:, 0, b], stage_n[:, b % 2, :].rearrange("p (m d) -> p m d", m=2), ACT.Copy).then_inc(s["np_hi"], 1)
                yield

            def np_lo(pool, trip, b):
                pool.wait_ge(s["np_hi"], at(trip, "np_hi", b + 1))
                pool.tensor_tensor(ctx_np[:, 1, b], stage_n[:, b % 2, :].rearrange("p (m d) -> p m d", m=2), ctx_np[:, 0, b],
                                   ALU.subtract).then_inc(s["np_lo"], 1)
                yield

            def last_hi(act, trip):
                act.wait_ge(s[f"l_in{lane}"], trip * 16 + 32)
                act.activation(ctx_lp[0:NB, 0, :], stage_l, ACT.Copy).then_inc(s["cl_hi"], 1)
                yield

            def last_lo(pool, trip):
                pool.wait_ge(s["cl_hi"], at(trip, "cl_hi", 1))
                pool.tensor_tensor(ctx_lp[0:NB, 1, :], stage_l, ctx_lp[0:NB, 0, :], ALU.subtract).then_inc(s["cl_lo"], 1)
                yield

            def scalar_before(act):
                for b in range(NB):
                    yield from np_hi(act, -1, b)
                    yield from tp_hi(act, -1, b)
                yield from last_hi(act, -1)

            def gpsimd_before(pool):
                for b in range(NB):
                    yield from np_lo(pool, -1, b)
                    yield from tp_lo(pool, -1, b)
                yield from last_lo(pool, -1)

            def load_n(sp, trip, b):
                if b >= 2 or not isinstance(trip, int):
                    sp.wait_ge(s["np_lo"], at(trip, "np_lo", b - 1))
                source = (TRIPS - 1 if isinstance(trip, int) else trip) * LANES + lane
                sp.dma_start(stage_n[:, b % 2, :], ctx_n[bass.ds(source, 1), b].rearrange("t p n -> (t p) n")).then_inc(s[f"n_in{b % 2}_{lane}"], 16)

            def load_t(sp, trip, b):
                if b >= 2 or not isinstance(trip, int):
                    sp.wait_ge(s["tp_lo"], at(trip, "tp_lo", b - 1))
                source = (TRIPS - 1 if isinstance(trip, int) else trip) * LANES + lane
                sp.dma_start(stage_t[:, b % 2, :], ctx_t[bass.ds(source, 1), b].rearrange("t p n -> (t p) n")).then_inc(s[f"t_in{b % 2}_{lane}"], 16)

            def load_l(sp, trip):
                if not isinstance(trip, int):
                    sp.wait_ge(s["cl_lo"], at(trip, "cl_lo", 0))
                source = (TRIPS - 1 if isinstance(trip, int) else trip) * LANES + lane
                sp.dma_start(stage_l, ctx_l[bass.ds(source, 1)].rearrange("t p d -> (t p) d")).then_inc(s[f"l_in{lane}"], 16)

            def load_x(sp, trip):
                if not isinstance(trip, int):
                    sp.wait_ge(s["x_1"], at(trip, "x_1", 1))
                source = (TRIPS - 1 if isinstance(trip, int) else trip) * LANES + lane
                sp.dma_start(x0[:, :], x_in[bass.ds(source, 1)].rearrange("t p d -> (t p) d")).then_inc(s[f"x_in{lane}"], 16)

            def store_x(sp, trip):
                sp.wait_ge(s["x_4"], at(trip, "x_4", 1))
                sp.dma_start(mid[bass.ds(trip * LANES + lane, 1)].rearrange("t p d -> (t p) d"), x[:, :]).then_inc(s[f"stored{lane}"], 16)

            def tensor(pe, t):
                def need(name, n=1):
                    pe.wait_ge(s[name], at(t, name, n))

                def transpose_x(n):
                    need("xn", n + 1)
                    for c in range(C):
                        last = pe.transpose(ps[:, 0, c * P:(c + 1) * P], xn[:, c * P:(c + 1) * P], ident)
                    last.then_inc(s["xt_ps"], 1)
                    yield
                    need("xt_lo", n + 1)

                yield from transpose_x(0)
                feature_major(pe, ps[:, 1], "q0t", D, xt, range(C)).then_inc(s["q0_ps"], 1)
                yield
                product(pe, ps[:, 3, 0:1], [((xt[:, 0, c], xt[:, 1, c]), (wbk_pair[:, 0, c:c + 1], wbk_pair[:, 1, c:c + 1]))
                                        for c in range(C)]).then_inc(s["qbk_ps"], 1)
                yield
                need("q0_lo")
                need("tp_lo", 0)
                for c in range(C):
                    for a, r in ((0, 0), (0, 1), (1, 0)):
                        for b in range(NB):
                            last = pe.matmul(ps[SEQ * b:SEQ * (b + 1), 0, 0:KEYS], qk[:, a, c, SEQ * b:SEQ * (b + 1)], ctx_tp[:, r, c, b, :],
                                             start=(c == 0 and a == 0 and r == 0), stop=(c == 1 and a == 1))
                last.then_inc(s["s1_ps"], 1)
                yield
                need("p1_last")
                for m in range(3):
                    src = probs[:, m * P:(m + 1) * P] if m < 2 else last_cols[:, 0, :]
                    last = pe.transpose(ps[:, 1, m * P:(m + 1) * P], src, ident)
                last.then_inc(s["pt1_ps"], 1)
                yield
                need("pt1_lo")
                need("cl_lo", 0)
                need("np_lo", 0)
                for c in range(C):
                    cols = slice(c * P, (c + 1) * P)
                    product(pe, ps[:, 2, cols], [((ctx_lp[:, 0, cols], ctx_lp[:, 1, cols]), (pt1[:, 0, 256:384], pt1[:, 1, 256:384]))], stop=False)
                    for b in range(NB):
                        for m in range(2):
                            toks = slice(m * P + SEQ * b, m * P + SEQ * (b + 1))
                            last = product(pe, ps[:, 2, c * P + SEQ * b:c * P + SEQ * (b + 1)],
                                           [((ctx_np[:, 0, b, m, cols], ctx_np[:, 1, b, m, cols]), (pt1[:, 0, toks], pt1[:, 1, toks]))],
                                           start=False, stop=(b == NB - 1 and m == 1))
                last.then_inc(s["a1_ps"], 1)
                yield
                need("a1_lo")
                token_major(pe, ps[:, 3, 0:D], "v0", D, op, 0, D).then_inc(s["y1_ps"], 1)
                yield

                yield from transpose_x(1)
                feature_major(pe, ps[:, 1], "qkv0", 3 * D, xt, range(4)).then_inc(s["qk_ps"], 1)
                yield
                token_major(pe, ps[:, 2, 0:D], "qkv0", 3 * D, xt, 2 * D, 3 * D).then_inc(s["v_ps"], 1)
                yield
                need("qbd2")
                need("qbd2_act", 3)
                for g in range(GROUPS):
                    c, h = g // 2, 4 * (g % 2)
                    for b in range(NB):
                        q = [qbd[:, a, c, b, h:h + 4, :].rearrange("p h q -> p (h q)") for a in range(2)]
                        k = [qk[:, a, 2 + c, SEQ * b:SEQ * (b + 1)] for a in range(2)]
                        last = product(pe, ps[:, 3, g * P + SEQ * b:g * P + SEQ * (b + 1)], [((q[0], q[1]), (k[0], k[1]))])
                last.then_inc(s["self_s"], 1)
                yield
                need("self_p")
                for g in range(GROUPS):
                    last = pe.transpose(ps[:, 0, g * P:(g + 1) * P], probs[:, g * P:(g + 1) * P], ident)
                last.then_inc(s["self_pt"], 1)
                yield
                need("self_v")
                need("pt2_lo")
                for g in range(GROUPS):
                    v = [vblk[:, a, g].rearrange("p b d -> p (b d)") for a in range(2)]
                    last = product(pe, ps[:, 1 + g // 2, (g % 2) * D:(g % 2 + 1) * D], [((pt2[:, 0, g], pt2[:, 1, g]), (v[0], v[1]))])
                last.then_inc(s["o2g_ps"], 1)
                yield
                need("o_lo")
                need("o_lo_v")
                for c in range(C):
                    for b in range(NB):
                        for a in range(2):
                            last = pe.matmul(ps[:, 3, c * P + SEQ * b:c * P + SEQ * (b + 1)], om[:, a, b, c * P:(c + 1) * P], sel16[:, :],
                                             start=(a == 0), stop=(a == 1))
                last.then_inc(s["o2_ps"], 1)
                yield
                need("o2_lo", 2)
                token_major(pe, ps[:, 0, 0:D], "o0", D, op, 0, D).then_inc(s["self_y"], 1)
                yield

                need("xq")
                for c in range(C):
                    last = pe.transpose(ps[:, 3, c * 64:(c + 1) * 64].bitcast(BF16), xq[:, c * P:(c + 1) * P], identb[:, :])
                last.then_inc(s["xq_ps"], 1)
                yield
                need("xqt")
                for j in range(4):
                    name = "gate_ps" if j < 2 else "up_ps"
                    wt = ffn_w[:, j // 2, :].rearrange("p (k n) -> p k n", k=C)
                    for kc in range(C):
                        last = pe.matmul(ps[:, j, :], xqt[:, kc], wt[:, kc, 512 * (j % 2):512 * (j % 2 + 1)], start=(kc == 0), stop=(kc == 1))
                    last.then_inc(s[name], 1)
                    yield
                need("hq")
                for k in range(8):
                    last = pe.transpose(ps[:, 0, k * 64:(k + 1) * 64].bitcast(BF16), hq[:, k * P:(k + 1) * P], identb[:, :])
                last.then_inc(s["hq_ps"], 1)
                yield
                need("hqt")
                wt = ffn_w[:, 2, :].rearrange("p (k n) -> p k n", k=8)
                for k in range(8):
                    last = pe.matmul(ps[:, 1, 0:D], hqt[:, k], wt[:, k, :], start=(k == 0), stop=(k == 7))
                last.then_inc(s["ffn_y"], 1)
                yield

                def keys_to_values(b):
                    if b >= 2:
                        need("v4_lo", b - 1)
                    for m in range(2):
                        last = product(pe, ps[:, 2 + b % 2, m * D:(m + 1) * D], [
                            ((ctx_tp[:, 0, kc, b, m * P:(m + 1) * P], ctx_tp[:, 1, kc, b, m * P:(m + 1) * P]),
                             (w("xkv", 0, C, 2 * D)[:, kc, D:2 * D], w("xkv", 1, C, 2 * D)[:, kc, D:2 * D])) for kc in range(C)])
                    last.then_inc(s["v4_ps"], 1)
                    yield

                yield from keys_to_values(0)
                yield from transpose_x(2)
                feature_major(pe, ps[:, 3], "xq", D, xt, range(C)).then_inc(s["q4_ps"], 1)
                yield
                product(pe, ps[0:NB, 1, 0:D], [((ctx_tp[:, 0, c, :, KEYS - 1], ctx_tp[:, 1, c, :, KEYS - 1]),
                                            (w("xkv", 0, C, 2 * D)[:, c, D:2 * D], w("xkv", 1, C, 2 * D)[:, c, D:2 * D])) for c in range(C)]
                        ).then_inc(s["vl_ps"], 1)
                yield
                need("q4_lo")

                def keys(b):
                    if b >= 1:
                        need("k4_lo", b)
                    for oc in range(C):
                        last = product(pe, ps[:, oc, 0:KEYS], [
                            ((w("xkv", 0, C, 2 * D)[:, kc, oc * P:(oc + 1) * P], w("xkv", 1, C, 2 * D)[:, kc, oc * P:(oc + 1) * P]),
                             (ctx_tp[:, 0, kc, b, :], ctx_tp[:, 1, kc, b, :])) for kc in range(C)])
                    last.then_inc(s["k4_ps"], 1)
                    yield

                def scores(u):
                    b, c = u // 2, u % 2
                    if u >= 2:
                        need("om4_f", u - 1)
                    elif u == 0:
                        need("k4_lo", NB)
                        need("qbd4", NB)
                    else:
                        need("v4_lo", NB)
                    for i in range(2):
                        q = [qbd[:, a, c, b, 4 * i:4 * i + 4, :].rearrange("p h q -> p (h q)") for a in range(2)]
                        last = product(pe, ps[:, 2 * c + i, 0:KEYS], [((q[0], q[1]), (kp[:, 0, c, b], kp[:, 1, c, b]))])
                    last.then_inc(s["s4_ps"], 1)
                    yield

                def turn_probs(u):
                    c = u % 2
                    need("p4_last", u + 1)
                    for i in range(2):
                        for m in range(3):
                            g = 2 * c + i
                            src = probs[:, KEYS * g + m * P:KEYS * g + (m + 1) * P] if m < 2 else last_cols[:, g, :]
                            last = pe.transpose(ps[:, g, m * P:(m + 1) * P], src, ident)
                    if u >= 2:
                        last = select(u - 2)
                    last.then_inc(s["pt4_ps"], 1)
                    yield

                def values(u):
                    b, c = u // 2, u % 2
                    need("pt4_lo", u + 1)
                    for i in range(2):
                        cols = slice(64 * (2 * c + i), 64 * (2 * c + i + 1))
                        pt = [[pt4[:, c, a, 384 * i + m * P:384 * i + (m + 1) * P] for a in range(2)] for m in range(3)]
                        last = product(pe, ps[:, 2 * c, 384 + 64 * i:448 + 64 * i], [
                            ((pt[m][0], pt[m][1]), (vp[:, 0, b, m, cols], vp[:, 1, b, m, cols])) if m < 2 else
                            ((pt[m][0], pt[m][1]), (vl[:, 0, cols], vl[:, 1, cols])) for m in range(3)])
                    last.then_inc(s["o4_ps"], 1)
                    yield

                def select(u):
                    b, c = u // 2, u % 2
                    need("om4_lo", u + 1)
                    for a in range(2):
                        last = pe.matmul(ps[:, 2 * c + 1, 384 + SEQ * b:384 + SEQ * (b + 1)], om4[:, c, a, :], sel16[:, :],
                                         start=(a == 0), stop=(a == 1))
                    return last

                yield from keys_to_values(1)
                for b in range(NB):
                    if b == 0:
                        need("vl_lo")
                    yield from keys(b)
                    if b + 2 < NB:
                        yield from keys_to_values(b + 2)
                yield from scores(0)
                for u in range(UNITS):
                    yield from turn_probs(u)
                    if u + 1 < UNITS:
                        yield from scores(u + 1)
                    yield from values(u)
                select(UNITS - 2)
                select(UNITS - 1).then_inc(s["sel_ps"], 1)
                yield
                need("sel_lo")
                token_major(pe, ps[:, 0, 0:D], "xo", D, op, 0, D).then_inc(s["y4_ps"], 1)
                yield

            def scalar(act, t):
                def copy(dst, src, done, ready, n=1):
                    act.wait_ge(s[ready], at(t, ready, n))
                    act.activation(dst, src, ACT.Copy).then_inc(s[done], 1)
                    yield

                def xt_hi(n):
                    yield from copy(xt[:, 0].rearrange("p c n -> p (c n)"), ps[:, 0, 0:D], "xt_hi", "xt_ps", n + 1)

                yield from xt_hi(0)
                act.wait_ge(s["q0_f"], at(t, "q0_f", 1))
                act.activation(qk[:, 0, 0:2], qk_f[:, 0:2], ACT.Copy).then_inc(s["q0_hi"], 1)
                yield
                act.wait_ge(s["exp_bias"], at(t, "exp_bias", 1))
                act.activation(probs[:, 0:KEYS], ps[:, 0, 0:KEYS], ACT.Exp, bias=small[:, 3:4], scale=D ** -0.5,
                               accum_out=small[:, 4:5]).then_inc(s["exps"], 1)
                yield
                yield from copy(pt1[:, 0, :], ps[:, 1, 0:384], "pt1_hi", "pt1_ps")
                yield from copy(op[:, 0].rearrange("p c n -> p (c n)"), ps[:, 2, 0:D], "a1_hi", "a1_ps")
                yield from last_hi(act, t)
                yield from xt_hi(1)
                act.wait_ge(s["qk_f"], at(t, "qk_f", 1))
                act.activation(qk[:, 0], qk_f[:, :, :], ACT.Copy).then_inc(s["qk_hi"], 1)
                yield
                act.wait_ge(s["qk2_lo"], at(t, "qk2_lo", 1))
                for h in range(5, 8):
                    act.activation(qbd.rearrange("p l c b h q -> p l (c b) h q")[:, :, :, h, :],
                                   qk[:, :, 0:2].rearrange("p l c (b q) -> p l (c b) q", b=NB), ACT.Copy, scale=mask8[:, h:h + 1]).then_inc(s["qbd2_act"], 1)
                    yield
                yield from copy(v2[:, 0, :], ps[:, 2, 0:D], "v_hi", "v_ps")
                act.wait_ge(s["self_shift"], at(t, "self_shift", 1))
                act.activation(probs[:, 0:512], s2, ACT.Exp, scale=16 ** -0.5).then_inc(s["self_p"], 1)
                yield
                yield from copy(pt2[:, 0].rearrange("p g n -> p (g n)"), ps[:, 0, :], "self_pt_hi", "self_pt")
                for i in range(2):
                    act.wait_ge(s["o_f"], at(t, "o_f", 2 * i + 2))
                    act.activation(om[:, 0, :, i * P:(i + 1) * P], om_f.rearrange("p (b n) -> p b n", b=NB)[:, :, i * P:(i + 1) * P], ACT.Copy).then_inc(s["o_hi"], 1)
                    yield
                for c in range(C):
                    if c == 0:
                        act.wait_ge(s["o2_ps"], at(t, "o2_ps", 1))
                    act.activation(op[:, 0, c], ps[:, 3, c * P:(c + 1) * P], ACT.Identity, bias=bcol("bv0")[:, c:c + 1]).then_inc(s["o2_hi"], 1)
                    yield
                for b in range(NB):
                    yield from np_hi(act, t, b)
                yield from copy(xqt.rearrange("p c n -> p (c n)"), ps[:, 3, 0:P].bitcast(BF16), "xqt", "xq_ps")
                act.wait_ge(s["gate_ps"], at(t, "gate_ps", 1))
                act.activation(th3[:, 0:512], ps[:, 0, :], ACT.Tanh, scale=small[:, 11:12]).then_inc(s["tanh"], 1)
                yield
                act.wait_ge(s["gate_ps"], at(t, "gate_ps", 2))
                act.activation(th3[:, 512:1024], ps[:, 1, :], ACT.Tanh, scale=small[:, 11:12]).then_inc(s["tanh"], 1)
                yield
                yield from copy(hqt.rearrange("p k n -> p (k n)"), ps[:, 0, :].bitcast(BF16), "hqt", "hq_ps")
                def k_hi(b):
                    yield from copy(kp[:, 0, :, b], ps[:, 0:2, 0:KEYS], "k4_hi", "k4_ps", b + 1)

                def v_hi(b):
                    yield from copy(vp[:, 0, b].rearrange("p m n -> p (m n)"), ps[:, 2 + b % 2, :], "v4_hi", "v4_ps", b + 1)

                yield from v_hi(0)
                yield from xt_hi(2)
                yield from copy(qk[:, 0, 0:2].rearrange("p c n -> p (c n)"), ps[:, 3, 0:D], "q4_hi", "q4_ps")
                yield from copy(vl[0:NB, 0, :], ps[0:NB, 1, 0:D], "vl_hi", "vl_ps")

                def exponentials(u):
                    act.wait_ge(s["s4_bias"], at(t, "s4_bias", u + 1))
                    for g in (2 * (u % 2), 2 * (u % 2) + 1):
                        act.activation(probs[:, KEYS * g:KEYS * (g + 1)], ps[:, g, 0:KEYS], ACT.Exp, bias=small[:, 24 + g:25 + g],
                                       scale=16 ** -0.5, accum_out=small[:, 28 + g:29 + g]).then_inc(s["p4"], 1)
                        yield

                def turned_hi(u):
                    c = u % 2
                    yield from copy(pt4[:, c, 0].rearrange("p (i n) -> p i n", i=2), ps[:, 2 * c:2 * c + 2, 0:384], "pt4_hi", "pt4_ps", u + 1)

                def om_hi(u):
                    yield from copy(om4[:, u % 2, 0, :], om4_f[:, u % 2, :], "om4_hi", "om4_f", u + 1)

                yield from v_hi(1)
                for b in range(NB):
                    yield from k_hi(b)
                    if b + 2 < NB:
                        yield from v_hi(b + 2)
                yield from exponentials(0)
                for u in range(UNITS):
                    yield from turned_hi(u)
                    if u + 1 < UNITS:
                        yield from exponentials(u + 1)
                    if u % 2:
                        yield from tp_hi(act, t, u // 2)
                    yield from om_hi(u)
                yield from copy(op[:, 0], ps.rearrange("p (c i) n -> p c i n", i=2)[:, :, 1, 384:512], "sel_hi", "sel_ps")

            def vector(dve, t):
                made = [0]

                def need(name, n=1):
                    dve.wait_ge(s[name], at(t, name, n))

                def then(ins):
                    made[0] += 1
                    ins.then_inc(s["dve_order"], 1)
                    yield
                    dve.wait_ge(s["dve_order"], at(t, "dve_order", made[0]))

                def alone():
                    made[0] += 1
                    dve.memset(waited[:, :], 0.0).then_inc(s["dve_order"], 1)
                    yield

                def lo(dst, src, hi, done, ready, n=1):
                    need(ready, n)
                    dve.tensor_tensor(dst, src, hi, ALU.subtract).then_inc(s[done], 1)
                    yield

                def normalise(n, src):
                    yield from then(dve.bn_stats(bn[:, :], src))
                    yield from alone()
                    yield from then(dve.bn_aggr(mv[:, :], bn[:, :]))
                    dve.tensor_scalar(var_eps[:, :], mv[:, 1:2], EPS, None, ALU.add).then_inc(s["ln_var"], 1)
                    yield
                    need("ln_rstd", n + 1)
                    return dve.tensor_scalar(xn[:, :], src, mv[:, 0:1], rstd[:, 0:1], ALU.subtract, ALU.mult)

                def normalised_t(k, n, src):
                    ins = yield from normalise(n, src)
                    ins.then_inc(s["xn"], 1)
                    yield
                    yield from lo(xt[:, 1].rearrange("p c n -> p (c n)"), ps[:, 0, 0:D], xt[:, 0].rearrange("p c n -> p (c n)"), "xt_lo", "xt_hi", k + 1)

                def mask_queries(done, heads=range(8)):
                    src = qk[:, :, 0:2].rearrange("p l c (b q) -> p l (c b) q", b=NB)
                    dst = qbd.rearrange("p l c b h q -> p l (c b) h q")
                    for h in heads:
                        ins = dve.tensor_scalar(dst[:, :, :, h, :], src, mask8[:, h:h + 1], None, ALU.mult)
                        if h < heads[-1]:
                            yield from then(ins)
                    ins.then_inc(s[done], 1)
                    yield

                dve.wait_ge(s[f"x_in{lane}"], t * 16 + 16)
                yield from normalised_t(0, 0, x0[:, :])
                need("q0_ps")
                dve.tensor_tensor(qk_f[:, 0:2], ps[:, 1, 0:D].rearrange("p (c n) -> p c n", c=C),
                                  qk_bias[:, 0:2].unsqueeze(2).to_broadcast([P, C, P]), ALU.add).then_inc(s["q0_f"], 1)
                yield
                yield from lo(qk[:, 1, 0:2], qk_f[:, 0:2], qk[:, 0, 0:2], "q0_lo", "q0_hi")
                need("qbk_ps")
                yield from then(dve.tensor_tensor(small[:, 0:1], ps[:, 3, 0:1], qk_bias[:, 4:5], ALU.add))
                need("s1_ps")
                yield from then(dve.tensor_reduce(small[:, 1:2], ps[:, 0, 0:KEYS], X, ALU.max))
                yield from then(dve.tensor_tensor(small[:, 2:3], small[:, 1:2], small[:, 0:1], ALU.add))
                yield from then(dve.tensor_tensor(small[:, 2:3], small[:, 0:1], small[:, 2:3], ALU.subtract))
                dve.tensor_scalar(small[:, 3:4], small[:, 2:3], D ** -0.5, None, ALU.mult).then_inc(s["exp_bias"], 1)
                yield
                need("exps")
                dve.tensor_scalar(last_cols[:, 0, 0:NB], quad, probs[:, KEYS - 1:KEYS], None, ALU.mult).then_inc(s["p1_last"], 1)
                yield
                yield from then(dve.reciprocal(small[:, 5:6], small[:, 4:5]))
                yield from lo(pt1[:, 1, :], ps[:, 1, 0:384], pt1[:, 0, :], "pt1_lo", "pt1_hi")
                yield from lo(op[:, 1].rearrange("p c n -> p (c n)"), ps[:, 2, 0:D], op[:, 0].rearrange("p c n -> p (c n)"), "a1_lo", "a1_hi")
                need("y1_ps")
                dve.wait_ge(s[f"stored{lane}"], t * 16 + 1)
                need("biased", 1)
                dve.scalar_tensor_tensor(x[:, :], ps[:, 3, 0:D], small[:, 5:6], x0[:, :], ALU.mult, ALU.add).then_inc(s["x_1"], 1)
                yield
                need("x_1")

                yield from normalised_t(1, 1, x[:, :])
                need("qk_ps")
                dve.tensor_tensor(qk_f[:, :, :], ps[:, 1].rearrange("p (c n) -> p c n", c=4),
                                  bcol("bqk0").unsqueeze(2).to_broadcast([P, 4, P]), ALU.add).then_inc(s["qk_f"], 1)
                yield
                need("qk_hi")
                dve.tensor_tensor(qk[:, 1], qk_f[:, :, :], qk[:, 0], ALU.subtract).then_inc(s["qk2_lo"], 1)
                yield
                need("qk2_lo")
                yield from mask_queries("qbd2", range(5))
                need("v_hi")
                yield from then(dve.tensor_tensor(v2[:, 1, :], ps[:, 2, 0:D], v2[:, 0, :], ALU.subtract))
                need("self_s")
                s2v = s2.rearrange("p (n k) -> p n k", k=SEQ)
                yield from then(dve.tensor_tensor(s2v, ps[:, 3, :].rearrange("p (n k) -> p n k", k=SEQ),
                                       causal.unsqueeze(1).to_broadcast([P, 16, SEQ]), ALU.add))
                yield from then(dve.tensor_reduce(small[:, 64:80], s2v, X, ALU.max))
                dve.tensor_tensor(s2v, s2v, small[:, 64:80].unsqueeze(2).to_broadcast([P, 16, SEQ]), ALU.subtract).then_inc(s["self_shift"], 1)
                yield
                for b in range(NB):
                    ins = dve.tensor_scalar(vblk.rearrange("p l g b d -> p (l g) b d")[:, :, b, :],
                                            v2.rearrange("p l (g d) -> p (l g) d", g=GROUPS), quad[:, b:b + 1], None, ALU.mult)
                    if b < NB - 1:
                        yield from then(ins)
                ins.then_inc(s["self_v"], 1)
                yield
                need("self_p")
                yield from then(dve.tensor_reduce(small[:, 64:80], probs[:, 0:512].rearrange("p (n k) -> p n k", k=SEQ), X, ALU.add))
                yield from then(dve.reciprocal(small[:, 80:96], small[:, 64:80]))
                rm = th_rm[:, :, :]
                yield from then(dve.tensor_tensor(rm, small[:, 80:96].unsqueeze(2).to_broadcast([P, 16, 4]),
                                       quad.unsqueeze(1).to_broadcast([P, 16, 4]), ALU.mult))
                yield from lo(pt2[:, 1].rearrange("p g n -> p (g n)"), ps[:, 0, :], pt2[:, 0].rearrange("p g n -> p (g n)"), "pt2_lo", "self_pt_hi")
                need("o2g_ps")
                for g in range(GROUPS):
                    dst = om_f.rearrange("p (b g h d) -> p g b h d", b=NB, g=GROUPS, h=4)[:, g]
                    src = ps[:, 1 + g // 2, (g % 2) * D:(g % 2 + 1) * D].rearrange("p (b h d) -> p b h d", b=NB, h=4)
                    dve.tensor_tensor(dst, src, rm[:, NB * g:NB * (g + 1), :].unsqueeze(3).to_broadcast([P, NB, 4, 16]),
                                      ALU.mult).then_inc(s["o_f"], 1)
                    yield
                need("o_hi", 2)
                dve.tensor_tensor(om[:, 1, :, P:D], om_f.rearrange("p (b n) -> p b n", b=NB)[:, :, P:D], om[:, 0, :, P:D], ALU.subtract).then_inc(s["o_lo_v"], 1)
                yield
                need("o2_hi", 2)
                for c in range(C):
                    dve.scalar_tensor_tensor(op[:, 1, c], ps[:, 3, c * P:(c + 1) * P], bcol("bv0")[:, c:c + 1], op[:, 0, c],
                                             ALU.add, ALU.subtract).then_inc(s["o2_lo"], 1)
                    yield
                need("self_y")
                need("biased", 2)
                yield from then(dve.tensor_tensor(x[:, :], ps[:, 0, 0:D], x[:, :], ALU.add))

                ins = yield from normalise(2, x[:, :])
                yield from then(ins)
                yield from then(dve.tensor_reduce(small[:, 8:9], xn[:, :], X, ALU.max, apply_absolute_value=True))
                yield from then(dve.tensor_scalar(small[:, 8:9], small[:, 8:9], 1e-5, None, ALU.max))
                yield from then(dve.reciprocal(small[:, 9:10], small[:, 8:9]))
                yield from then(dve.tensor_scalar(small[:, 9:10], small[:, 9:10], 127.0, None, ALU.mult))
                yield from then(dve.tensor_scalar(xq_f, xn[:, :], small[:, 9:10], ROUND, ALU.mult, ALU.add))
                yield from then(dve.tensor_scalar(xq, xq_f, ROUND, 127.0, ALU.subtract, ALU.min))
                yield from then(dve.tensor_scalar(small[:, 10:11], small[:, 8:9], 1.0 / 127.0, None, ALU.mult))
                yield from then(dve.tensor_scalar(small[:, 11:12], small[:, 10:11], ffn_inv[:, 0:1], 0.5, ALU.mult, ALU.mult))
                yield from then(dve.tensor_scalar(small[:, 12:13], small[:, 10:11], ffn_inv[:, 1:2], small[:, 11:12], ALU.mult, ALU.mult))
                dve.tensor_scalar(xq, xq, -128.0, None, ALU.max).then_inc(s["xq"], 1)
                yield
                for i in range(2):
                    cols = slice(512 * i, 512 * (i + 1))
                    need("tanh", i + 1)
                    yield from then(dve.scalar_tensor_tensor(r3[:, cols], th3[:, cols], 1.0, ps[:, i, :], ALU.add, ALU.mult))
                for i in range(2):
                    cols = slice(512 * i, 512 * (i + 1))
                    need("up_ps", i + 1)
                    yield from then(dve.tensor_tensor(r3[:, cols], r3[:, cols], ps[:, 2 + i, :], ALU.mult))
                yield from then(dve.tensor_reduce(small[:, 13:14], r3, X, ALU.max, apply_absolute_value=True))
                yield from then(dve.tensor_scalar(small[:, 13:14], small[:, 13:14], small[:, 12:13], 1e-5, ALU.mult, ALU.max))
                yield from then(dve.reciprocal(small[:, 14:15], small[:, 13:14]))
                yield from then(dve.tensor_scalar(small[:, 15:16], small[:, 14:15], small[:, 12:13], 127.0, ALU.mult, ALU.mult))
                yield from then(dve.tensor_scalar(rq3, r3, small[:, 15:16], ROUND, ALU.mult, ALU.add))
                yield from then(dve.tensor_scalar(hq, rq3, ROUND, 127.0, ALU.subtract, ALU.min))
                dve.tensor_scalar(hq, hq, -128.0, None, ALU.max).then_inc(s["hq"], 1)
                yield
                yield from then(dve.tensor_scalar(small[:, 16:17], small[:, 13:14], ffn_inv[:, 2:3], 1.0 / 127.0, ALU.mult, ALU.mult))
                need("ffn_y")
                yield from then(dve.scalar_tensor_tensor(x[:, :], ps[:, 1, 0:D], small[:, 16:17], x[:, :], ALU.mult, ALU.add))

                def k_lo(b):
                    yield from lo(kp[:, 1, :, b], ps[:, 0:2, 0:KEYS], kp[:, 0, :, b], "k4_lo", "k4_hi", b + 1)

                def v_lo(b):
                    yield from lo(vp[:, 1, b].rearrange("p m n -> p (m n)"), ps[:, 2 + b % 2, :], vp[:, 0, b].rearrange("p m n -> p (m n)"), "v4_lo", "v4_hi", b + 1)

                ins = yield from normalise(3, x[:, :])
                ins.then_inc(s["xn"], 1)
                yield
                yield from v_lo(0)
                yield from lo(xt[:, 1].rearrange("p c n -> p (c n)"), ps[:, 0, 0:D], xt[:, 0].rearrange("p c n -> p (c n)"), "xt_lo", "xt_hi", 3)
                need("q4_hi")
                dve.tensor_tensor(qk[:, 1, 0:2].rearrange("p c n -> p (c n)"), ps[:, 3, 0:D], qk[:, 0, 0:2].rearrange("p c n -> p (c n)"),
                                  ALU.subtract).then_inc(s["q4_lo"], 1)
                yield
                need("q4_lo")
                yield from lo(vl[0:NB, 1, :], ps[0:NB, 1, 0:D], vl[0:NB, 0, :], "vl_lo", "vl_hi")

                def maximum(u):
                    c = u % 2
                    need("s4_ps", u + 1)
                    yield from then(dve.tensor_reduce(small[:, 20 + 2 * c:22 + 2 * c], ps[:, 2 * c:2 * c + 2, 0:KEYS], X, ALU.max))
                    dve.tensor_scalar(small[:, 24 + 2 * c:26 + 2 * c], small[:, 20 + 2 * c:22 + 2 * c], -(16 ** -0.5), None, ALU.mult).then_inc(s["s4_bias"], 1)
                    yield

                def scale_mask(u):
                    return th_rm[:, 2 * (u % 4):2 * (u % 4) + 2, :]

                def last_key(u):
                    b, c = u // 2, u % 2
                    need("p4", 2 * (u + 1))
                    if u >= 2:
                        need("pt4_ps", u - 1)
                    pv = probs[:, 2 * c * KEYS:(2 * c + 2) * KEYS].rearrange("p (g m) -> p g m", g=2)
                    dve.tensor_tensor(last_cols[:, 2 * c:2 * c + 2, 0:NB], pv[:, :, KEYS - 1:KEYS].to_broadcast([P, 2, NB]),
                                      eye4[:, b, :].unsqueeze(1).to_broadcast([P, 2, NB]), ALU.mult).then_inc(s["p4_last"], 1)
                    yield
                    yield from then(dve.reciprocal(small[:, 32 + 2 * c:34 + 2 * c], small[:, 28 + 2 * c:30 + 2 * c]))
                    yield from then(dve.tensor_tensor(scale_mask(u), small[:, 32 + 2 * c:34 + 2 * c].unsqueeze(2).to_broadcast([P, 2, 4]),
                                                      quad.unsqueeze(1).to_broadcast([P, 2, 4]), ALU.mult))

                def om_mask(u):
                    need("o4_ps", u + 1)
                    if u >= 2:
                        need("om4_lo", u - 1)
                    dve.tensor_tensor(om4_f[:, u % 2, :].rearrange("p (n d) -> p n d", d=16), ps[:, 2 * (u % 2), 384:512].rearrange("p (n d) -> p n d", d=16),
                                      scale_mask(u).rearrange("p n h -> p (n h)").unsqueeze(2).to_broadcast([P, 8, 16]), ALU.mult).then_inc(s["om4_f"], 1)
                    yield

                def turned_lo(u):
                    c = u % 2
                    yield from lo(pt4[:, c, 1].rearrange("p (i n) -> p i n", i=2), ps[:, 2 * c:2 * c + 2, 0:384],
                                  pt4[:, c, 0].rearrange("p (i n) -> p i n", i=2), "pt4_lo", "pt4_hi", u + 1)

                yield from v_lo(1)
                for b in range(NB):
                    yield from k_lo(b)
                    yield from mask_queries("qbd4", range(2 * b, 2 * b + 2))
                    if b + 2 < NB:
                        yield from v_lo(b + 2)
                yield from maximum(0)
                for u in range(UNITS):
                    yield from last_key(u)
                    yield from turned_lo(u)
                    if u + 1 < UNITS:
                        yield from maximum(u + 1)
                    yield from om_mask(u)
                yield from lo(op[:, 1], ps.rearrange("p (c i) n -> p c i n", i=2)[:, :, 1, 384:512], op[:, 0], "sel_lo", "sel_hi")
                need("y4_ps")
                need("biased", 3)
                dve.tensor_tensor(x[:, :], ps[:, 0, 0:D], x[:, :], ALU.add).then_inc(s["x_4"], 1)
                yield
                assert made[0] == FIRST["dve_order"], made[0]

            def gpsimd(pool, t):
                def power(n):
                    pool.wait_ge(s["ln_var"], at(t, "ln_var", n + 1))
                    pool.tensor_tensor(rstd[:, :], var_eps[:, :], neg_half[:, :], ALU.pow).then_inc(s["ln_rstd"], 1)
                    yield

                def om_lo(u):
                    pool.wait_ge(s["om4_hi"], at(t, "om4_hi", u + 1))
                    pool.tensor_tensor(om4[:, u % 2, 1, :], om4_f[:, u % 2, :], om4[:, u % 2, 0, :], ALU.subtract).then_inc(s["om4_lo"], 1)
                    yield

                def add_bias(n, dst, row):
                    pool.wait_ge(s["xn"], at(t, "xn", n + 1))
                    pool.tensor_tensor(dst, dst, row_bias[:, row, :], ALU.add).then_inc(s["biased"], 1)
                    yield

                yield from power(0)
                yield from add_bias(0, x0[:, :], 0)
                yield from power(1)
                yield from add_bias(1, x[:, :], 1)
                yield from last_lo(pool, t)
                pool.wait_ge(s["o_hi"], at(t, "o_hi", 1))
                pool.tensor_tensor(om[:, 1, :, 0:P], om_f.rearrange("p (b n) -> p b n", b=NB)[:, :, 0:P], om[:, 0, :, 0:P], ALU.subtract).then_inc(s["o_lo"], 1)
                yield
                yield from power(2)
                for b in range(NB):
                    yield from np_lo(pool, t, b)
                yield from power(3)
                yield from add_bias(2, x[:, :], 2)
                for u in range(UNITS):
                    yield from om_lo(u)
                    if u % 2:
                        yield from tp_lo(pool, t, u // 2)

            return dict(ctx_lp=ctx_lp, tensor=tensor, scalar=scalar, vector=vector, gpsimd=gpsimd, scalar_before=scalar_before,
                                   gpsimd_before=gpsimd_before, load_n=load_n, load_t=load_t, load_l=load_l, load_x=load_x,
                                   store_x=store_x, at=at)

        def second_half(lane):
            me = own[lane]
            x0, x, x_out, xn, xt, bn, mv, var_eps, rstd = me["x0"], me["x"], me["x_out"], me["xn"], me["xt"], me["bn"], me["mv"], me["var_eps"], me["rstd"]
            small, idx, waited, gate_p = me["small"], me["idx"], me["waited"], me["gate_p"]
            qk = [me["qk"], carve(me["qk_f"].rearrange("p c n -> p (c n)"), 0, 512, F16).rearrange("p (l c n) -> p l c n", l=2, c=4)]
            at = counter(SECOND, FIRST, lane)
            ps = psum[:, 4 * lane:4 * lane + 4, :]
            arena = mem[:, W_COLS[1] + LANE_2 * lane:W_COLS[1] + LANE_2 * (lane + 1)]
            qk_f = carve(arena, 7168, 1024).rearrange("p (s c n) -> p s c n", s=2, c=4)
            qb5 = carve(arena, 6144, 1024, F16).rearrange("p (l c b h q) -> p l c b h q", l=2, c=C, b=NB, h=4)
            v5 = carve(arena, 0, 1024, F16).rearrange("p (l n) -> p l n", l=2)
            s5 = carve(arena, 1024, 512)
            pt5 = carve(arena, 1536, 512, F16).rearrange("p (l g n) -> p l g n", l=2, g=GROUPS)
            ptb = carve(arena, 2048, 2048, F16).rearrange("p (l g b n) -> p l g b n", l=2, g=GROUPS, b=NB)
            o5_f = carve(arena, 4096, 1024)
            o5 = carve(arena, 5120, 1024, F16).rearrange("p (l j n) -> p l j n", l=2, j=8)
            wb = carve(arena, 0, 1024).rearrange("p (e n) -> p e n", e=EXPERTS)
            mb = carve(arena, 1024, 1024).rearrange("p (e n) -> p e n", e=EXPERTS)
            u4 = [carve(arena, at_, 512).rearrange("p (c n) -> p c n", c=4) for at_ in (2048, 2560, 7168)]
            th6 = carve(arena, 3072, 512)
            v6 = carve(arena, 3584, 256)
            h_f = carve(arena, 3840, 512)
            hp = carve(arena, 4352, 512, F16)
            x2_f = carve(arena, 4864, 256)
            a3_f = carve(arena, 5120, 256)
            y = carve(arena, 5376, 256)
            prod = carve(arena, 5632, 256)

            def load_x(sp, trip):
                sp.wait_ge(s["x_5"], at(trip, "x_5", 0))
                sp.dma_start(x0[:, :], mid[bass.ds(trip * LANES + lane, 1)].rearrange("t p d -> (t p) d")).then_inc(s[f"x_in{lane}"], 16)

            def store_out(act, trip):
                act.wait_ge(s["x_final"], at(trip, "x_final", 1))
                act.dma_start(out[bass.ds(trip * LANES + lane, 1)].rearrange("t p d -> (t p) d"), x_out[:, :]).then_inc(s[f"stored{lane}"], 16)

            def tensor(pe, t):
                def need(name, n=1):
                    pe.wait_ge(s[name], at(t, name, n))

                def transpose_x(n):
                    need("xn", n + 1)
                    for c in range(C):
                        last = pe.transpose(ps[:, 0, c * P:(c + 1) * P], xn[:, c * P:(c + 1) * P], ident)
                    last.then_inc(s["xt_ps"], 1)
                    yield
                    need("xt_lo", n + 1)

                def self_scores(g):
                    need("qb5", g + 1)
                    for b in range(NB):
                        last = product(pe, ps[:, 2, g * P + SEQ * b:g * P + SEQ * (b + 1)], [
                            ((qb5[:, 0, c, b].rearrange("p h q -> p (h q)"), qb5[:, 1, c, b].rearrange("p h q -> p (h q)")),
                             (qk[g % 2][:, 0, 2 + c, SEQ * b:SEQ * (b + 1)], qk[g % 2][:, 1, 2 + c, SEQ * b:SEQ * (b + 1)])) for c in range(C)])
                    last.then_inc(s["self_s"], 1)
                    yield

                yield from transpose_x(0)

                def queries_keys(g):
                    if g >= 2:
                        need("qk_f", g - 1)
                    bank = ps[:, g % 2]
                    feature_major(pe, bank[:, 0:D], "aq", WIDE, xt, range(2 * g, 2 * g + 2))
                    feature_major(pe, bank[:, D:2 * D], "ak", WIDE, xt, range(2 * g, 2 * g + 2)).then_inc(s["qk_ps"], 1)
                    yield

                yield from queries_keys(0)
                yield from queries_keys(1)
                for g in range(GROUPS):
                    if g + 2 < GROUPS:
                        yield from queries_keys(g + 2)
                    yield from self_scores(g)
                need("qk_f", GROUPS)
                for j in range(2):
                    last = token_major(pe, ps[:, j, :], "av", WIDE, xt, 512 * j, 512 * (j + 1))
                last.then_inc(s["v_ps"], 1)
                yield
                need("p5_norm")
                for g in range(GROUPS):
                    last = pe.transpose(ps[:, 3, g * P:(g + 1) * P], s5[:, g * P:(g + 1) * P], ident)
                last.then_inc(s["self_pt"], 1)
                yield
                need("ptb")
                need("ptb_act")
                need("self_v")
                for j in range(8):
                    hh = (j % 2) * 64
                    pt = [ptb[:, a, j // 2, :, hh:hh + 64] for a in range(2)]
                    last = product(pe, ps[:, j // 2, (j % 2) * D:(j % 2 + 1) * D],
                                   [((v5[:, 0, j * P:(j + 1) * P], v5[:, 1, j * P:(j + 1) * P]), (pt[0], pt[1]))])
                    if j % 2:
                        last.then_inc(s["o5_ps"], 1)
                        yield
                for i in range(2):
                    need(("o_lo", "o_lo_v")[i])
                    last = product(pe, ps[:, 0, 0:D], [
                        ((o5[:, 0, k], o5[:, 1, k]), (w("ao", 0, 8, D)[:, k, :], w("ao", 1, 8, D)[:, k, :])) for k in range(4 * i, 4 * i + 4)],
                        start=i == 0, stop=i == 1)
                    last.then_inc(s["self_y"], 1)
                    yield

                yield from transpose_x(1)
                token_major(pe, ps[:, 3, 0:EXPERTS], "gate", EXPERTS, xt, 0, EXPERTS).then_inc(s["gate_ps"], 1)
                yield
                feature_major(pe, ps[:, 1], "sw1", SHARED, xt, range(4))
                feature_major(pe, ps[:, 2], "sw2", SHARED, xt, range(4)).then_inc(s["sh_ps"], 1)
                yield
                need("gate_p")
                for e in range(EXPERTS):
                    for a in range(2):
                        last = pe.matmul(ps[:, (3, 0)[e // 4], (e % 4) * P:(e % 4 + 1) * P], gate_p[:, a, e:e + 1].to_broadcast([P, P]), ident16[:, :],
                                         start=(a == 0), stop=(a == 1))
                last.then_inc(s["wb_ps"], 1)
                yield
                need("sh_f")
                for e in range(EXPERTS):
                    last = pe.matmul(ps[:, 1 + e // 4, (e % 4) * P:(e % 4 + 1) * P], gate_p[:, 2, e:e + 1].to_broadcast([P, P]), ident16[:, :],
                                     start=True, stop=True)
                last.then_inc(s["mb_ps"], 1)
                yield

                def expert_in(e):
                    if e < 2:
                        need("mb")
                    else:
                        need("u4", e - 1)
                    bank = ps[:, 1 + e % 2]
                    feature_major(pe, bank[:, 0:D], "w1", D, xt, range(C), first=e * C * D)
                    feature_major(pe, bank[:, D:2 * D], "w3", D, xt, range(C), first=e * C * D).then_inc(s["e13_ps"], 1)
                    yield

                he = hp[:, 0:512].rearrange("p (l k n) -> p l k n", l=2, k=C)
                yield from expert_in(0)
                yield from expert_in(1)
                need("sh_lo")
                need("wb", 2)
                sp_pair = hp.rearrange("p (l k n) -> p l k n", l=2, k=4)
                feature_major(pe, ps[:, 0], "sw3", D, sp_pair, range(C), k=4).then_inc(s["z_ps"], 1)
                yield
                for e in range(EXPERTS):
                    if e + 2 < EXPERTS:
                        yield from expert_in(e + 2)
                    need("he_lo", e + 1)
                    if e == 1:
                        need("y_0")
                    if e >= 2:
                        need("x2", 2 * (e - 1))
                    feature_major(pe, ps[:, (3, 0)[e % 2]], "w2", D, he, range(C), first=e * C * D).then_inc(s["e2_ps"], 1)
                    yield
                need("y_add", EXPERTS)
                for c in range(C):
                    last = pe.transpose(ps[:, 0, c * P:(c + 1) * P], y[:, c * P:(c + 1) * P], ident)
                last.then_inc(s["ffn_y"], 1)
                yield

            def scalar(act, t):
                def copy(dst, src, done, ready, n=1):
                    act.wait_ge(s[ready], at(t, ready, n))
                    act.activation(dst, src, ACT.Copy).then_inc(s[done], 1)
                    yield

                def xt_hi(n):
                    yield from copy(xt[:, 0].rearrange("p c n -> p (c n)"), ps[:, 0, 0:D], "xt_hi", "xt_ps", n + 1)

                yield from xt_hi(0)
                for g in range(GROUPS):
                    act.wait_ge(s["qk_f"], at(t, "qk_f", g + 1))
                    act.activation(qk[g % 2][:, 0], qk_f[:, g % 2], ACT.Copy).then_inc(s["qk_hi"], 1)
                    yield
                act.wait_ge(s["self_shift"], at(t, "self_shift", 1))
                act.activation(s5, s5, ACT.Exp, scale=64 ** -0.5).then_inc(s["self_p"], 1)
                yield
                yield from copy(v5[:, 0, :], ps[:, 0:2, :].rearrange("p a n -> p (a n)"), "v_hi", "v_ps")
                yield from copy(pt5[:, 0].rearrange("p g n -> p (g n)"), ps[:, 3, :], "self_pt_hi", "self_pt")
                act.wait_ge(s["pt5_lo"], at(t, "pt5_lo", 1))
                act.activation(ptb.rearrange("p l g b n -> p (l g) b n")[:, :, NB - 1, :], pt5.rearrange("p l g n -> p (l g) n"), ACT.Copy,
                               scale=quad[:, NB - 1:NB]).then_inc(s["ptb_act"], 1)
                yield
                for i in range(2):
                    act.wait_ge(s["o_f"], at(t, "o_f", 4 * i + 4))
                    act.activation(o5[:, 0, 4 * i:4 * i + 4].rearrange("p j n -> p (j n)"), o5_f[:, 512 * i:512 * (i + 1)], ACT.Copy).then_inc(s["o_hi"], 1)
                    yield
                yield from xt_hi(1)
                act.wait_ge(s["exp_bias"], at(t, "exp_bias", 1))
                act.activation(small[:, 48:56], ps[:, 3, 0:EXPERTS], ACT.Exp, bias=small[:, 40:41], accum_out=small[:, 41:42]).then_inc(s["exps"], 1)
                yield
                act.wait_ge(s["sh_ps"], at(t, "sh_ps", 1))
                act.activation(th6, ps[:, 1, :], ACT.Tanh, scale=0.5).then_inc(s["tanh"], 1)
                yield
                for i in range(2):
                    yield from copy(wb[:, 4 * i:4 * i + 4], ps[:, (3, 0)[i], :].rearrange("p (e n) -> p e n", n=P), "wb", "wb_ps")
                yield from copy(mb, ps[:, 1:3, :].rearrange("p a (e n) -> p (a e) n", n=P), "mb", "mb_ps")
                act.wait_ge(s["sh_f"], at(t, "sh_f", 1))
                act.activation(hp[:, 0:512], h_f, ACT.Copy).then_inc(s["sh_hi"], 1)
                yield

                def second_product(e):
                    if e >= 1:
                        act.wait_ge(s["prod"], at(t, "prod", e))
                    act.wait_ge(s["e2_ps"], at(t, "e2_ps", e + 1))
                    for c in range(C):
                        k = e * C + c
                        act.activation(x2_f[:, c * P:(c + 1) * P], ps[:, (3, 0)[e % 2], c * P:(c + 1) * P], ACT.Identity,
                                       bias=bcol("b2")[:, k:k + 1], scale=0.5).then_inc(s["x2"], 1)
                        yield

                for e in range(EXPERTS):
                    act.wait_ge(s["u4"], at(t, "u4", e + 1))
                    for c in range(C):
                        k = e * C + c
                        act.activation(th6[:, c * P:(c + 1) * P], u4[e % 3][:, c], ACT.Tanh, scale=0.5, bias=half_b1[:, k:k + 1]).then_inc(s["th_e"], 1)
                        yield
                    for c in range(C):
                        k = e * C + c
                        act.activation(v6[:, c * P:(c + 1) * P], u4[e % 3][:, c], ACT.Identity, bias=bcol("b1")[:, k:k + 1]).then_inc(s["th_e"], 1)
                        yield
                    act.wait_ge(s["he_f"], at(t, "he_f", e + 1))
                    if e >= 1:
                        act.wait_ge(s["e2_ps"], at(t, "e2_ps", e))
                    act.activation(hp[:, 0:256], h_f[:, 0:256], ACT.Copy).then_inc(s["he_hi"], 1)
                    yield
                    if e >= 1:
                        yield from second_product(e - 1)
                yield from second_product(EXPERTS - 1)
                store_out(act, t)
                yield

            def vector(dve, t):
                made = [0]

                def need(name, n=1):
                    dve.wait_ge(s[name], at(t, name, n))

                def then(ins):
                    made[0] += 1
                    ins.then_inc(s["dve_order"], 1)
                    yield
                    dve.wait_ge(s["dve_order"], at(t, "dve_order", made[0]))

                def alone():
                    made[0] += 1
                    dve.memset(waited[:, :], 0.0).then_inc(s["dve_order"], 1)
                    yield

                def lo(dst, src, hi, done, ready, n=1):
                    need(ready, n)
                    dve.tensor_tensor(dst, src, hi, ALU.subtract).then_inc(s[done], 1)
                    yield

                def normalise(n, src):
                    yield from then(dve.bn_stats(bn[:, :], src))
                    yield from alone()
                    yield from then(dve.bn_aggr(mv[:, :], bn[:, :]))
                    dve.tensor_scalar(var_eps[:, :], mv[:, 1:2], EPS, None, ALU.add).then_inc(s["ln_var"], 1)
                    yield
                    need("ln_rstd", n + 1)
                    return dve.tensor_scalar(xn[:, :], src, mv[:, 0:1], rstd[:, 0:1], ALU.subtract, ALU.mult)

                def normalised_t(k, n, src):
                    ins = yield from normalise(n, src)
                    ins.then_inc(s["xn"], 1)
                    yield
                    yield from lo(xt[:, 1].rearrange("p c n -> p (c n)"), ps[:, 0, 0:D], xt[:, 0].rearrange("p c n -> p (c n)"), "xt_lo", "xt_hi", k + 1)

                dve.wait_ge(s[f"x_in{lane}"], (TRIPS + t) * 16 + 32)
                yield from normalised_t(0, 0, x0[:, :])
                def biased(g):
                    need("qk_ps", g + 1)
                    if g >= 2:
                        need("self_s", g - 1)
                    dve.tensor_tensor(qk_f[:, g % 2], ps[:, g % 2].rearrange("p (c n) -> p c n", c=4),
                                      bcol("bqk1")[:, 4 * g:4 * g + 4].unsqueeze(2).to_broadcast([P, 4, P]), ALU.add).then_inc(s["qk_f"], 1)
                    yield

                yield from biased(0)
                for g in range(GROUPS):
                    if g + 1 < GROUPS:
                        yield from biased(g + 1)
                    need("qk5_lo", g + 1)
                    if g >= 1:
                        need("self_s", g)
                    for h in range(4):
                        c = h // 2
                        ins = dve.tensor_scalar(qb5[:, :, c, :, h, :], qk[g % 2][:, :, c].rearrange("p l (b q) -> p l b q", b=NB),
                                                half[:, h % 2:h % 2 + 1], None, ALU.mult)
                        if h < 3:
                            yield from then(ins)
                    ins.then_inc(s["qb5"], 1)
                    yield
                need("self_s", GROUPS)
                s5v = s5.rearrange("p (n k) -> p n k", k=SEQ)
                psv = ps[:, 2, :].rearrange("p (n k) -> p n k", k=SEQ)
                yield from then(dve.tensor_reduce(small[:, 64:80], psv, X, ALU.max))
                dve.tensor_tensor(s5v, psv, small[:, 64:80].unsqueeze(2).to_broadcast([P, 16, SEQ]), ALU.subtract).then_inc(s["self_shift"], 1)
                yield
                need("self_p")
                yield from then(dve.tensor_reduce(small[:, 64:80], s5v, X, ALU.add))
                yield from then(dve.reciprocal(small[:, 80:96], small[:, 64:80]))
                dve.tensor_tensor(s5v, s5v, small[:, 80:96].unsqueeze(2).to_broadcast([P, 16, SEQ]), ALU.mult).then_inc(s["p5_norm"], 1)
                yield
                yield from lo(v5[:, 1, :], ps[:, 0:2, :].rearrange("p a n -> p (a n)"), v5[:, 0, :], "self_v", "v_hi")
                need("self_pt_hi")
                dve.tensor_tensor(pt5[:, 1].rearrange("p g n -> p (g n)"), ps[:, 3, :], pt5[:, 0].rearrange("p g n -> p (g n)"), ALU.subtract).then_inc(s["pt5_lo"], 1)
                yield
                need("pt5_lo")
                for b in range(NB - 1):
                    ins = dve.tensor_scalar(ptb.rearrange("p l g b n -> p (l g) b n")[:, :, b, :],
                                            pt5.rearrange("p l g n -> p (l g) n"), quad[:, b:b + 1], None, ALU.mult)
                    if b < NB - 2:
                        yield from then(ins)
                ins.then_inc(s["ptb"], 1)
                yield
                for i in range(4):
                    need("o5_ps", i + 1)
                    for hh in range(2):
                        pr = slice(64 * hh, 64 * hh + 64)
                        src = ps[pr, i, :].rearrange("p (j b h q) -> p j b h q", j=2, b=NB, h=2)[:, :, :, hh, :]
                        dst = o5_f[pr, 256 * i:256 * (i + 1)].rearrange("p (j b q) -> p j b q", j=2, b=NB)
                        a0 = B_AT["bv1"][0] + 2 * i
                        dve.tensor_tensor(dst, src, bias[pr, a0:a0 + 2].unsqueeze(2).unsqueeze(3).to_broadcast([64, 2, NB, SEQ]),
                                          ALU.add).then_inc(s["o_f"], 1)
                        yield
                need("o_hi", 2)
                dve.tensor_tensor(o5[:, 1, 4:8].rearrange("p j n -> p (j n)"), o5_f[:, 512:1024], o5[:, 0, 4:8].rearrange("p j n -> p (j n)"),
                                  ALU.subtract).then_inc(s["o_lo_v"], 1)
                yield
                need("self_y", 2)
                need("biased")
                dve.tensor_tensor(x[:, :], ps[:, 0, 0:D], x0[:, :], ALU.add).then_inc(s["x_5"], 1)
                yield
                need("x_5")

                yield from normalised_t(1, 1, x[:, :])
                need("gate_ps")
                yield from then(dve.tensor_reduce(small[:, 42:43], ps[:, 3, 0:EXPERTS], X, ALU.max))
                dve.tensor_scalar(small[:, 40:41], small[:, 42:43], -1.0, None, ALU.mult).then_inc(s["exp_bias"], 1)
                yield
                need("exps")
                yield from then(dve.reciprocal(small[:, 43:44], small[:, 41:42]))
                yield from then(dve.tensor_scalar(small[:, 48:56], small[:, 48:56], small[:, 43:44], None, ALU.mult))
                yield from alone()
                yield from then(dve.max(small[:, 56:64], small[:, 48:56]))
                yield from alone()
                yield from then(dve.max_index(idx[:, :], small[:, 56:64], small[:, 48:56]))
                yield from then(dve.tensor_copy(small[:, 56:64], idx[:, :]))
                yield from then(dve.tensor_scalar(small[:, 80:88], const("iota8"), small[:, 56:57], None, ALU.is_equal))
                yield from then(dve.scalar_tensor_tensor(gate_p[:, 2, :], const("iota8"), small[:, 57:58], small[:, 80:88], ALU.is_equal, ALU.add))
                yield from then(dve.tensor_copy(gate_p[:, 0, :], small[:, 48:56]))
                dve.tensor_tensor(gate_p[:, 1, :], small[:, 48:56], gate_p[:, 0, :], ALU.subtract).then_inc(s["gate_p"], 1)
                yield
                need("tanh")
                yield from then(dve.scalar_tensor_tensor(h_f, th6, 1.0, ps[:, 1, :], ALU.add, ALU.mult))
                dve.scalar_tensor_tensor(h_f, h_f, 0.5, ps[:, 2, :], ALU.mult, ALU.mult).then_inc(s["sh_f"], 1)
                yield
                def scale_in(e):
                    need("e13_ps", e + 1)
                    if e == 0:
                        need("wb", 2)
                    dve.tensor_tensor(u4[e % 3], ps[:, 1 + e % 2].rearrange("p (c n) -> p c n", c=4),
                                      wb[:, e].unsqueeze(1).to_broadcast([P, 4, P]), ALU.mult).then_inc(s["u4"], 1)
                    yield

                def combine(e):
                    if e >= 1:
                        need("prod", e)
                    for c in range(C):
                        k = e * C + c
                        dve.scalar_tensor_tensor(a3_f[:, c * P:(c + 1) * P], u4[e % 3][:, 2 + c], bcol("b3")[:, k:k + 1], mb[:, e],
                                                 ALU.add, ALU.mult).then_inc(s["a3"], 1)
                        yield

                yield from scale_in(0)
                need("z_ps")
                dve.tensor_copy(y, ps[:, 0, 0:D]).then_inc(s["y_0"], 1)
                yield
                for e in range(EXPERTS):
                    need("th_e", 4 * (e + 1))
                    if e >= 1:
                        need("he_lo", e)
                    dve.scalar_tensor_tensor(h_f[:, 0:256], th6[:, 0:256], 1.0, v6, ALU.add, ALU.mult).then_inc(s["he_f"], 1)
                    yield
                    if e + 1 < EXPERTS:
                        if e >= 2:
                            need("a3", C * (e - 1))
                        yield from scale_in(e + 1)
                    need("he_hi", e + 1)
                    dve.tensor_tensor(hp[:, 256:512], h_f[:, 0:256], hp[:, 0:256], ALU.subtract).then_inc(s["he_lo"], 1)
                    yield
                    if e >= 1:
                        yield from combine(e - 1)
                yield from combine(EXPERTS - 1)
                need("ffn_y")
                dve.wait_ge(s[f"stored{lane}"], (TRIPS + t) * 16 + 1)
                dve.tensor_tensor(x_out[:, :], ps[:, 0, 0:D], x[:, :], ALU.add).then_inc(s["x_final"], 1)
                yield
                assert made[0] == SECOND["dve_order"], made[0]

            def gpsimd(pool, t):
                def power(n):
                    pool.wait_ge(s["ln_var"], at(t, "ln_var", n + 1))
                    pool.tensor_tensor(rstd[:, :], var_eps[:, :], neg_half[:, :], ALU.pow).then_inc(s["ln_rstd"], 1)
                    yield

                def add_bias(n, dst, row):
                    pool.wait_ge(s["xn"], at(t, "xn", n + 1))
                    pool.tensor_tensor(dst, dst, row_bias[:, row, :], ALU.add).then_inc(s["biased"], 1)
                    yield

                yield from power(0)
                yield from add_bias(0, x0[:, :], 3)
                for g in range(GROUPS):
                    pool.wait_ge(s["qk_hi"], at(t, "qk_hi", g + 1))
                    pool.tensor_tensor(qk[g % 2][:, 1], qk_f[:, g % 2], qk[g % 2][:, 0], ALU.subtract).then_inc(s["qk5_lo"], 1)
                    yield
                pool.wait_ge(s["o_hi"], at(t, "o_hi", 1))
                pool.tensor_tensor(o5[:, 1, 0:4].rearrange("p j n -> p (j n)"), o5_f[:, 0:512],
                                   o5[:, 0, 0:4].rearrange("p j n -> p (j n)"), ALU.subtract).then_inc(s["o_lo"], 1)
                yield
                yield from power(1)
                pool.wait_ge(s["sh_hi"], at(t, "sh_hi", 1))
                pool.tensor_tensor(hp[:, 512:1024], h_f, hp[:, 0:512], ALU.subtract).then_inc(s["sh_lo"], 1)
                yield
                def add_expert(e):
                    if e == 0:
                        pool.wait_ge(s["y_0"], at(t, "y_0", 1))
                    pool.wait_ge(s["x2"], at(t, "x2", C * (e + 1)))
                    pool.wait_ge(s["a3"], at(t, "a3", C * (e + 1)))
                    pool.tensor_tensor(prod, x2_f, a3_f, ALU.mult).then_inc(s["prod"], 1)
                    yield
                    pool.wait_ge(s["prod"], at(t, "prod", e + 1))
                    pool.tensor_tensor(y, y, prod, ALU.add).then_inc(s["y_add"], 1)
                    yield
                    pool.wait_ge(s["y_add"], at(t, "y_add", e + 1))

                for e in range(EXPERTS):
                    yield from add_expert(e)

            return dict(tensor=tensor, scalar=scalar, vector=vector, gpsimd=gpsimd, load_x=load_x, store_out=store_out, qb5=qb5)

        first = [first_half(k) for k in range(LANES)]
        second = [second_half(k) for k in range(LANES)]
        chunks = [0, W_GROUPS[0] * W_SLOTS, (W_GROUPS[0] + W_GROUPS[1]) * W_SLOTS]
        block = ctx.enter_context(nc.Block())

        @block.sync
        def _(sp):
            sp.sem_inc(s["x_5"], 2)
            for lane in range(LANES):
                sp.sem_inc(s[f"stored{lane}"], 1)
            sp.dma_start(cst[:, :], consts).then_inc(s["const_in"], 16)
            sp.dma_start(bias[:, :], biases).then_inc(s["const_in"], 16)
            sp.dma_start(row_bias[:, :, :], rows.rearrange("p (r n) -> p r n", r=4)).then_inc(s["const_in"], 16)
            for i in range(3):
                sp.dma_start(ffn_stage[i], ffn[i]).then_inc(s["ffn_in"], 16)
            for j in range(W_SLOTS):
                sp.dma_start(w_stage[0][j], weights[:, W_CHUNK[0] * j:W_CHUNK[0] * (j + 1)]).then_inc(s[f"w_in{j}"], 16)
            for lane in first:
                lane["load_x"](sp, -1)
                lane["load_l"](sp, -1)
            for b in range(NB):
                for lane in first:
                    lane["load_n"](sp, -1, b)
                    lane["load_t"](sp, -1, b)
            with sp.Fori(0, TRIPS) as t:
                for b in range(2):
                    for lane in first:
                        lane["load_n"](sp, t, b)
                for b in range(2):
                    for lane in first:
                        lane["load_t"](sp, t, b)
                for lane in first:
                    lane["load_l"](sp, t)
                    lane["load_x"](sp, t)
                for b in range(2, NB):
                    for lane in first:
                        lane["load_n"](sp, t, b)
                for b in range(2, NB):
                    for lane in first:
                        lane["load_t"](sp, t, b)
                for lane in first:
                    lane["store_x"](sp, t)
            for lane in range(LANES):
                sp.wait_ge(s[f"stored{lane}"], 16 * TRIPS + 1)
                for name in ("tp_lo", "np_lo", "cl_lo"):
                    sp.wait_ge(s[name], first[lane]["at"](TRIPS, name, 0))
            sp.sem_inc(s["first_over"], 1)
            for lane in second:
                lane["load_x"](sp, 0)
            with sp.Fori(0, W_GROUPS[1]) as g:
                for j in range(W_SLOTS):
                    sp.wait_ge(s["w_split"], g * W_SLOTS + j + 1)
                    sp.dma_start(w_stage[1][j], weights[:, bass.ds(W_COLS[0] + (g * W_SLOTS + j) * W_CHUNK[1], W_CHUNK[1])]).then_inc(s[f"w_in{j}"], 16)
            with sp.Fori(1, TRIPS) as t:
                for lane in second:
                    lane["load_x"](sp, t)
            for lane in range(LANES):
                sp.wait_ge(s[f"stored{lane}"], 32 * TRIPS + 1)

        @block.gpsimd
        def _(pool):
            pool.memset(ones[:, :], 1.0).then_inc(s["pool_set"], 1)
            pool.memset(neg_half[:, :], -0.5).then_inc(s["pool_set"], 1)
            for lane in range(LANES):
                pool.memset(own[lane]["last_cols"][:, :, :], 0.0).then_inc(s["pool_set"], 1)
                pool.memset(own[lane]["vl"][:, :, :], 0.0).then_inc(s["pool_set"], 1)
                pool.memset(first[lane]["ctx_lp"][:, :, :], 0.0).then_inc(s["pool_set"], 1)
            pool.wait_ge(s["const_in"], 48)
            pool.tensor_copy(ident16[:, :], ident).then_inc(s["pool_set"], 1)
            pool.tensor_copy(identb[:, :], ident).then_inc(s["pool_set"], 1)
            pool.tensor_copy(sel16[:, :], const("sel")).then_inc(s["pool_set"], 1)
            pool.wait_ge(s["pool_set"], POOL_SETUP)
            in_turns(*(lane["gpsimd_before"](pool) for lane in first))
            with pool.Fori(0, TRIPS) as t:
                in_turns(*(lane["gpsimd"](pool, t) for lane in first))
            pool.wait_ge(s["first_over"], 1)
            for lane in second:
                pool.memset(lane["qb5"][:, :, :, :, :, :], 0.0).then_inc(s["pool_set"], 1)
            with pool.Fori(0, TRIPS) as t:
                in_turns(*(lane["gpsimd"](pool, t) for lane in second))

        @block.scalar
        def _(act):
            for j in range(W_SLOTS):
                act.wait_ge(s[f"w_in{j}"], 16)
                act.activation(wp[0][:, 0, W_CHUNK[0] * j:W_CHUNK[0] * (j + 1)], w_stage[0][j], ACT.Copy).then_inc(s["w_hi"], 1)
            act.wait_ge(s["pool_set"], POOL_SETUP)
            in_turns(*(lane["scalar_before"](act) for lane in first))
            with act.Fori(0, TRIPS) as t:
                in_turns(*(lane["scalar"](act, t) for lane in first))
            with act.Fori(0, W_GROUPS[1]) as g:
                for j in range(W_SLOTS):
                    act.wait_ge(s[f"w_in{j}"], g * 16 + 32)
                    act.activation(wp[1][:, 0, bass.ds((g * W_SLOTS + j) * W_CHUNK[1], W_CHUNK[1])], w_stage[1][j], ACT.Copy).then_inc(s["w_hi"], 1)
            act.wait_ge(s["w_split"], chunks[2])
            with act.Fori(0, TRIPS) as t:
                in_turns(*(lane["scalar"](act, t) for lane in second))

        @block.tensor
        def _(pe):
            pe.wait_ge(s["pool_set"], POOL_SETUP)
            pe.wait_ge(s["ffn_abs"], 3)
            pe.matmul(psum[:, 0, 0:3], ones[:, :], stat[:, 0:3], start=True, stop=True).then_inc(s["ffn_sum"], 1)
            pe.wait_ge(s["w_split"], chunks[1])
            pe.wait_ge(s["dve_setup"], SETUP_STEPS)
            for dc in range(C):
                wq_t = [w("q0t", a, C, D)[:, :, dc * P:(dc + 1) * P] for a in range(2)]
                wk_t = [w("k0t", a, C, D)[:, :, dc * P:(dc + 1) * P] for a in range(2)]
                product(pe, psum[:, 1, dc * D:(dc + 1) * D], [
                    ((wq_t[0][:, ec], wq_t[1][:, ec]), (w("k0t", 0, C, D)[:, ec], w("k0t", 1, C, D)[:, ec])) for ec in range(C)])
                product(pe, psum[:, 2, dc:dc + 1], [
                    ((wk_t[0][:, ec], wk_t[1][:, ec]), (bq_pair[:, 0, ec:ec + 1], bq_pair[:, 1, ec:ec + 1])) for ec in range(C)])
                product(pe, psum[:, 2, C + dc:C + dc + 1], [
                    ((wq_t[0][:, ec], wq_t[1][:, ec]), (bk_pair[:, 0, ec:ec + 1], bk_pair[:, 1, ec:ec + 1])) for ec in range(C)])
            product(pe, psum[:, 2, 2 * C:2 * C + 1], [
                ((bq_pair[:, 0, ec:ec + 1].to_broadcast([P, P]), bq_pair[:, 1, ec:ec + 1].to_broadcast([P, P])),
                 (bk_pair[:, 0, ec:ec + 1], bk_pair[:, 1, ec:ec + 1])) for ec in range(C)]).then_inc(s["wqk_ps"], 1)
            pe.wait_ge(s["wqk"], 5)
            with pe.Fori(0, TRIPS) as t:
                in_turns(*(lane["tensor"](pe, t) for lane in first))
            pe.wait_ge(s["w_split"], chunks[2])
            with pe.Fori(0, TRIPS) as t:
                in_turns(*(lane["tensor"](pe, t) for lane in second))

        @block.vector
        def _(dve):
            dve.wait_ge(s["ffn_in"], 48)
            n0 = [0]

            def step(ins):
                n0[0] += 1
                ins.then_inc(s["dve_setup"], 1)
                dve.wait_ge(s["dve_setup"], n0[0])

            for i in range(3):
                dve.tensor_reduce(stat[:, i:i + 1], ffn_stage[i], X, ALU.add, apply_absolute_value=True).then_inc(s["ffn_abs"], 1)
            dve.wait_ge(s["ffn_sum"], 1)
            step(dve.tensor_scalar(ffn_inv[:, :], psum[:, 0, 0:3], 1.0 / (WIDE * D), 1e-5, ALU.mult, ALU.max))
            step(dve.reciprocal(stat[:, 4:7], ffn_inv[:, :]))
            for i in range(3):
                wf = ffn_stage[i]
                step(dve.tensor_scalar(wf, wf, stat[:, 4 + i:5 + i], 2.0, ALU.mult, ALU.min))
                step(dve.tensor_scalar(wf, wf, -2.0, ROUND, ALU.max, ALU.add))
                step(dve.tensor_scalar(wf, wf, ROUND, 1.0, ALU.subtract, ALU.min))
                step(dve.tensor_scalar(ffn_w[:, i, :], wf, -1.0, None, ALU.max))
            dve.wait_ge(s["const_in"], 48)
            for pair, name in ((bq_pair, "bq0"), (bk_pair, "bk0")):
                step(dve.tensor_copy(pair[:, 0, :], bcol(name)))
                step(dve.tensor_tensor(pair[:, 1, :], bcol(name), pair[:, 0, :], ALU.subtract))
            step(dve.tensor_scalar(half_b1[:, :], bcol("b1"), 0.5, None, ALU.mult))
            assert n0[0] == SETUP_STEPS
            for j in range(W_SLOTS):
                dve.wait_ge(s["w_hi"], j + 1)
                cols = slice(W_CHUNK[0] * j, W_CHUNK[0] * (j + 1))
                dve.tensor_tensor(wp[0][:, 1, cols], w_stage[0][j], wp[0][:, 0, cols], ALU.subtract).then_inc(s["w_split"], 1)
            dve.wait_ge(s["w_split"], chunks[1])
            dve.wait_ge(s["wqk_ps"], 1)
            dve.tensor_copy(wp[0][:, 0, 0:C * D], psum[:, 1, :]).then_inc(s["wqk"], 1)
            dve.tensor_copy(qk_bias[:, :], psum[:, 2, 0:5]).then_inc(s["wqk"], 1)
            dve.wait_ge(s["wqk"], 2)
            dve.tensor_tensor(wp[0][:, 1, 0:C * D], psum[:, 1, :], wp[0][:, 0, 0:C * D], ALU.subtract).then_inc(s["wqk"], 1)
            dve.tensor_copy(wbk_pair[:, 0, :], qk_bias[:, 2:4]).then_inc(s["wqk"], 1)
            dve.wait_ge(s["wqk"], 4)
            dve.tensor_tensor(wbk_pair[:, 1, :], qk_bias[:, 2:4], wbk_pair[:, 0, :], ALU.subtract).then_inc(s["wqk"], 1)
            dve.wait_ge(s["wqk"], 5)
            with dve.Fori(0, TRIPS) as t:
                in_turns(*(lane["vector"](dve, t) for lane in first))
            with dve.Fori(0, W_GROUPS[1]) as g:
                for j in range(W_SLOTS):
                    dve.wait_ge(s["w_hi"], g * W_SLOTS + j + chunks[1] + 1)
                    cols = bass.ds((g * W_SLOTS + j) * W_CHUNK[1], W_CHUNK[1])
                    dve.tensor_tensor(wp[1][:, 1, cols], w_stage[1][j], wp[1][:, 0, cols], ALU.subtract).then_inc(s["w_split"], 1)
            dve.wait_ge(s["w_split"], chunks[2])
            dve.wait_ge(s["pool_set"], POOL_SETUP + LANES)
            with dve.Fori(0, TRIPS) as t:
                in_turns(*(lane["vector"](dve, t) for lane in second))


def _stacked(m, k):
    import numpy as np

    return np.ascontiguousarray(m.reshape(k, P, -1).transpose(1, 0, 2).reshape(P, -1))


def _columns(v):
    return v.reshape(-1, P).T


def _constants():
    import numpy as np

    p = np.arange(P)
    parts = {
        "ident": np.eye(P), "sel": p[:, None] % SEQ == np.arange(SEQ)[None], "causal": np.where(np.arange(SEQ)[None] <= p[:, None] % SEQ, 0.0, FAR),
        "mask8": p[:, None] // 16 == np.arange(8)[None], "quad": p[:, None] // SEQ == np.arange(4)[None],
        "half": p[:, None] // 64 == np.arange(2)[None], "eye4": np.tile(np.eye(4).reshape(1, 16), (P, 1)),
        "iota8": np.tile(np.arange(8)[None], (P, 1)),
    }
    return np.concatenate([parts[n] for n, _ in _CONSTS], axis=1).astype(np.float32)


def kernel(**inputs):
    import numpy as np
    from concourse import bacc
    from concourse.bass_utils import run_bass_kernel_spmd

    a = {k: np.asarray(v) for k, v in inputs.items()}
    c = a["ctx_1024"]
    qkv_b, h = a["L0_attn_qkv_b"], a["L1_attn_W_Q"].shape[0]
    flat = {n: a["L1_attn_W_" + n].reshape(WIDE, D).T for n in "QKV"}
    experts = {n: np.concatenate([_stacked(a["L1_ffn_" + n][e].T, C) for e in range(EXPERTS)], axis=1) for n in ("w1", "w2", "w3")}

    def rolled(m):
        return np.roll(m, -LANES, axis=0)

    packed = {
        "q0t": _stacked(a["L0_xattn_Wq"].T, C), "k0t": _stacked(a["L0_xattn_Wk"].T, C), "v0": _stacked(a["L0_xattn_Wv"], C),
        "qkv0": _stacked(a["L0_attn_qkv_w"].T, C), "o0": _stacked(a["L0_attn_o_w"].T, C),
        "xq": _stacked(a["L1_xattn_w_q"].T, C), "xkv": _stacked(a["L1_xattn_w_kv"].T, C), "xo": _stacked(a["L1_xattn_w_out"].T, C),
        "aq": _stacked(flat["Q"], C), "ak": _stacked(flat["K"], C), "av": _stacked(flat["V"], C),
        "ao": _stacked(a["L1_attn_W_O"].transpose(0, 2, 1).reshape(WIDE, D), WIDE // P),
        "gate": _stacked(a["L1_ffn_gate_w"].T, C), **experts,
        "sw1": _stacked(a["L1_ffn_sw1"].T, C), "sw2": _stacked(a["L1_ffn_sw2"].T, C), "sw3": _stacked(a["L1_ffn_sw3"].T, SHARED // P),
    }
    bq, bk = _columns(a["L1_attn_b_Q"].reshape(-1)), _columns(a["L1_attn_b_K"].reshape(-1))
    columns = {
        "bq0": _columns(a["L0_xattn_bq"]), "bk0": _columns(a["L0_xattn_bk"]),
        "bqk0": _columns(qkv_b[0:2 * D]), "bv0": _columns(qkv_b[2 * D:3 * D]),
        "bqk1": np.concatenate([m[:, 2 * g:2 * g + 2] for g in range(GROUPS) for m in (bq, bk)], axis=1),
        "bv1": _columns(a["L1_attn_b_V"].reshape(-1)),
        **{n: _columns(a["L1_ffn_" + n].reshape(-1)) for n in ("b1", "b2", "b3")},
    }
    rows = np.stack([a["L0_xattn_bv"], a["L0_attn_o_b"], a["L1_xattn_b_out"], a["L1_attn_b_O"]])
    arrays = {
        "x_tok": rolled(a["x"].reshape(TILES, P, D)),
        "ctx_t": rolled(c.reshape(TILES, NB, KEYS, C, P).transpose(0, 1, 4, 3, 2).reshape(TILES, NB, P, C * KEYS)),
        "ctx_n": rolled(c[:, 0:2 * P].reshape(TILES, NB, 2, P, D).transpose(0, 1, 3, 2, 4).reshape(TILES, NB, P, 2 * D)),
        "ctx_l": rolled(c[:, KEYS - 1].reshape(TILES, NB, D)),
        "weights": np.concatenate([packed[n] for half in _SIZES for n, _ in half], axis=1),
        "ffn": np.stack([_stacked(a["L0_ffn_w_gate"].T, C), _stacked(a["L0_ffn_w_up"].T, C), _stacked(a["L0_ffn_w_down"].T, 8)]),
        "consts": _constants(),
        "biases": np.concatenate([columns[n] for n, _ in _BIASES], axis=1),
        "rows": np.tile(rows.reshape(1, -1), (P, 1)),
    }
    arrays = {"in_" + k: np.ascontiguousarray(v) for k, v in arrays.items()}
    nc = bacc.Bacc("TRN2", target_bir_lowering=False, num_devices=1)
    args = [nc.dram_tensor(k, v.shape, mybir.dt.from_np(v.dtype), kind="ExternalInput").ap() for k, v in arrays.items()]
    mid = nc.dram_tensor("x_mid", (TILES, P, D), F32, kind="Internal").ap()
    out = nc.dram_tensor("y_tok", (TILES, P, D), F32, kind="ExternalOutput").ap()
    build(nc, *args, mid, out)
    r = run_bass_kernel_spmd(nc, [arrays], core_ids=[0])
    return r.results[0]["y_tok"].reshape(SEQS, SEQ, D)
```
